# Optimizing a Trainium2 kernel written in Bass

```python
import numpy as np
import jax
import jax.numpy as jnp

def _softmax(x, axis=-1):
    return jax.nn.softmax(x, axis=axis)

def _gelu(x):
    return jax.nn.gelu(x, approximate=True)

def _silu(x):
    return jax.nn.silu(x)

def _sigmoid(x):
    return jax.nn.sigmoid(x)

def _layernorm(x, axis=-1, eps=1e-05):
    m = jnp.mean(x, axis=axis, keepdims=True)
    v = jnp.var(x, axis=axis, keepdims=True)
    return (x - m) / jnp.sqrt(v + eps)

def _scatter_add(tgt, idx, src, axis=0):
    return tgt.at[idx].add(src)

def _segment_sum(src, seg, n):
    return jax.ops.segment_sum(src, seg, n)
kernel_name = 'mk_adaln_attn_ffn_d2_seqx_r4_53e89f'

def setup_inputs(seed: int=0):
    np.random.seed(seed)
    _w = jnp.asarray

    def _rec_inputs():
        import jax
        import jax.numpy as jnp
        _rk = jax.random.key(seed)
        x = -0.000125 + 0.9999 * jax.random.normal(jax.random.fold_in(_rk, 1), (4, 512, 512), jnp.float32)
        _lenS = 512 - jax.random.randint(jax.random.fold_in(_rk, 7), (4,), 0, max(1, 512 // 4) + 1, jnp.int32)
        _lenS2 = 512 - jax.random.randint(jax.random.fold_in(_rk, 8), (4,), 0, max(1, 512 // 4) + 1, jnp.int32)
        fside_BxSxS_0 = -1.52775e-05 + 0.999936 * jax.random.normal(jax.random.fold_in(_rk, 11), (4, 512, 512), jnp.float32)
        cond_512 = -5.03954e-05 + 1.00559 * jax.random.normal(jax.random.fold_in(_rk, 12), (4, 128), jnp.float32)
        return (x, fside_BxSxS_0, cond_512)
    x, fside_BxSxS_0, cond_512 = _rec_inputs()

    def _L0_cond_setup():
        import jax, jax.numpy as jnp
        from jax import lax
        import numpy as np
        B, T, C, TD = (8, 512, 512, 128)

        def _bi_wkv(r, k, v, w, u, time_emb):
            tf = jax.nn.sigmoid(jnp.sum(time_emb, axis=-1))[:, None, None]
            decay = jnp.exp(-jnp.exp(w.astype(jnp.float32)))[None, :] * (0.5 + 0.5 * tf[:, :, 0])
            kf = k.astype(jnp.float32)
            vf = v.astype(jnp.float32)
            ek = jnp.exp(jnp.minimum(kf, 30.0))
            ekv = ek * vf

            def step(carry, x):
                a, b = carry
                ekv_t, ek_t = x
                a = a * decay + ekv_t
                b = b * decay + ek_t
                return ((a, b), (a, b))
            ekv_t = jnp.swapaxes(ekv, 0, 1)
            ek_t = jnp.swapaxes(ek, 0, 1)
            init = (jnp.zeros_like(decay), jnp.zeros_like(decay))
            _, (nf, df) = lax.scan(step, init, (ekv_t, ek_t))
            _, (nb, db) = lax.scan(step, init, (ekv_t, ek_t), reverse=True)
            nf = jnp.swapaxes(nf, 0, 1)
            df = jnp.swapaxes(df, 0, 1)
            nb = jnp.swapaxes(nb, 0, 1)
            db = jnp.swapaxes(db, 0, 1)
            euk = jnp.exp(jnp.minimum(u.astype(jnp.float32)[None, None, :] + kf, 30.0))
            num = nf + nb - ekv + euk * vf
            den = df + db - ek + euk
            base = jax.nn.sigmoid(r.astype(jnp.float32)) * (num / jnp.maximum(den, 1e-08))
            out = base * (0.8 + 0.2 * tf)
            return out.astype(r.dtype)
        key = jax.random.key(seed)
        ks = jax.random.split(key, 6)
        return {'r': jax.random.normal(ks[0], (B, T, C), dtype=jnp.float32), 'k': jax.random.normal(ks[1], (B, T, C), dtype=jnp.float32), 'v': jax.random.normal(ks[2], (B, T, C), dtype=jnp.float32), 'w': jax.random.normal(ks[3], (C,), dtype=jnp.float32), 'u': jax.random.normal(ks[4], (C,), dtype=jnp.float32), 'time_emb': jax.random.normal(ks[5], (B, TD), dtype=jnp.float32)}
    _L0_cond_all = _L0_cond_setup()
    _L0_cond_in = {k: v for k, v in _L0_cond_all.items() if k in ('w', 'u')}
    del _L0_cond_all

    def _L0_attn_setup():
        import jax, jax.numpy as jnp
        import numpy as np
        NQ, NKV, HD, SW = (32, 8, 64, 128)
        QM = NQ // NKV

        def _rope_tables(L):
            inv_freq = (1.0 / 1024.0) ** jnp.linspace(0.0, 1.0, HD // 4)
            inv_freq = jnp.concatenate([inv_freq, jnp.zeros(HD // 4)])
            theta = jnp.arange(L, dtype=jnp.float32)[:, None] * inv_freq[None, :]
            return (jnp.cos(theta), jnp.sin(theta))

        def _apply_rope(x, cos, sin):
            x1, x2 = jnp.split(x, 2, axis=-1)
            return jnp.concatenate([x1 * cos + x2 * sin, -x1 * sin + x2 * cos], axis=-1)
        key = jax.random.key(seed)
        k1, k2, k3 = jax.random.split(key, 3)
        B, L, D = (1, 512, 512)
        x = jax.random.normal(k1, (B, L, D), jnp.float32)
        W_qkv = jax.random.normal(k2, (D, (NQ + 2 * NKV) * HD), jnp.float32) * 0.02
        W_out = jax.random.normal(k3, (NQ * HD, D), jnp.float32) * 0.02
        s = jnp.zeros((1, NKV, QM), jnp.float32)
        return {'x': x, 'W_qkv': W_qkv, 'W_out': W_out, 's': s}
    _L0_attn_all = _L0_attn_setup()
    _L0_attn_in = {k: v for k, v in _L0_attn_all.items() if k in ('W_qkv', 'W_out', 's')}
    del _L0_attn_all

    def _L0_cond2_setup():
        import jax, jax.numpy as jnp
        from jax import lax
        import numpy as np
        B, T, C, TD = (8, 512, 512, 128)

        def _bi_wkv(r, k, v, w, u, time_emb):
            tf = jax.nn.sigmoid(jnp.sum(time_emb, axis=-1))[:, None, None]
            decay = jnp.exp(-jnp.exp(w.astype(jnp.float32)))[None, :] * (0.5 + 0.5 * tf[:, :, 0])
            kf = k.astype(jnp.float32)
            vf = v.astype(jnp.float32)
            ek = jnp.exp(jnp.minimum(kf, 30.0))
            ekv = ek * vf

            def step(carry, x):
                a, b = carry
                ekv_t, ek_t = x
                a = a * decay + ekv_t
                b = b * decay + ek_t
                return ((a, b), (a, b))
            ekv_t = jnp.swapaxes(ekv, 0, 1)
            ek_t = jnp.swapaxes(ek, 0, 1)
            init = (jnp.zeros_like(decay), jnp.zeros_like(decay))
            _, (nf, df) = lax.scan(step, init, (ekv_t, ek_t))
            _, (nb, db) = lax.scan(step, init, (ekv_t, ek_t), reverse=True)
            nf = jnp.swapaxes(nf, 0, 1)
            df = jnp.swapaxes(df, 0, 1)
            nb = jnp.swapaxes(nb, 0, 1)
            db = jnp.swapaxes(db, 0, 1)
            euk = jnp.exp(jnp.minimum(u.astype(jnp.float32)[None, None, :] + kf, 30.0))
            num = nf + nb - ekv + euk * vf
            den = df + db - ek + euk
            base = jax.nn.sigmoid(r.astype(jnp.float32)) * (num / jnp.maximum(den, 1e-08))
            out = base * (0.8 + 0.2 * tf)
            return out.astype(r.dtype)
        key = jax.random.key(seed)
        ks = jax.random.split(key, 6)
        return {'r': jax.random.normal(ks[0], (B, T, C), dtype=jnp.float32), 'k': jax.random.normal(ks[1], (B, T, C), dtype=jnp.float32), 'v': jax.random.normal(ks[2], (B, T, C), dtype=jnp.float32), 'w': jax.random.normal(ks[3], (C,), dtype=jnp.float32), 'u': jax.random.normal(ks[4], (C,), dtype=jnp.float32), 'time_emb': jax.random.normal(ks[5], (B, TD), dtype=jnp.float32)}
    _L0_cond2_all = _L0_cond2_setup()
    _L0_cond2_in = {k: v for k, v in _L0_cond2_all.items() if k in ('w', 'u')}
    del _L0_cond2_all

    def _L0_ffn_setup():
        import jax, jax.numpy as jnp
        import numpy as np

        def _sparsify_2to4(h):
            B, S, I = h.shape
            g = h.reshape(B, S, I // 4, 4)
            a = jnp.abs(g)
            _, idx = jax.lax.top_k(a, 2)
            pos = jnp.arange(4)
            mask = (pos == idx[..., 0:1]) | (pos == idx[..., 1:2])
            return (g * mask.astype(g.dtype)).reshape(B, S, I)
        key = jax.random.key(seed)
        k1, k2, k3, k4 = jax.random.split(key, 4)
        B, S, H, I = (4, 512, 512, 2048)
        x = jax.random.normal(k1, (B, S, H), dtype=jnp.float32)
        w_gate = jax.random.normal(k2, (H, I), dtype=jnp.float32) / np.sqrt(H)
        w_up = jax.random.normal(k3, (H, I), dtype=jnp.float32) / np.sqrt(H)
        w_down = jax.random.normal(k4, (I, H), dtype=jnp.float32) / np.sqrt(I)
        return {'x': x, 'w_gate': w_gate, 'w_up': w_up, 'w_down': w_down}
    _L0_ffn_all = _L0_ffn_setup()
    _L0_ffn_in = {k: v for k, v in _L0_ffn_all.items() if k in ('w_gate', 'w_up', 'w_down')}
    del _L0_ffn_all

    def _L1_cond_setup():
        import jax, jax.numpy as jnp
        from jax import lax
        import numpy as np
        B, T, C, TD = (8, 512, 512, 128)

        def _bi_wkv(r, k, v, w, u, time_emb):
            tf = jax.nn.sigmoid(jnp.sum(time_emb, axis=-1))[:, None, None]
            decay = jnp.exp(-jnp.exp(w.astype(jnp.float32)))[None, :] * (0.5 + 0.5 * tf[:, :, 0])
            kf = k.astype(jnp.float32)
            vf = v.astype(jnp.float32)
            ek = jnp.exp(jnp.minimum(kf, 30.0))
            ekv = ek * vf

            def step(carry, x):
                a, b = carry
                ekv_t, ek_t = x
                a = a * decay + ekv_t
                b = b * decay + ek_t
                return ((a, b), (a, b))
            ekv_t = jnp.swapaxes(ekv, 0, 1)
            ek_t = jnp.swapaxes(ek, 0, 1)
            init = (jnp.zeros_like(decay), jnp.zeros_like(decay))
            _, (nf, df) = lax.scan(step, init, (ekv_t, ek_t))
            _, (nb, db) = lax.scan(step, init, (ekv_t, ek_t), reverse=True)
            nf = jnp.swapaxes(nf, 0, 1)
            df = jnp.swapaxes(df, 0, 1)
            nb = jnp.swapaxes(nb, 0, 1)
            db = jnp.swapaxes(db, 0, 1)
            euk = jnp.exp(jnp.minimum(u.astype(jnp.float32)[None, None, :] + kf, 30.0))
            num = nf + nb - ekv + euk * vf
            den = df + db - ek + euk
            base = jax.nn.sigmoid(r.astype(jnp.float32)) * (num / jnp.maximum(den, 1e-08))
            out = base * (0.8 + 0.2 * tf)
            return out.astype(r.dtype)
        key = jax.random.key(seed)
        ks = jax.random.split(key, 6)
        return {'r': jax.random.normal(ks[0], (B, T, C), dtype=jnp.float32), 'k': jax.random.normal(ks[1], (B, T, C), dtype=jnp.float32), 'v': jax.random.normal(ks[2], (B, T, C), dtype=jnp.float32), 'w': jax.random.normal(ks[3], (C,), dtype=jnp.float32), 'u': jax.random.normal(ks[4], (C,), dtype=jnp.float32), 'time_emb': jax.random.normal(ks[5], (B, TD), dtype=jnp.float32)}
    _L1_cond_all = _L1_cond_setup()
    _L1_cond_in = {k: v for k, v in _L1_cond_all.items() if k in ('w', 'u')}
    del _L1_cond_all

    def _L1_attn_setup():
        import jax, jax.numpy as jnp
        import numpy as np
        NUM_HEADS = 16

        def _l2_normalize_complex(z):
            n = jnp.sqrt(jnp.sum(jnp.abs(z) ** 2, axis=-1, keepdims=True))
            return z / n
        key = jax.random.key(seed)
        k1, k2, k3, k4 = jax.random.split(key, 4)
        B, S, D = (4, 1024, 512)
        scale = 1.0 / np.sqrt(D)
        return {'x': jax.random.normal(k1, (B, S, D), dtype=jnp.float32), 'W_q': jax.random.normal(k2, (D, D), dtype=jnp.float32) * scale, 'W_kv': jax.random.normal(k3, (D, D), dtype=jnp.float32) * scale, 'W_o': jax.random.normal(k4, (D, D), dtype=jnp.float32) * scale}
    _L1_attn_all = _L1_attn_setup()
    _L1_attn_in = {k: v for k, v in _L1_attn_all.items() if k in ('W_q', 'W_kv', 'W_o')}
    del _L1_attn_all

    def _L1_cond2_setup():
        import jax, jax.numpy as jnp
        from jax import lax
        import numpy as np
        B, T, C, TD = (8, 512, 512, 128)

        def _bi_wkv(r, k, v, w, u, time_emb):
            tf = jax.nn.sigmoid(jnp.sum(time_emb, axis=-1))[:, None, None]
            decay = jnp.exp(-jnp.exp(w.astype(jnp.float32)))[None, :] * (0.5 + 0.5 * tf[:, :, 0])
            kf = k.astype(jnp.float32)
            vf = v.astype(jnp.float32)
            ek = jnp.exp(jnp.minimum(kf, 30.0))
            ekv = ek * vf

            def step(carry, x):
                a, b = carry
                ekv_t, ek_t = x
                a = a * decay + ekv_t
                b = b * decay + ek_t
                return ((a, b), (a, b))
            ekv_t = jnp.swapaxes(ekv, 0, 1)
            ek_t = jnp.swapaxes(ek, 0, 1)
            init = (jnp.zeros_like(decay), jnp.zeros_like(decay))
            _, (nf, df) = lax.scan(step, init, (ekv_t, ek_t))
            _, (nb, db) = lax.scan(step, init, (ekv_t, ek_t), reverse=True)
            nf = jnp.swapaxes(nf, 0, 1)
            df = jnp.swapaxes(df, 0, 1)
            nb = jnp.swapaxes(nb, 0, 1)
            db = jnp.swapaxes(db, 0, 1)
            euk = jnp.exp(jnp.minimum(u.astype(jnp.float32)[None, None, :] + kf, 30.0))
            num = nf + nb - ekv + euk * vf
            den = df + db - ek + euk
            base = jax.nn.sigmoid(r.astype(jnp.float32)) * (num / jnp.maximum(den, 1e-08))
            out = base * (0.8 + 0.2 * tf)
            return out.astype(r.dtype)
        key = jax.random.key(seed)
        ks = jax.random.split(key, 6)
        return {'r': jax.random.normal(ks[0], (B, T, C), dtype=jnp.float32), 'k': jax.random.normal(ks[1], (B, T, C), dtype=jnp.float32), 'v': jax.random.normal(ks[2], (B, T, C), dtype=jnp.float32), 'w': jax.random.normal(ks[3], (C,), dtype=jnp.float32), 'u': jax.random.normal(ks[4], (C,), dtype=jnp.float32), 'time_emb': jax.random.normal(ks[5], (B, TD), dtype=jnp.float32)}
    _L1_cond2_all = _L1_cond2_setup()
    _L1_cond2_in = {k: v for k, v in _L1_cond2_all.items() if k in ('w', 'u')}
    del _L1_cond2_all

    def _L1_ffn_setup():
        import jax, jax.numpy as jnp
        import numpy as np
        D = 512
        H_TOTAL = 2048
        E = 8
        K = 2
        HE = H_TOTAL // E
        B, S = (2, 512)
        key = jax.random.key(seed)
        ks = jax.random.split(key, 8)
        scale_up = 1.0 / np.sqrt(D)
        scale_dn = 1.0 / np.sqrt(HE)
        return {'x': jax.random.normal(ks[0], (B, S, D), dtype=jnp.float32), 'Wg1': jax.random.normal(ks[1], (E, D), dtype=jnp.float32) * 0.02, 'Wg2': jax.random.normal(ks[2], (E, E), dtype=jnp.float32) * 0.2, 'Wup': jax.random.uniform(ks[3], (E, HE, D), dtype=jnp.float32, minval=-scale_up, maxval=scale_up), 'bup': jax.random.uniform(ks[4], (E, HE), dtype=jnp.float32, minval=-scale_up, maxval=scale_up), 'Wdown': jax.random.uniform(ks[5], (E, D, HE), dtype=jnp.float32, minval=-scale_dn, maxval=scale_dn), 'bdown': jax.random.uniform(ks[6], (E, D), dtype=jnp.float32, minval=-scale_dn, maxval=scale_dn)}
    _L1_ffn_all = _L1_ffn_setup()
    _L1_ffn_in = {k: v for k, v in _L1_ffn_all.items() if k in ('Wg1', 'Wg2', 'Wup', 'bup', 'Wdown', 'bdown')}
    del _L1_ffn_all
    return {'x': x, 'fside_BxSxS_0': fside_BxSxS_0, 'cond_512': cond_512, 'L0_cond_w': _L0_cond_in['w'], 'L0_cond_u': _L0_cond_in['u'], 'L0_attn_W_qkv': _L0_attn_in['W_qkv'], 'L0_attn_W_out': _L0_attn_in['W_out'], 'L0_attn_s': _L0_attn_in['s'], 'L0_cond2_w': _L0_cond2_in['w'], 'L0_cond2_u': _L0_cond2_in['u'], 'L0_ffn_w_gate': _L0_ffn_in['w_gate'], 'L0_ffn_w_up': _L0_ffn_in['w_up'], 'L0_ffn_w_down': _L0_ffn_in['w_down'], 'L1_cond_w': _L1_cond_in['w'], 'L1_cond_u': _L1_cond_in['u'], 'L1_attn_W_q': _L1_attn_in['W_q'], 'L1_attn_W_kv': _L1_attn_in['W_kv'], 'L1_attn_W_o': _L1_attn_in['W_o'], 'L1_cond2_w': _L1_cond2_in['w'], 'L1_cond2_u': _L1_cond2_in['u'], 'L1_ffn_Wg1': _L1_ffn_in['Wg1'], 'L1_ffn_Wg2': _L1_ffn_in['Wg2'], 'L1_ffn_Wup': _L1_ffn_in['Wup'], 'L1_ffn_bup': _L1_ffn_in['bup'], 'L1_ffn_Wdown': _L1_ffn_in['Wdown'], 'L1_ffn_bdown': _L1_ffn_in['bdown']}

def reference(x, fside_BxSxS_0, cond_512, L0_cond_w, L0_cond_u, L0_attn_W_qkv, L0_attn_W_out, L0_attn_s, L0_cond2_w, L0_cond2_u, L0_ffn_w_gate, L0_ffn_w_up, L0_ffn_w_down, L1_cond_w, L1_cond_u, L1_attn_W_q, L1_attn_W_kv, L1_attn_W_o, L1_cond2_w, L1_cond2_u, L1_ffn_Wg1, L1_ffn_Wg2, L1_ffn_Wup, L1_ffn_bup, L1_ffn_Wdown, L1_ffn_bdown):
    import jax
    import jax.numpy as jnp

    def _L0_cond_ref(r, k, v, w, u, time_emb):
        import jax, jax.numpy as jnp
        from jax import lax
        import numpy as np
        B, T, C, TD = (8, 512, 512, 128)

        def _bi_wkv(r, k, v, w, u, time_emb):
            tf = jax.nn.sigmoid(jnp.sum(time_emb, axis=-1))[:, None, None]
            decay = jnp.exp(-jnp.exp(w.astype(jnp.float32)))[None, :] * (0.5 + 0.5 * tf[:, :, 0])
            kf = k.astype(jnp.float32)
            vf = v.astype(jnp.float32)
            ek = jnp.exp(jnp.minimum(kf, 30.0))
            ekv = ek * vf

            def step(carry, x):
                a, b = carry
                ekv_t, ek_t = x
                a = a * decay + ekv_t
                b = b * decay + ek_t
                return ((a, b), (a, b))
            ekv_t = jnp.swapaxes(ekv, 0, 1)
            ek_t = jnp.swapaxes(ek, 0, 1)
            init = (jnp.zeros_like(decay), jnp.zeros_like(decay))
            _, (nf, df) = lax.scan(step, init, (ekv_t, ek_t))
            _, (nb, db) = lax.scan(step, init, (ekv_t, ek_t), reverse=True)
            nf = jnp.swapaxes(nf, 0, 1)
            df = jnp.swapaxes(df, 0, 1)
            nb = jnp.swapaxes(nb, 0, 1)
            db = jnp.swapaxes(db, 0, 1)
            euk = jnp.exp(jnp.minimum(u.astype(jnp.float32)[None, None, :] + kf, 30.0))
            num = nf + nb - ekv + euk * vf
            den = df + db - ek + euk
            base = jax.nn.sigmoid(r.astype(jnp.float32)) * (num / jnp.maximum(den, 1e-08))
            out = base * (0.8 + 0.2 * tf)
            return out.astype(r.dtype)
        return _bi_wkv(r, k, v, w, u, time_emb)

    def _L0_attn_ref(x, W_qkv, W_out, s):
        import jax, jax.numpy as jnp
        import numpy as np
        NQ, NKV, HD, SW = (32, 8, 64, 128)
        QM = NQ // NKV

        def _rope_tables(L):
            inv_freq = (1.0 / 1024.0) ** jnp.linspace(0.0, 1.0, HD // 4)
            inv_freq = jnp.concatenate([inv_freq, jnp.zeros(HD // 4)])
            theta = jnp.arange(L, dtype=jnp.float32)[:, None] * inv_freq[None, :]
            return (jnp.cos(theta), jnp.sin(theta))

        def _apply_rope(x, cos, sin):
            x1, x2 = jnp.split(x, 2, axis=-1)
            return jnp.concatenate([x1 * cos + x2 * sin, -x1 * sin + x2 * cos], axis=-1)
        B, L, D = x.shape
        proj = x @ W_qkv
        q, k, v = jnp.split(proj, (NQ * HD, (NQ + NKV) * HD), axis=-1)
        cos, sin = _rope_tables(L)
        q = _apply_rope(q.reshape(B, L, NKV, QM, HD), cos[None, :, None, None, :], sin[None, :, None, None, :])
        k = _apply_rope(k.reshape(B, L, NKV, HD), cos[None, :, None, :], sin[None, :, None, :])
        v = v.reshape(B, L, NKV, HD)
        sm_scale = 1.0 / jnp.sqrt(jnp.float32(HD))
        attn = jnp.einsum('bqhmd,bkhd->bhmqk', q, k) * sm_scale
        q_pos = jnp.arange(L)[:, None]
        k_pos = jnp.arange(L)[None, :]
        mask = (q_pos >= k_pos) & (q_pos < k_pos + SW)
        attn = jnp.where(mask, -jnp.inf, attn)
        sink = jnp.broadcast_to(s[:, :, :, None, None], attn.shape[:-1] + (1,))
        w = jax.nn.softmax(jnp.concatenate([attn, sink], axis=-1), axis=-1)[..., :-1]
        out = jnp.einsum('bhmqk,bkhd->bqhmd', w, v).reshape(B, L, NQ * HD)
        return out @ W_out

    def _L0_cond2_ref(r, k, v, w, u, time_emb):
        import jax, jax.numpy as jnp
        from jax import lax
        import numpy as np
        B, T, C, TD = (8, 512, 512, 128)

        def _bi_wkv(r, k, v, w, u, time_emb):
            tf = jax.nn.sigmoid(jnp.sum(time_emb, axis=-1))[:, None, None]
            decay = jnp.exp(-jnp.exp(w.astype(jnp.float32)))[None, :] * (0.5 + 0.5 * tf[:, :, 0])
            kf = k.astype(jnp.float32)
            vf = v.astype(jnp.float32)
            ek = jnp.exp(jnp.minimum(kf, 30.0))
            ekv = ek * vf

            def step(carry, x):
                a, b = carry
                ekv_t, ek_t = x
                a = a * decay + ekv_t
                b = b * decay + ek_t
                return ((a, b), (a, b))
            ekv_t = jnp.swapaxes(ekv, 0, 1)
            ek_t = jnp.swapaxes(ek, 0, 1)
            init = (jnp.zeros_like(decay), jnp.zeros_like(decay))
            _, (nf, df) = lax.scan(step, init, (ekv_t, ek_t))
            _, (nb, db) = lax.scan(step, init, (ekv_t, ek_t), reverse=True)
            nf = jnp.swapaxes(nf, 0, 1)
            df = jnp.swapaxes(df, 0, 1)
            nb = jnp.swapaxes(nb, 0, 1)
            db = jnp.swapaxes(db, 0, 1)
            euk = jnp.exp(jnp.minimum(u.astype(jnp.float32)[None, None, :] + kf, 30.0))
            num = nf + nb - ekv + euk * vf
            den = df + db - ek + euk
            base = jax.nn.sigmoid(r.astype(jnp.float32)) * (num / jnp.maximum(den, 1e-08))
            out = base * (0.8 + 0.2 * tf)
            return out.astype(r.dtype)
        return _bi_wkv(r, k, v, w, u, time_emb)

    def _L0_ffn_ref(x, w_gate, w_up, w_down):
        import jax, jax.numpy as jnp
        import numpy as np

        def _sparsify_2to4(h):
            B, S, I = h.shape
            g = h.reshape(B, S, I // 4, 4)
            a = jnp.abs(g)
            _, idx = jax.lax.top_k(a, 2)
            pos = jnp.arange(4)
            mask = (pos == idx[..., 0:1]) | (pos == idx[..., 1:2])
            return (g * mask.astype(g.dtype)).reshape(B, S, I)
        h = jax.nn.silu(jnp.einsum('bsh,hi->bsi', x, w_gate)) * jnp.einsum('bsh,hi->bsi', x, w_up)
        h_sparse = _sparsify_2to4(h)
        return jnp.einsum('bsi,ih->bsh', h_sparse, w_down)

    def _L1_cond_ref(r, k, v, w, u, time_emb):
        import jax, jax.numpy as jnp
        from jax import lax
        import numpy as np
        B, T, C, TD = (8, 512, 512, 128)

        def _bi_wkv(r, k, v, w, u, time_emb):
            tf = jax.nn.sigmoid(jnp.sum(time_emb, axis=-1))[:, None, None]
            decay = jnp.exp(-jnp.exp(w.astype(jnp.float32)))[None, :] * (0.5 + 0.5 * tf[:, :, 0])
            kf = k.astype(jnp.float32)
            vf = v.astype(jnp.float32)
            ek = jnp.exp(jnp.minimum(kf, 30.0))
            ekv = ek * vf

            def step(carry, x):
                a, b = carry
                ekv_t, ek_t = x
                a = a * decay + ekv_t
                b = b * decay + ek_t
                return ((a, b), (a, b))
            ekv_t = jnp.swapaxes(ekv, 0, 1)
            ek_t = jnp.swapaxes(ek, 0, 1)
            init = (jnp.zeros_like(decay), jnp.zeros_like(decay))
            _, (nf, df) = lax.scan(step, init, (ekv_t, ek_t))
            _, (nb, db) = lax.scan(step, init, (ekv_t, ek_t), reverse=True)
            nf = jnp.swapaxes(nf, 0, 1)
            df = jnp.swapaxes(df, 0, 1)
            nb = jnp.swapaxes(nb, 0, 1)
            db = jnp.swapaxes(db, 0, 1)
            euk = jnp.exp(jnp.minimum(u.astype(jnp.float32)[None, None, :] + kf, 30.0))
            num = nf + nb - ekv + euk * vf
            den = df + db - ek + euk
            base = jax.nn.sigmoid(r.astype(jnp.float32)) * (num / jnp.maximum(den, 1e-08))
            out = base * (0.8 + 0.2 * tf)
            return out.astype(r.dtype)
        return _bi_wkv(r, k, v, w, u, time_emb)

    def _L1_attn_ref(x, W_q, W_kv, W_o):
        import jax, jax.numpy as jnp
        import numpy as np
        NUM_HEADS = 16

        def _l2_normalize_complex(z):
            n = jnp.sqrt(jnp.sum(jnp.abs(z) ** 2, axis=-1, keepdims=True))
            return z / n
        B, S, D = x.shape
        H = NUM_HEADS
        hd = D // H
        q = (x @ W_q.T).reshape(B, S, H, hd)
        kv = (x @ W_kv.T).reshape(B, S, H, hd)
        qf = jnp.fft.fft(q, axis=-1)
        kvf = jnp.fft.fft(kv, axis=-1)
        qf = _l2_normalize_complex(qf)
        kvf = _l2_normalize_complex(kvf)
        kvf = jnp.cumsum(kvf, axis=1)
        qv = qf * kvf
        values_hat = jnp.fft.ifft(qv, axis=-1).real.astype(x.dtype)
        values_hat = values_hat.reshape(B, S, D)
        return values_hat @ W_o.T

    def _L1_cond2_ref(r, k, v, w, u, time_emb):
        import jax, jax.numpy as jnp
        from jax import lax
        import numpy as np
        B, T, C, TD = (8, 512, 512, 128)

        def _bi_wkv(r, k, v, w, u, time_emb):
            tf = jax.nn.sigmoid(jnp.sum(time_emb, axis=-1))[:, None, None]
            decay = jnp.exp(-jnp.exp(w.astype(jnp.float32)))[None, :] * (0.5 + 0.5 * tf[:, :, 0])
            kf = k.astype(jnp.float32)
            vf = v.astype(jnp.float32)
            ek = jnp.exp(jnp.minimum(kf, 30.0))
            ekv = ek * vf

            def step(carry, x):
                a, b = carry
                ekv_t, ek_t = x
                a = a * decay + ekv_t
                b = b * decay + ek_t
                return ((a, b), (a, b))
            ekv_t = jnp.swapaxes(ekv, 0, 1)
            ek_t = jnp.swapaxes(ek, 0, 1)
            init = (jnp.zeros_like(decay), jnp.zeros_like(decay))
            _, (nf, df) = lax.scan(step, init, (ekv_t, ek_t))
            _, (nb, db) = lax.scan(step, init, (ekv_t, ek_t), reverse=True)
            nf = jnp.swapaxes(nf, 0, 1)
            df = jnp.swapaxes(df, 0, 1)
            nb = jnp.swapaxes(nb, 0, 1)
            db = jnp.swapaxes(db, 0, 1)
            euk = jnp.exp(jnp.minimum(u.astype(jnp.float32)[None, None, :] + kf, 30.0))
            num = nf + nb - ekv + euk * vf
            den = df + db - ek + euk
            base = jax.nn.sigmoid(r.astype(jnp.float32)) * (num / jnp.maximum(den, 1e-08))
            out = base * (0.8 + 0.2 * tf)
            return out.astype(r.dtype)
        return _bi_wkv(r, k, v, w, u, time_emb)

    def _L1_ffn_ref(x, Wg1, Wg2, Wup, bup, Wdown, bdown):
        import jax, jax.numpy as jnp
        import numpy as np
        D = 512
        H_TOTAL = 2048
        E = 8
        K = 2
        HE = H_TOTAL // E
        B, S = (2, 512)
        Bd, Sd, Dd = x.shape
        T = Bd * Sd
        xt = x.reshape(T, Dd)
        logits = jnp.tanh(xt @ Wg1.T) @ Wg2.T
        _, top_idx = jax.lax.top_k(logits, K)
        top_logits = jnp.take_along_axis(logits, top_idx, axis=1)
        top_scores = jax.nn.softmax(top_logits.astype(jnp.float32), axis=1).astype(logits.dtype)
        rows = jnp.arange(T)[:, None]
        scores = jnp.zeros_like(logits).at[rows, top_idx].set(top_scores)
        up = jnp.einsum('td,ehd->teh', xt, Wup) + bup
        h = jax.nn.silu(up)
        down = jnp.einsum('teh,eoh->teo', h, Wdown) + bdown
        out = jnp.einsum('te,teo->to', scores, down)
        return out.reshape(Bd, Sd, Dd)
    x = x + _L0_attn_ref(_L0_cond_ref(x, fside_BxSxS_0, fside_BxSxS_0, L0_cond_w, L0_cond_u, cond_512), L0_attn_W_qkv, L0_attn_W_out, L0_attn_s)
    x = x + _L0_ffn_ref(_L0_cond2_ref(x, fside_BxSxS_0, fside_BxSxS_0, L0_cond2_w, L0_cond2_u, cond_512), L0_ffn_w_gate, L0_ffn_w_up, L0_ffn_w_down)
    x = x + _L1_attn_ref(_L1_cond_ref(x, fside_BxSxS_0, fside_BxSxS_0, L1_cond_w, L1_cond_u, cond_512), L1_attn_W_q, L1_attn_W_kv, L1_attn_W_o)
    x = x + _L1_ffn_ref(_L1_cond2_ref(x, fside_BxSxS_0, fside_BxSxS_0, L1_cond2_w, L1_cond2_u, cond_512), L1_ffn_Wg1, L1_ffn_Wg2, L1_ffn_Wup, L1_ffn_bup, L1_ffn_Wdown, L1_ffn_bdown)
    return x

_drawn_inputs = setup_inputs


def setup_inputs(seed=0):
    import zlib

    import numpy as np

    out = dict(_drawn_inputs(seed))
    spreads = {'L0_attn_s': (0.0, 0.8)}
    factors = {'L0_cond_u': 5.445,
     'L0_cond2_u': 3.189,
     'L1_cond2_u': 3.941,
     'L1_ffn_bup': 8.0,
     'L1_ffn_bdown': 3.089}
    for name, (base, spread) in spreads.items():
        noise = np.random.default_rng([zlib.crc32(name.encode()), seed]).standard_normal(out[name].shape)
        drawn = base * np.exp(spread * noise) if base else spread * noise
        out[name] = jnp.asarray(drawn.astype(out[name].dtype))
    for name, factor in factors.items():
        out[name] = (out[name] * factor).astype(out[name].dtype)
    return out
```

```python
from contextlib import ExitStack

import numpy as np
import concourse.bass as bass
from concourse import mybir

F32 = mybir.dt.float32
BF16 = mybir.dt.bfloat16
ALU = mybir.AluOpType
ACT = mybir.ActivationFunctionType
AX_X = mybir.AxisListType.X

P = 128
B, T, C = 4, 512, 512
NC_ = C // P
NT = T // P
TD = 128
NCOND = 4
E30 = float(np.exp(np.float32(30.0)))



class Count:

    def __init__(self, sem, per, credit, by):
        self.sem, self.per, self.credit, self.by = sem, per, credit, by

    def open(self, eng):
        eng.sem_inc(self.sem, self.credit)

    def wait(self, eng, turn, n):
        assert n * self.by + self.credit > 0, self.sem
        eng.wait_ge(self.sem, turn * (self.per * self.by) + (n * self.by + self.credit))


def settle(eng, passed):
    eng.sem_inc(passed, 1)


class Space:

    def __init__(self, nc, ctx, tag):
        self.nc, self.ctx, self.tag = nc, ctx, tag

    def sb(self, name, shape, dt=F32):
        return self.ctx.enter_context(self.nc.sbuf_tensor(f"{self.tag}_{name}", shape, dt))

    def ps(self, name, shape, dt=F32):
        return self.ctx.enter_context(self.nc.psum_tensor(f"{self.tag}_{name}", shape, dt))

    def sem(self, name):
        return self.ctx.enter_context(self.nc.semaphore(f"{self.tag}_{name}"))

    def count(self, name, per, credit=1, by=1):
        return Count(self.sem(name), per, credit, by)


def prepare(nc, x, fside, cond, ws, us, ident, xT, gates):
    with ExitStack() as ctx:
        m = Space(nc, ctx, "prep")
        xin, fin = m.sb("xin", [P, NT, C]), m.sb("fin", [P, NT, C])
        fT, ek, ekv = m.sb("fT", [P, NC_, T]), m.sb("ek", [P, NC_, T]), m.sb("ekv", [P, NC_, T])
        fwd_n, fwd_d = m.sb("fwd_n", [P, 2, NC_, T]), m.sb("fwd_d", [P, NC_, T])
        bwd_n, bwd_d = m.sb("bwd_n", [P, 2, NC_, T + 1]), m.sb("bwd_d", [P, NC_, T + 1])
        euk, eukv = m.sb("euk", [P, 2, NC_, T]), m.sb("eukv", [P, 2, NC_, T])
        ratio = m.sb("ratio", [P, 2, NC_, T])
        wcol, ucol = m.sb("wcol", [P, NCOND * NC_]), m.sb("ucol", [P, NCOND * NC_])
        emb = m.sb("emb", [P, B, TD])
        embsum, embtanh = m.sb("embsum", [P, B]), m.sb("embtanh", [P, B])
        half, lngain = m.sb("half", [P, B]), m.sb("lngain", [P, B])
        decay = m.sb("decay", [P, B, NCOND * NC_])
        tp = m.ps("tp", [P, 8, T])

        params_in, par_act, par_dve, par_pool = m.sem("params_in"), m.sem("par_act"), m.sem("par_dve"), m.sem("par_pool")
        loaded = m.count("loaded", 2, by=16)
        act_passed = m.sem("act_passed")
        stored = [m.count(f"stored{h}", NCOND // 2, 17, by=16) for h in range(2)]
        f_turned, x_turned = m.count("f_turned", NC_), m.count("x_turned", NC_)
        f_copied, x_copied = m.count("f_copied", NC_), m.count("x_copied", NC_)
        ek_done, ekv_done = m.count("ek_done", 1), m.count("ekv_done", 2)
        euk_done = m.count("euk_done", NCOND * NC_)
        scans = m.count("scans", NCOND * 4 * NC_)
        eukv_done = m.count("eukv_done", NCOND, 3)
        den_done = m.count("den_done", 3 * NCOND, 1)
        rden_done = m.count("rden_done", 2 * NCOND)
        num_done = m.count("num_done", 2 * NCOND, 5)
        ratio_done = m.count("ratio_done", NCOND, 3)
        block = ctx.enter_context(nc.Block())

        @block.sync
        def _(sp):
            loaded.open(sp)
            for s in stored:
                s.open(sp)
            sp.dma_start(wcol[:, :], ws).then_inc(params_in, 16)
            sp.dma_start(ucol[:, :], us).then_inc(params_in, 16)
            sp.dma_start(emb[:, :, :], cond.rearrange("(o b) d -> o b d", o=1).to_broadcast([P, B, TD])).then_inc(params_in, 16)
            with sp.Fori(0, B) as b:
                f_turned.wait(sp, b, 0)
                x_turned.wait(sp, b, 0)
                sp.dma_start(fin[:, :, :], fside[bass.ds(b, 1)].rearrange("o (t p) c -> p (o t) c", p=P)).then_inc(loaded.sem, 16)
                sp.dma_start(xin[:, :, :], x[bass.ds(b, 1)].rearrange("o (t p) c -> p (o t) c", p=P)).then_inc(loaded.sem, 16)
                for i in range(NCOND):
                    ratio_done.wait(sp, b, i + 1)
                    sp.dma_start(gates[i, bass.ds(b, 1)].rearrange("o p c t -> p (o c) t"), ratio[:, i % 2]).then_inc(stored[i % 2].sem, 16)
            for s in stored:
                s.wait(sp, B, 0)

        @block.tensor
        def _(pe):
            f_turned.open(pe)
            x_turned.open(pe)
            with pe.Fori(0, B) as b:
                for n, (src, bank, copied, turned) in enumerate(((fin, 0, f_copied, f_turned), (xin, NC_, x_copied, x_turned))):
                    loaded.wait(pe, b, 2)
                    copied.wait(pe, b, 0)
                    for c in range(NC_):
                        for t in range(NT):
                            last = pe.transpose(tp[:, bank + c, t * P:(t + 1) * P], src[:, t, c * P:(c + 1) * P], ident[:, :])
                        last.then_inc(turned.sem, 1)

        @block.scalar
        def _(act):
            for s in (f_copied, ek_done, euk_done, rden_done):
                s.open(act)
            act.wait_ge(params_in, 16 * 3)
            act.activation(wcol[:, :], wcol[:, :], ACT.Exp).then_inc(par_act, 1)
            act.wait_ge(par_act, 1)
            act.activation(wcol[:, :], wcol[:, :], ACT.Exp, scale=-1.0).then_inc(par_act, 1)
            act.wait_ge(par_dve, 1)
            act.activation(embtanh[:, :], embsum[:, :], ACT.Tanh, scale=0.5).then_inc(par_act, 1)
            act.wait_ge(par_dve, 3)
            act.activation(lngain[:, :], lngain[:, :], ACT.Ln).then_inc(par_act, 1)
            act.wait_ge(par_act, 4)
            with act.Fori(0, B) as b:
                eukv_done.wait(act, b, 0)
                scans.wait(act, b, 0)
                euk_done.wait(act, b, 0)
                ekv_done.wait(act, b, 0)
                for c in range(NC_):
                    f_turned.wait(act, b, c + 1)
                    act.activation(fT[:, c, :], tp[:, c, :], ACT.Copy).then_inc(f_copied.sem, 1)
                f_copied.wait(act, b, NC_)
                act.activation(ek[:, :, :], fT[:, :, :], ACT.Exp).then_inc(ek_done.sem, 1)
                for i in range(NCOND + 1):
                    if i < NCOND:
                        ratio_done.wait(act, b, i - 1)
                        eukv_done.wait(act, b, i - 1)
                        for c in range(NC_):
                            act.activation(euk[:, i % 2, c, :], fT[:, c, :], ACT.Exp,
                                           bias=ucol[:, i * NC_ + c:i * NC_ + c + 1]).then_inc(euk_done.sem, 1)
                    if i >= 1:
                        j = i - 1
                        den_done.wait(act, b, 3 * j + 3)
                        act.activation(euk[:, j % 2], euk[:, j % 2], ACT.Ln).then_inc(rden_done.sem, 1)
                        rden_done.wait(act, b, 2 * j + 1)
                        settle(act, act_passed)
                        act.activation(euk[:, j % 2], euk[:, j % 2], ACT.Exp, scale=-1.0,
                                       bias=lngain[:, bass.ds(b, 1)]).then_inc(rden_done.sem, 1)

        @block.vector
        def _(dve):
            for s in (x_copied, ekv_done, scans, eukv_done, den_done):
                s.open(dve)
            dve.wait_ge(params_in, 16 * 3)
            dve.tensor_reduce(embsum[:, :], emb[:, :, :], AX_X, ALU.add).then_inc(par_dve, 1)
            dve.wait_ge(par_act, 3)
            dve.tensor_scalar(half[:, :], embtanh[:, :], 0.25, 0.75, ALU.mult, ALU.add).then_inc(par_dve, 1)
            dve.tensor_scalar(lngain[:, :], embtanh[:, :], 0.05, 0.45, ALU.mult, ALU.add).then_inc(par_dve, 1)
            dve.wait_ge(par_dve, 3)
            for b in range(B):
                dve.tensor_scalar(decay[:, b, :], wcol[:, :], half[:, b:b + 1], None, ALU.mult).then_inc(par_dve, 1)
            for h in range(2):
                dve.memset(bwd_n[:, h, :, T:T + 1], 0.0).then_inc(par_dve, 1)
            dve.memset(bwd_d[:, :, T:T + 1], 0.0).then_inc(par_dve, 1)
            dve.wait_ge(par_dve, 3 + B + 3)
            with dve.Fori(0, B) as b:
                for c in range(NC_):
                    x_turned.wait(dve, b, c + 1)
                    dve.tensor_copy(xT[:, c, bass.ds(b * T, T)], tp[:, NC_ + c, :]).then_inc(x_copied.sem, 1)
                ek_done.wait(dve, b, 1)
                dve.tensor_scalar(ek[:, :, :], ek[:, :, :], E30, None, ALU.min).then_inc(ekv_done.sem, 1)
                ekv_done.wait(dve, b, 1)
                dve.tensor_tensor(ekv[:, :, :], ek[:, :, :], fT[:, :, :], ALU.mult).then_inc(ekv_done.sem, 1)
                ekv_done.wait(dve, b, 2)
                for i in range(NCOND):
                    h = i % 2
                    ratio_done.wait(dve, b, i - 1)
                    den_done.wait(dve, b, 3 * i)
                    for c in range(NC_):
                        d = decay[:, bass.ds(b, 1), i * NC_ + c:i * NC_ + c + 1].rearrange("p o k -> p (o k)").to_broadcast([P, T])
                        for fwd, bwd, v in ((fwd_n[:, h], bwd_n[:, h], ekv), (fwd_d, bwd_d, ek)):
                            dve.tensor_tensor_scan(fwd[:, c, :], d, v[:, c, :], 0.0, ALU.mult, ALU.add).then_inc(scans.sem, 1)
                            dve.tensor_tensor_scan(bwd[:, c, 0:T][:, ::-1], v[:, c, ::-1], d, 0.0, ALU.add, ALU.mult).then_inc(scans.sem, 1)
                    euk_done.wait(dve, b, (i + 1) * NC_)
                    dve.scalar_tensor_tensor(eukv[:, h], euk[:, h], E30, fT[:, :, :], ALU.min, ALU.mult).then_inc(eukv_done.sem, 1)
                    scans.wait(dve, b, (i + 1) * 4 * NC_)
                    eukv_done.wait(dve, b, i + 1)
                    dve.scalar_tensor_tensor(euk[:, h], euk[:, h], E30, fwd_d[:, :, :], ALU.min, ALU.add).then_inc(den_done.sem, 1)
                    den_done.wait(dve, b, 3 * i + 1)
                    dve.tensor_tensor(euk[:, h], euk[:, h], bwd_d[:, :, 1:T + 1], ALU.add).then_inc(den_done.sem, 1)
                    den_done.wait(dve, b, 3 * i + 2)
                    dve.tensor_scalar(euk[:, h], euk[:, h], 1e-8, None, ALU.max).then_inc(den_done.sem, 1)

        @block.gpsimd
        def _(pool):
            for s in (num_done, ratio_done):
                s.open(pool)
            with pool.Fori(0, B) as b:
                for i in range(NCOND):
                    h = i % 2
                    scans.wait(pool, b, (i + 1) * 4 * NC_)
                    pool.tensor_tensor(fwd_n[:, h], fwd_n[:, h], bwd_n[:, h, :, 1:T + 1], ALU.add).then_inc(num_done.sem, 1)
                    num_done.wait(pool, b, 2 * i + 1)
                    eukv_done.wait(pool, b, i + 1)
                    pool.tensor_tensor(fwd_n[:, h], fwd_n[:, h], eukv[:, h], ALU.add).then_inc(num_done.sem, 1)
                    num_done.wait(pool, b, 2 * i + 2)
                    rden_done.wait(pool, b, 2 * i + 2)
                    stored[h].wait(pool, b, i // 2)
                    pool.tensor_tensor(ratio[:, h], fwd_n[:, h], euk[:, h], ALU.mult).then_inc(ratio_done.sem, 1)


NKV, QM, HD = 8, 4, 64
NPAIR = NKV // 2
NTILE = NPAIR * QM
NHEAD = 2 * NTILE
MASKED = 1e30
MW = T + (NT - 1) * P


def attention_jobs():
    jobs = [("k", 0), ("k", 1), ("kp", 0), ("k", 2), ("kp", 1), ("k", 3), ("kp", 2), ("q", 0), ("kp", 3),
            ("v", 0), ("qp", 0), ("v", 1), ("v", 2), ("v", 3)]
    for n in range(NHEAD):
        t, h = divmod(n, 2)
        p, j = divmod(t, QM)
        if p > 0 and j == 0:
            jobs += [("o", (p - 1) * NC_ + 2 * h), ("o", (p - 1) * NC_ + 2 * h + 1)]
        if h == 0 and t + 1 < NTILE:
            jobs += [("q", t + 1), ("qp", t + 1)]
    jobs += [("o", (NPAIR - 1) * NC_ + oc) for oc in range(NC_)]
    return jobs


def attention(nc, ident, xT, gate, wqkv, wout, sink, tables, mask, perm):
    with ExitStack() as ctx:
        m = Space(nc, ctx, "att")
        wq_sb = m.sb("wq", [P, NC_, NTILE * P])
        wk_sb, wv_sb = m.sb("wk", [P, NC_, NKV * HD]), m.sb("wv", [P, NC_, NKV * HD])
        wo_sb = m.sb("wo", [P, NTILE, C])
        ratio, y = m.sb("ratio", [P, NC_, T]), m.sb("y", [P, NC_, T])
        vals = m.sb("vals", [P, NT, NKV * HD])
        kz = m.sb("kz", [P, NPAIR, 2, T])
        cos_t, sin_t, mask_t = m.sb("cos", [P, T]), m.sb("sin", [P, T]), m.sb("mask", [P, MW])
        perm_t = m.sb("perm", [P, P])
        sink_t, nsink_t = m.sb("sink", [P, NHEAD]), m.sb("nsink", [P, NHEAD])
        raw, rcos, rsin = m.sb("raw", [P, 2, T]), m.sb("rcos", [P, T]), m.sb("rsin", [P, T])
        qrot = m.sb("qrot", [P, 2, T])
        probs, probsT = m.sb("probs", [P, 2, NT, T]), m.sb("probsT", [P, NT, T])
        negmax, rowsum = m.sb("negmax", [P, 2, NT]), m.sb("rowsum", [P, 2, NT])
        sinkexp, rinv = m.sb("sinkexp", [P, 2, NT]), m.sb("rinv", [P, 2, NT])
        heads = m.sb("heads", [P, QM, T])
        pj = [m.ps(f"pj{i}", [P, T]) for i in range(2)]
        sc = [m.ps(f"sc{i}", [P, T]) for i in range(3)]
        pt = [m.ps(f"pt{i}", [P, T]) for i in range(2)]
        po = m.ps("po", [P, T])

        jobs = attention_jobs()
        where = {job: n for n, job in enumerate(jobs)}
        by_act = [j for j in jobs if j[0] in "kqv"]
        by_dve = [j for j in jobs if j[0] in ("kp", "qp", "o")]
        NJ = len(jobs)
        assert NJ % 2 == 0

        act_passed, dve_passed, pool_passed = m.sem("act_passed"), m.sem("dve_passed"), m.sem("pool_passed")
        weights_in, small_in, setup = m.sem("weights_in"), m.sem("small_in"), m.sem("setup")
        ratio_in = m.count("ratio_in", 1, by=16)
        tanh_done, y_done = m.count("tanh_done", 1), m.count("y_done", 1)
        pj_ready = m.count("pj_ready", NJ, NJ)
        pj_act, pj_dve = m.count("pj_act", len(by_act), 3), m.count("pj_dve", len(by_dve), 3)
        rcos_done = m.count("rcos_done", NPAIR + NTILE, 2)
        krot_done, qrot_done = m.count("krot_done", 2 * NPAIR), m.count("qrot_done", NTILE, 2)
        sc_ready, masked = m.count("sc_ready", NHEAD * NT, 9), m.count("masked", NHEAD * NT, 4)
        exp_done, sink_done = m.count("exp_done", NHEAD * NT), m.count("sink_done", NHEAD)
        den_done = m.count("den_done", 2 * NHEAD)
        normed = m.count("normed", NHEAD * NT)
        pt_ready = m.count("pt_ready", NHEAD * NT, 5)
        pt_act, pt_dve = m.count("pt_act", NHEAD * 2, 2), m.count("pt_dve", NHEAD * 2, 2)
        pv_done, head_copied = m.count("pv_done", NHEAD * NT, 5), m.count("head_copied", NTILE, 5)
        block = ctx.enter_context(nc.Block())

        def wait_emptied(eng, b, n):
            job = jobs[(n - 2) % NJ]
            back = 0 if n >= 2 else 1
            if job in by_act:
                pj_act.wait(eng, b, by_act.index(job) + 1 - back * len(by_act))
            else:
                pj_dve.wait(eng, b, by_dve.index(job) + 1 - back * len(by_dve))

        @block.sync
        def _(sp):
            ratio_in.open(sp)
            for dst, src in ((cos_t, tables[0]), (sin_t, tables[1]), (mask_t, mask), (perm_t, perm)):
                sp.dma_start(dst[:, :], src).then_inc(small_in, 16)
            sp.dma_start(sink_t[:, :], sink.to_broadcast([P, NHEAD])).then_inc(small_in, 16)
            for c in range(NC_):
                for dst, src in ((wk_sb, wqkv[1]), (wv_sb, wqkv[2]), (wq_sb, wqkv[0])):
                    sp.dma_start(dst[:, c, :], src[c * P:(c + 1) * P, :]).then_inc(weights_in, 16)
            sp.dma_start(wo_sb[:, :, :], wout.rearrange("(t p) c -> p t c", p=P)).then_inc(weights_in, 16)
            with sp.Fori(0, B) as b:
                y_done.wait(sp, b, 0)
                sp.dma_start(ratio[:, :, :], gate[bass.ds(b, 1)].rearrange("o p c t -> p (o c) t")).then_inc(ratio_in.sem, 16)

        @block.gpsimd
        def _(pool):
            rcos_done.open(pool)
            qrot_done.open(pool)
            normed.open(pool)
            pool.wait_ge(small_in, 16 * 5)

            def rot_cos(b, r):
                job = ("k", r) if r < NPAIR else ("q", r - NPAIR)
                pj_act.wait(pool, b, by_act.index(job) + 1)
                if 0 < r <= NPAIR:
                    krot_done.wait(pool, b, 2 * r)
                qrot_done.wait(pool, b, max(0, r - NPAIR))
                pool.tensor_tensor(rcos[:, :], raw[:, r % 2, :], cos_t[:, :], ALU.mult).then_inc(rcos_done.sem, 1)

            def rot_sum(b, t):
                rcos_done.wait(pool, b, NPAIR + t + 1)
                job = ("qp", t)
                pj_dve.wait(pool, b, by_dve.index(job) + 1)
                sc_ready.wait(pool, b, (t - 1) * 2 * NT)
                pool.tensor_tensor(qrot[:, t % 2, :], rcos[:, :], rsin[:, :], ALU.add).then_inc(qrot_done.sem, 1)

            def norm(b, n):
                den_done.wait(pool, b, 2 * n + 2)
                settle(pool, pool_passed)
                for q in range(NT):
                    pool.tensor_scalar(probs[:, n % 2, q, :], probs[:, n % 2, q, :], rinv[:, n % 2, q:q + 1], 1.0,
                                       ALU.mult, ALU.mult).then_inc(normed.sem, 1)

            with pool.Fori(0, B) as b:
                for r in range(NPAIR + 1):
                    rot_cos(b, r)
                rot_sum(b, 0)
                norm(b, 0)
                for n in range(NHEAD):
                    t, h = divmod(n, 2)
                    if h == 0 and t + 1 < NTILE:
                        rot_cos(b, NPAIR + t + 1)
                        rot_sum(b, t + 1)
                    if n + 1 < NHEAD:
                        norm(b, n + 1)

        @block.tensor
        def _(pe):
            pj_ready.open(pe)
            sc_ready.open(pe)
            pt_ready.open(pe)
            pv_done.open(pe)
            pe.wait_ge(weights_in, 16 * (3 * NC_ + 1))
            pe.wait_ge(small_in, 16 * 5)
            pe.wait_ge(setup, 3)

            def run(b, kind, i):
                n = where[kind, i]
                bank = pj[n % 2]
                wait_emptied(pe, b, n)
                if kind in "kqv":
                    for c in range(NC_):
                        if kind == "v":
                            w, a = y[:, c, i * P:(i + 1) * P], wv_sb[:, c, :]
                        else:
                            w, a = (wk_sb if kind == "k" else wq_sb)[:, c, i * P:(i + 1) * P], y[:, c, :]
                        last = pe.matmul(bank[:, :], w, a, start=c == 0, stop=c == NC_ - 1)
                elif kind in ("kp", "qp"):
                    r = i if kind == "kp" else NPAIR + i
                    pj_act.wait(pe, b, by_act.index((kind[0], i)) + 1)
                    last = pe.matmul(bank[:, :], perm_t[:, :], raw[:, r % 2, :], start=True, stop=True)
                else:
                    p, oc = divmod(i, NC_)
                    head_copied.wait(pe, b, (p + 1) * QM)
                    for j in range(QM):
                        last = pe.matmul(bank[:, :], wo_sb[:, p * QM + j, oc * P:(oc + 1) * P], heads[:, j, :],
                                         start=j == 0, stop=j == QM - 1)
                last.then_inc(pj_ready.sem, 1)

            def scores(b, n, q):
                t, h = divmod(n, 2)
                s = n * NT + q
                if q == 0:
                    qrot_done.wait(pe, b, t + 1)
                masked.wait(pe, b, s - 2)
                pe.matmul(sc[s % 3][:, :], qrot[:, t % 2, q * P:(q + 1) * P], kz[:, t // QM, h, :],
                          start=True, stop=True).then_inc(sc_ready.sem, 1)

            def turn(b, n, k):
                if k == 0:
                    normed.wait(pe, b, (n + 1) * NT)
                (pt_act if k % 2 == 0 else pt_dve).wait(pe, b, 2 * n + k // 2)
                for q in range(NT):
                    last = pe.transpose(pt[k % 2][:, q * P:(q + 1) * P], probs[:, n % 2, q, k * P:(k + 1) * P], ident[:, :])
                last.then_inc(pt_ready.sem, 1)

            def values(b, n, k):
                t, h = divmod(n, 2)
                g = 2 * (t // QM) + h
                if k == 0 and h == 0:
                    head_copied.wait(pe, b, t)
                (pt_act if k % 2 == 0 else pt_dve).wait(pe, b, 2 * n + k // 2 + 1)
                pe.matmul(po[h * HD:(h + 1) * HD, :], vals[:, k, g * HD:(g + 1) * HD], probsT[:, k, :],
                          start=k == 0, stop=k == NT - 1).then_inc(pv_done.sem, 1)

            with pe.Fori(0, B) as b:
                y_done.wait(pe, b, 1)
                prologue = jobs[:14]
                for kind, i in prologue:
                    run(b, kind, i)
                krot_done.wait(pe, b, 2 * NPAIR)
                pj_act.wait(pe, b, by_act.index(("v", NT - 1)) + 1)
                for q in range(NT):
                    scores(b, 0, q)
                for n in range(NHEAD):
                    t, h = divmod(n, 2)
                    p, j = divmod(t, QM)
                    if p > 0 and j == 0:
                        run(b, "o", (p - 1) * NC_ + 2 * h)
                        run(b, "o", (p - 1) * NC_ + 2 * h + 1)
                    if h == 0 and t + 1 < NTILE:
                        run(b, "q", t + 1)
                    more = n + 1 < NHEAD
                    if more and h == 0:
                        scores(b, n + 1, 0)
                    turn(b, n, 0)
                    if more and h == 0:
                        scores(b, n + 1, 1)
                    turn(b, n, 1)
                    if h == 0 and t + 1 < NTILE:
                        run(b, "qp", t + 1)
                    if more and h == 1:
                        scores(b, n + 1, 0)
                        scores(b, n + 1, 1)
                    if more:
                        scores(b, n + 1, 2)
                        scores(b, n + 1, 3)
                    turn(b, n, 2)
                    values(b, n, 0)
                    turn(b, n, 3)
                    for k in range(1, NT):
                        values(b, n, k)
                for oc in range(NC_):
                    run(b, "o", (NPAIR - 1) * NC_ + oc)

        @block.scalar
        def _(act):
            for s in (tanh_done, pj_act, exp_done, sink_done, pt_act, head_copied):
                s.open(act)
            act.wait_ge(small_in, 16 * 5)

            def copy(b, kind, i):
                pj_ready.wait(act, b, where[kind, i] + 1)
                if kind == "v":
                    pv_done.wait(act, b, 0)
                    dst = vals[:, i, :]
                else:
                    r = i if kind == "k" else NPAIR + i
                    rcos_done.wait(act, b, r - 1)
                    back = r - 2
                    if back >= 0:
                        pj_ready.wait(act, b, where[("kp", back) if back < NPAIR else ("qp", back - NPAIR)] + 1)
                    dst = raw[:, r % 2, :]
                act.activation(dst, pj[where[kind, i] % 2][:, :], ACT.Copy).then_inc(pj_act.sem, 1)

            def exps(b, n, q):
                s = n * NT + q
                masked.wait(act, b, s + 1)
                act.activation(probs[:, n % 2, q, :], probs[:, n % 2, q, :], ACT.Exp, scale=-1.0,
                               bias=negmax[:, n % 2, q:q + 1], accum_out=rowsum[:, n % 2, q:q + 1]).then_inc(exp_done.sem, 1)

            def sinks(b, n):
                act.activation(sinkexp[:, n % 2, :], negmax[:, n % 2, :], ACT.Exp, bias=sink_t[:, n:n + 1]).then_inc(sink_done.sem, 1)

            def copy_turned(b, n, k):
                pt_ready.wait(act, b, n * NT + k + 1)
                pv_done.wait(act, b, (n - 1) * NT + k + 1)
                act.activation(probsT[:, k, :], pt[k % 2][:, :], ACT.Copy).then_inc(pt_act.sem, 1)

            with act.Fori(0, B) as b:
                pj_ready.wait(act, b, where["q", NTILE - 1] + 1 - NJ)
                settle(act, act_passed)
                act.activation(y[:, :, :], xT[:, :, bass.ds(b * T, T)], ACT.Tanh, scale=0.5).then_inc(tanh_done.sem, 1)
                for kind, i in [j for j in jobs[:14] if j in by_act]:
                    copy(b, kind, i)
                for q in range(NT):
                    exps(b, 0, q)
                sinks(b, 0)
                for n in range(NHEAD):
                    t, h = divmod(n, 2)
                    if h == 0 and t + 1 < NTILE:
                        copy(b, "q", t + 1)
                    copy_turned(b, n, 0)
                    if n + 1 < NHEAD:
                        exps(b, n + 1, 0)
                        exps(b, n + 1, 1)
                    copy_turned(b, n, 2)
                    if n + 1 < NHEAD:
                        exps(b, n + 1, 2)
                        exps(b, n + 1, 3)
                        sinks(b, n + 1)
                    if h == 1:
                        pv_done.wait(act, b, (n + 1) * NT)
                        if t % QM == 0 and t > 0:
                            pj_ready.wait(act, b, where["o", t // QM * NC_ - 1] + 1)
                        if t == 0:
                            pj_ready.wait(act, b, 0)
                        act.activation(heads[:, t % QM, :], po[:, :], ACT.Copy).then_inc(head_copied.sem, 1)

        @block.vector
        def _(dve):
            for s in (y_done, pj_dve, krot_done, masked, den_done, pt_dve):
                s.open(dve)
            dve.memset(kz[0:HD, :, 1, :], 0.0).then_inc(setup, 1)
            dve.memset(kz[HD:P, :, 0, :], 0.0).then_inc(setup, 1)
            dve.wait_ge(small_in, 16 * 5)
            dve.tensor_scalar(nsink_t[:, :], sink_t[:, :], -1.0, None, ALU.mult).then_inc(setup, 1)
            dve.wait_ge(setup, 3)

            def rot_sin(b, kind, i):
                n = where[kind, i]
                r = i if kind == "kp" else NPAIR + i
                pj_ready.wait(dve, b, n + 1)
                if 0 < r <= NPAIR:
                    krot_done.wait(dve, b, 2 * r)
                qrot_done.wait(dve, b, max(0, r - NPAIR))
                dve.tensor_tensor(rsin[:, :], pj[n % 2][:, :], sin_t[:, :], ALU.mult).then_inc(pj_dve.sem, 1)
                if kind == "kp":
                    pj_dve.wait(dve, b, by_dve.index((kind, i)) + 1)
                    rcos_done.wait(dve, b, r + 1)
                    sc_ready.wait(dve, b, 0)
                    for h in range(2):
                        rows = slice(h * HD, (h + 1) * HD)
                        dve.scalar_tensor_tensor(kz[rows, i, h, :], rcos[rows, :], -1.0, rsin[rows, :],
                                                 ALU.mult, ALU.subtract).then_inc(krot_done.sem, 1)

            def add_out(b, i):
                n = where["o", i]
                oc = i % NC_
                pj_ready.wait(dve, b, n + 1)
                if i >= NC_:
                    pj_dve.wait(dve, b, by_dve.index(("o", i - NC_)) + 1)
                x_oc = xT[:, oc, bass.ds(b * T, T)]
                dve.tensor_tensor(x_oc, x_oc, pj[n % 2][:, :], ALU.add).then_inc(pj_dve.sem, 1)

            def masking(b, n, q):
                s = n * NT + q
                sc_ready.wait(dve, b, s + 1)
                if q == 0:
                    pt_ready.wait(dve, b, (n - 1) * NT)
                    sink_done.wait(dve, b, max(n - 1, 0))
                settle(dve, dve_passed)
                dve.tensor_tensor_reduce(out=probs[:, n % 2, q, :], in0=sc[s % 3][:, :],
                                         in1=mask_t[:, (NT - 1 - q) * P:(NT - 1 - q) * P + T],
                                         scale=HD ** -0.5, scalar=nsink_t[:, n:n + 1], op0=ALU.add, op1=ALU.min,
                                         accum_out=negmax[:, n % 2, q:q + 1]).then_inc(masked.sem, 1)

            def denominators(b, n):
                exp_done.wait(dve, b, (n + 1) * NT)
                sink_done.wait(dve, b, n + 1)
                normed.wait(dve, b, max(n - 1, 0) * NT)
                dve.tensor_tensor(sinkexp[:, n % 2, :], sinkexp[:, n % 2, :], rowsum[:, n % 2, :], ALU.add).then_inc(den_done.sem, 1)
                den_done.wait(dve, b, 2 * n + 1)
                dve.reciprocal(rinv[:, n % 2, :], sinkexp[:, n % 2, :]).then_inc(den_done.sem, 1)

            def copy_turned(b, n, k):
                pt_ready.wait(dve, b, n * NT + k + 1)
                pv_done.wait(dve, b, (n - 1) * NT + k + 1)
                dve.tensor_copy(probsT[:, k, :], pt[k % 2][:, :]).then_inc(pt_dve.sem, 1)

            with dve.Fori(0, B) as b:
                tanh_done.wait(dve, b, 1)
                ratio_in.wait(dve, b, 1)
                dve.scalar_tensor_tensor(y[:, :, :], y[:, :, :], 1.0, ratio[:, :, :], ALU.add, ALU.mult).then_inc(y_done.sem, 1)
                for kind, i in [j for j in jobs[:14] if j in by_dve]:
                    rot_sin(b, kind, i)
                for q in range(NT):
                    masking(b, 0, q)
                denominators(b, 0)
                for n in range(NHEAD):
                    t, h = divmod(n, 2)
                    p, j = divmod(t, QM)
                    if p > 0 and j == 0:
                        add_out(b, (p - 1) * NC_ + 2 * h)
                        add_out(b, (p - 1) * NC_ + 2 * h + 1)
                    if n + 1 < NHEAD and h == 0:
                        masking(b, n + 1, 0)
                        masking(b, n + 1, 1)
                    copy_turned(b, n, 1)
                    if h == 0 and t + 1 < NTILE:
                        rot_sin(b, "qp", t + 1)
                    if n + 1 < NHEAD:
                        if h == 1:
                            masking(b, n + 1, 0)
                            masking(b, n + 1, 1)
                        masking(b, n + 1, 2)
                        masking(b, n + 1, 3)
                    copy_turned(b, n, 3)
                    if n + 1 < NHEAD:
                        denominators(b, n + 1)
                for oc in range(NC_):
                    add_out(b, (NPAIR - 1) * NC_ + oc)


def gate_all(xT, tanh_buf, y, tanh_done, y_done, ratio_in):

    def load(sp, gate):
        for b in range(B):
            sp.dma_start(y[:, :, b * T:(b + 1) * T], gate[b]).then_inc(ratio_in[b], 16)

    def scalar(act):
        for b in range(B):
            if b >= 2:
                act.wait_ge(y_done, b - 1)
            act.activation(tanh_buf[:, b % 2], xT[:, :, b * T:(b + 1) * T], ACT.Tanh, scale=0.5).then_inc(tanh_done, 1)

    def vector(dve):
        for b in range(B):
            dve.wait_ge(tanh_done, b + 1)
            dve.wait_ge(ratio_in[b], 16)
            y_b = y[:, :, b * T:(b + 1) * T]
            dve.scalar_tensor_tensor(y_b, tanh_buf[:, b % 2], 1.0, y_b, ALU.add, ALU.mult).then_inc(y_done, 1)

    return load, scalar, vector


NG = 4
NHID = 4 * NG


def sparse_ffn(nc, xT, gate, wgate, wup, wdown):
    with ExitStack() as ctx:
        m = Space(nc, ctx, "ffn")
        wg_sb, wu_sb = m.sb("wg", [P, NC_, NHID * P]), m.sb("wu", [P, NC_, NHID * P])
        wd_sb = m.sb("wd", [P, NHID, C])
        y, tanh_buf = m.sb("y", [P, NC_, B * T]), m.sb("tanh_buf", [P, 2, NC_, T])
        tanh_g, size = m.sb("tanh_g", [P, 2, T]), m.sb("size", [P, 4, T])
        hid = tanh_buf
        beats, votes = m.sb("beats", [P, 6, T], BF16), m.sb("votes", [P, 4, T], BF16)
        pg = [m.ps(f"pg{i}", [P, T]) for i in range(2)]
        pu = [m.ps(f"pu{i}", [P, T]) for i in range(2)]
        pd = [m.ps(f"pd{i}", [P, T]) for i in range(NC_)]

        ratio_in = [m.sem(f"ratio_in{b}") for b in range(B)]
        tanh_done, y_done = m.sem("tanh_done"), m.sem("y_done")
        up_in = [m.sem(f"up_in{c}") for c in range(NG)]
        down_in = m.sem("down_in")
        g_ready, u_ready = m.count("g_ready", NHID), m.count("u_ready", NHID)
        tanh_g_done = m.count("tanh_g_done", NHID)
        silu_done, hid_done = m.count("silu_done", NHID, 3), m.count("hid_done", NHID, 3)
        size_done = m.count("size_done", NHID, 5)
        beats_done, votes_done = m.count("beats_done", 3 * NG, 4), m.count("votes_done", 4 * NG, 5)
        sparse_done = m.count("sparse_done", NHID, 9)
        down_done, added = m.count("down_done", NHID * NC_, 40), m.count("added", NC_)
        load_y, act_y, dve_y = gate_all(xT, tanh_buf, y, tanh_done, y_done, ratio_in)
        block = ctx.enter_context(nc.Block())

        @block.sync
        def _(sp):
            load_y(sp, gate)
            for g in range(NG):
                cols = slice(g * 4 * P, (g + 1) * 4 * P)
                for dst, src in ((wg_sb, wgate), (wu_sb, wup)):
                    sp.dma_start(dst[:, :, cols], src[:, cols].rearrange("(c p) n -> p c n", p=P)).then_inc(up_in[g], 16)
            sp.dma_start(wd_sb[:, :, :], wdown.rearrange("(t p) n -> p t n", p=P)).then_inc(down_in, 16)

        @block.tensor
        def _(pe):
            for s in (g_ready, u_ready, down_done):
                s.open(pe)

            def up(b, i):
                for w, bank, ready, free in ((wg_sb, pg, g_ready, silu_done), (wu_sb, pu, u_ready, hid_done)):
                    free.wait(pe, b, i - 1)
                    for c in range(NC_):
                        last = pe.matmul(bank[i % 2][:, :], w[:, c, i * P:(i + 1) * P], y[:, c, bass.ds(b * T, T)],
                                         start=c == 0, stop=c == NC_ - 1)
                    last.then_inc(ready.sem, 1)

            def down(b, i):
                sparse_done.wait(pe, b, i + 1)
                if i == 0:
                    added.wait(pe, b, 0)
                for oc in range(NC_):
                    pe.matmul(pd[oc][:, :], wd_sb[:, i, oc * P:(oc + 1) * P], hid[:, (i // 4) % 2, i % 4, :],
                              start=i == 0, stop=i == NHID - 1).then_inc(down_done.sem, 1)

            def batch(b, first):
                pe.wait_ge(y_done, b + 1)
                for i in range(NHID):
                    if first:
                        pe.wait_ge(up_in[i // 4], 32)
                    up(b, i)
                    if i >= 4:
                        if first and i == 4:
                            pe.wait_ge(down_in, 16)
                        down(b, i - 4)
                    elif not first:
                        down(b - 1, NHID - 4 + i)

            batch(0, True)
            with pe.Fori(1, B) as b:
                batch(b, False)
            for i in range(NHID - 4, NHID):
                down(B - 1, i)

        def sizes(act, b, i):
            hid_done.wait(act, b, i + 1)
            beats_done.wait(act, b, 3 * (i // 4))
            act.activation(size[:, i % 4, :], hid[:, (i // 4) % 2, i % 4, :], ACT.Abs).then_inc(size_done.sem, 1)

        @block.scalar
        def _(act):
            tanh_g_done.open(act)
            size_done.open(act)
            act_y(act)
            with act.Fori(0, B) as b:
                for i in range(NHID):
                    g_ready.wait(act, b, i + 1)
                    silu_done.wait(act, b, i - 1)
                    hid_done.wait(act, b, i - 1)
                    act.activation(tanh_g[:, i % 2, :], pg[i % 2][:, :], ACT.Tanh, scale=0.5).then_inc(tanh_g_done.sem, 1)
                    if i >= 1:
                        sizes(act, b, i - 1)
                sizes(act, b, NHID - 1)

        @block.vector
        def _(dve):
            for s in (silu_done, hid_done, beats_done, votes_done, sparse_done, added):
                s.open(dve)
            dve_y(dve)
            dve.wait_ge(y_done, B)

            def hidden(b, i):
                tanh_g_done.wait(dve, b, i + 1)
                dve.scalar_tensor_tensor(tanh_g[:, i % 2, :], tanh_g[:, i % 2, :], 1.0, pg[i % 2][:, :],
                                         ALU.add, ALU.mult).then_inc(silu_done.sem, 1)
                u_ready.wait(dve, b, i + 1)
                silu_done.wait(dve, b, i + 1)
                down_done.wait(dve, b, (i - 7) * NC_)
                dve.tensor_tensor(hid[:, (i // 4) % 2, i % 4, :], tanh_g[:, i % 2, :], pu[i % 2][:, :],
                                  ALU.mult).then_inc(hid_done.sem, 1)

            def sparsify(b, g):
                s, v, h = size, votes, hid[:, g % 2]
                size_done.wait(dve, b, 4 * (g + 1))
                votes_done.wait(dve, b, 4 * g)
                for i, (lo, n) in enumerate(((0, 3), (3, 2), (5, 1))):
                    dve.tensor_tensor(beats[:, lo:lo + n, :], s[:, i:i + 1, :].to_broadcast([P, n, T]), s[:, i + 1:4, :],
                                      ALU.is_ge).then_inc(beats_done.sem, 1)
                beats_done.wait(dve, b, 3 * (g + 1))
                sparse_done.wait(dve, b, 4 * g)
                dve.tensor_tensor(v[:, 0:2, :], beats[:, 0:6:3, :], beats[:, 1:6:3, :], ALU.add).then_inc(votes_done.sem, 1)
                dve.tensor_tensor(v[:, 2:4, :], beats[:, 1:3, :], beats[:, 3:5, :], ALU.add).then_inc(votes_done.sem, 1)
                votes_done.wait(dve, b, 4 * g + 2)
                dve.tensor_tensor(v[:, 0:4:3, :], v[:, 0:4:3, :], beats[:, 2:6:3, :], ALU.add).then_inc(votes_done.sem, 1)
                dve.tensor_tensor(v[:, 1:3, :], v[:, 1:3, :], beats[:, 0:6:5, :], ALU.subtract).then_inc(votes_done.sem, 1)
                votes_done.wait(dve, b, 4 * g + 4)
                for j, (op, limit) in enumerate(((ALU.is_ge, 2.0), (ALU.is_ge, 1.0), (ALU.is_le, 0.0), (ALU.is_le, 1.0))):
                    dve.scalar_tensor_tensor(h[:, j, :], v[:, j, :], limit, h[:, j, :], op, ALU.mult).then_inc(sparse_done.sem, 1)

            def add_out(b):
                down_done.wait(dve, b, NHID * NC_)
                for oc in range(NC_):
                    x_oc = xT[:, oc, bass.ds(b * T, T)]
                    dve.scalar_tensor_tensor(x_oc, pd[oc][:, :], 0.5, x_oc, ALU.mult, ALU.add).then_inc(added.sem, 1)

            def batch(b, first):
                for g in range(NG):
                    for j in range(4):
                        hidden(b, 4 * g + j)
                    if g == 0 and not first:
                        add_out(b - 1)
                    sparsify(b, g)

            batch(0, True)
            with dve.Fori(1, B) as b:
                batch(b, False)
            add_out(B - 1)


NCH = 16
BINS = 16


def fourier_attention(nc, xT, gate, wq, wkv, woT, dft, idftT, norm_mat, dc_cols):
    with ExitStack() as ctx:
        m = Space(nc, ctx, "fft")
        raw_w = [m.sb(f"raw_{n}", [P, NC_, C]) for n in ("q", "kv", "o")]
        f_sb, fi_sb = m.sb("dft", [P, NC_, C]), m.sb("idft", [P, NC_, C])
        fold = [m.sb(f"fold_{n}", [P, NC_, C]) for n in ("kv", "q", "o")]
        norm_t, dc_t = m.sb("norm", [P, P]), m.sb("dc", [P, 3])
        y, tanh_buf = m.sb("y", [P, NC_, B * T]), m.sb("tanh_buf", [P, 2, NC_, T])
        square, rnorm = m.sb("square", [P, 2, 2, T]), m.sb("rnorm", [P, 2, T])
        hat_k, hat_q = m.sb("hat_k", [P, 2, T]), m.sb("hat_q", [P, 2, T])
        total = m.sb("total", [P, 2, T])
        other = m.sb("other", [P, 3, T])
        parts = m.sb("parts", [P, 4, T])
        prod = m.sb("prod", [P, 1, 4, T])
        pl = [m.ps(f"pl{i}", [P, T]) for i in range(4)]
        pn = [m.ps(f"pn{i}", [P, T]) for i in range(2)]
        pd = [m.ps(f"pd{i}", [P, T]) for i in range(2)]

        ratio_in = [m.sem(f"ratio_in{b}") for b in range(B)]
        tanh_done, y_done, w_in = m.sem("tanh_done"), m.sem("y_done"), m.sem("w_in")
        folded, fold_copied = m.sem("folded"), m.sem("fold_copied")
        planes = m.count("planes", 8, 5)
        squared, norm_ready = m.count("squared", 8, 5), m.count("norm_ready", 4, 3)
        rnormed, hatted = m.count("rnormed", 8, 5), m.count("hatted", 8, 5)
        summed, others = m.count("summed", 4, 3), m.count("others", 6, 4)
        dve_parts, pool_parts = m.count("dve_parts", 4, 3), m.count("pool_parts", 4, 3)
        prod_re, prod_im = m.count("prod_re", 2, 3), m.count("prod_im", 2, 3)
        out_ready, added = m.count("out_ready", NC_, 9), m.count("added", NC_, 9)
        load_y, act_y, dve_y = gate_all(xT, tanh_buf, y, tanh_done, y_done, ratio_in)
        block = ctx.enter_context(nc.Block())

        @block.sync
        def _(sp):
            for dst, src in ((raw_w[0], wq), (raw_w[1], wkv), (raw_w[2], woT), (f_sb, dft), (fi_sb, idftT)):
                sp.dma_start(dst[:, :, :], src.rearrange("(k p) n -> p k n", p=P)).then_inc(w_in, 16)
            sp.dma_start(norm_t[:, :], norm_mat).then_inc(w_in, 16)
            sp.dma_start(dc_t[:, :], dc_cols).then_inc(w_in, 16)
            load_y(sp, gate)

        @block.tensor
        def _(pe):
            for s in (planes, norm_ready, out_ready):
                s.open(pe)
            pe.wait_ge(w_in, 16 * 7)
            n = 0
            for w in (raw_w[1], raw_w[0]):
                for mc in range(NC_):
                    if n >= 4:
                        pe.wait_ge(fold_copied, n - 3)
                    for half in range(2):
                        for k in range(2):
                            last = pe.matmul(pl[n % 4][:, :].rearrange("p (r h s) -> p r h s", r=2, h=2)[:, :, half, :],
                                             w[:, 2 * half + k, mc * P:(mc + 1) * P],
                                             f_sb[:, 2 * half + k, :].rearrange("p (r h s) -> p r h s", r=2, h=2)[:, :, half, :],
                                             start=k == 0, stop=k == 1)
                    last.then_inc(folded, 1)
                    n += 1
            for ft in range(4):
                pe.wait_ge(fold_copied, n - 3)
                for k in range(2):
                    last = pe.matmul(pl[n % 4][:, :], fi_sb[:, 2 * (ft % 2) + k, ft * P:(ft + 1) * P],
                                     raw_w[2][:, 2 * (ft % 2) + k, :], start=k == 0, stop=k == 1)
                last.then_inc(folded, 1)
                n += 1
            pe.wait_ge(fold_copied, 12)

            def norm(b, u):
                squared.wait(pe, b, 2 * u + 2)
                rnormed.wait(pe, b, 2 * u - 3)
                for r in range(2):
                    last = pe.matmul(pn[u % 2][:, :], norm_t[:, :], square[:, u % 2, r, :], start=r == 0, stop=r == 1)
                last.then_inc(norm_ready.sem, 1)

            def out(b, oc):
                added.wait(pe, b, oc - 1)
                if oc == 0:
                    prod_re.wait(pe, b, 2)
                    prod_im.wait(pe, b, 2)
                for ft in range(4):
                    last = pe.matmul(pd[oc % 2][:, :], fold[2][:, ft, oc * P:(oc + 1) * P], prod[:, 0, ft, :],
                                     start=ft == 0, stop=ft == 3)
                last.then_inc(out_ready.sem, 1)

            def unit(b, u):
                kind, half = u % 2, u // 2
                for r in range(2):
                    tile = 2 * r + half
                    hatted.wait(pe, b, 2 * u + r - 3)
                    squared.wait(pe, b, 2 * u + r - 3)
                    for c in range(NC_):
                        last = pe.matmul(pl[2 * (u % 2) + r][:, :], fold[kind][:, c, tile * P:(tile + 1) * P],
                                         y[:, c, bass.ds(b * T, T)], start=c == 0, stop=c == NC_ - 1)
                    last.then_inc(planes.sem, 1)

            with pe.Fori(0, B) as b:
                pe.wait_ge(y_done, b + 1)
                for u in range(4):
                    unit(b, u)
                    if u >= 1:
                        norm(b, u - 1)
                norm(b, 3)
                for oc in range(NC_):
                    out(b, oc)

        @block.scalar
        def _(act):
            squared.open(act)
            rnormed.open(act)
            for n in range(12):
                act.wait_ge(folded, n + 1)
                act.activation(fold[n // 4][:, n % 4, :], pl[n % 4][:, :], ACT.Copy).then_inc(fold_copied, 1)
            act_y(act)

            def rnorm_of(b, u):
                norm_ready.wait(act, b, u + 1)
                hatted.wait(act, b, 2 * u - 2)
                act.activation(rnorm[:, u % 2, :], pn[u % 2][:, :], ACT.Ln).then_inc(rnormed.sem, 1)
                rnormed.wait(act, b, 2 * u + 1)
                act.activation(rnorm[:, u % 2, :], rnorm[:, u % 2, :], ACT.Exp, scale=-0.5).then_inc(rnormed.sem, 1)

            with act.Fori(0, B) as b:
                for u in range(4):
                    norm_ready.wait(act, b, u - 1)
                    for r in range(2):
                        planes.wait(act, b, 2 * u + r + 1)
                        act.activation(square[:, u % 2, r, :], pl[2 * (u % 2) + r][:, :], ACT.Square).then_inc(squared.sem, 1)
                    if u >= 1:
                        rnorm_of(b, u - 1)
                rnorm_of(b, 3)

        @block.vector
        def _(dve):
            for s in (hatted, summed, others, dve_parts, prod_im, added):
                s.open(dve)
            dve.wait_ge(w_in, 16 * 7)
            dve_y(dve)

            def hat(b, u):
                kind, half = u % 2, u // 2
                hat_t = hat_k if kind == 0 else hat_q
                rnormed.wait(dve, b, 2 * u + 2)
                if kind == 0:
                    summed.wait(dve, b, 2 * half)
                else:
                    pool_parts.wait(dve, b, 2 * half)
                    dve_parts.wait(dve, b, 2 * half)
                for r in range(2):
                    dve.tensor_tensor(hat_t[:, r, :], pl[2 * (u % 2) + r][:, :], rnorm[:, u % 2, :], ALU.mult).then_inc(hatted.sem, 1)

            def sums(b, half):
                hatted.wait(dve, b, 4 * half + 2)
                pool_parts.wait(dve, b, 2 * half)
                others.wait(dve, b, 3 * half)
                for r in range(2):
                    dve.tensor_tensor_scan(total[:, r, :], dc_t[:, 2:3].to_broadcast([P, T]), hat_k[:, r, :], 0.0,
                                           ALU.mult, ALU.add).then_inc(summed.sem, 1)
                summed.wait(dve, b, 2 * half + 2)
                dve_parts.wait(dve, b, 2 * half)
                dve.tensor_scalar(other[:, 0, :], total[:, 1, :], dc_t[:, 0:1], None, ALU.mult).then_inc(others.sem, 1)
                dve.tensor_scalar(other[:, 1, :], total[:, 0, :], dc_t[:, 0:1], None, ALU.mult).then_inc(others.sem, 1)
                others.wait(dve, b, 3 * half + 2)
                dve.scalar_tensor_tensor(other[:, 2, :], total[:, 1, :], dc_t[:, 1:2], other[:, 1, :],
                                         ALU.mult, ALU.add).then_inc(others.sem, 1)

            def product_im(b, half):
                hatted.wait(dve, b, 4 * half + 4)
                others.wait(dve, b, 3 * half + 3)
                prod_im.wait(dve, b, half)
                dve.tensor_tensor(parts[:, 2, :], hat_q[:, 0, :], other[:, 0, :], ALU.mult).then_inc(dve_parts.sem, 1)
                dve.tensor_tensor(parts[:, 3, :], hat_q[:, 1, :], other[:, 2, :], ALU.mult).then_inc(dve_parts.sem, 1)
                dve_parts.wait(dve, b, 2 * half + 2)
                out_ready.wait(dve, b, 0)
                dve.tensor_tensor(prod[:, 0, 2 + half, :], parts[:, 2, :], parts[:, 3, :], ALU.add).then_inc(prod_im.sem, 1)

            with dve.Fori(0, B) as b:
                hat(b, 0)
                sums(b, 0)
                hat(b, 1)
                product_im(b, 0)
                hat(b, 2)
                sums(b, 1)
                hat(b, 3)
                product_im(b, 1)
                for oc in range(NC_):
                    out_ready.wait(dve, b, oc + 1)
                    x_oc = xT[:, oc, bass.ds(b * T, T)]
                    dve.tensor_tensor(x_oc, x_oc, pd[oc % 2][:, :], ALU.add).then_inc(added.sem, 1)

        @block.gpsimd
        def _(pool):
            pool_parts.open(pool)
            prod_re.open(pool)
            with pool.Fori(0, B) as b:
                for half in range(2):
                    hatted.wait(pool, b, 4 * half + 4)
                    others.wait(pool, b, 3 * half + 1)
                    prod_re.wait(pool, b, half)
                    pool.tensor_tensor(parts[:, 0, :], hat_q[:, 0, :], total[:, 0, :], ALU.mult).then_inc(pool_parts.sem, 1)
                    pool.tensor_tensor(parts[:, 1, :], hat_q[:, 1, :], other[:, 0, :], ALU.mult).then_inc(pool_parts.sem, 1)
                    pool_parts.wait(pool, b, 2 * half + 2)
                    out_ready.wait(pool, b, 0)
                    pool.tensor_tensor(prod[:, 0, half, :], parts[:, 0, :], parts[:, 1, :], ALU.subtract).then_inc(prod_re.sem, 1)


NE, HE = 8, 256
NEH = NE * HE // P


def expert_ffn(nc, ident, xT, gate, wg1T, wg2T, wupT, bup, wdownT, bdown, lower, onehot, out):
    with ExitStack() as ctx:
        m = Space(nc, ctx, "moe")
        wu_sb, wd_sb = m.sb("wu", [P, NC_, NE * HE]), m.sb("wd", [P, NEH, C])
        wg1_sb, wg2_sb = m.sb("wg1", [P, NC_, NE]), m.sb("wg2", [NE, NE])
        bd_sb, onehot_sb = m.sb("bd", [NE, C]), m.sb("onehot", [NE, NE * P])
        bup_t, half_bup, lower_t = m.sb("bup", [P, NEH]), m.sb("half_bup", [P, NEH]), m.sb("lower", [P, NE, NE])
        y, tanh_buf = m.sb("y", [P, NC_, B * T]), m.sb("tanh_buf", [P, 2, NC_, T])
        inner, logit = m.sb("inner", [NE, T]), m.sb("logit", [P, NT, NE])
        above, equal = m.sb("above", [P, NT, NE, NE]), m.sb("equal", [P, NT, NE, NE])
        rank, top, share = m.sb("rank", [P, NT, NE]), m.sb("top", [P, NT]), m.sb("share", [P, NT, NE])
        denom = m.sb("denom", [P, NT])
        scoreT, score2 = m.sb("scoreT", [NE, B * T]), m.sb("score2", [NE, T])
        spread, tanh_u = m.sb("spread", [P, 2, T]), m.sb("tanh_u", [P, 2, T])
        lin, hid = m.sb("lin", [P, T]), m.sb("hid", [P, 2, T])
        x2, rows = m.sb("x2", [P, NC_, T]), m.sb("rows", [P, NT, C])
        pu = [m.ps(f"pu{i}", [P, T]) for i in range(2)]
        pb = [m.ps(f"pb{i}", [P, T]) for i in range(2)]
        pd = [m.ps(f"pd{i}", [P, T]) for i in range(NT)]

        ratio_in = [m.sem(f"ratio_in{b}") for b in range(B)]
        tanh_done, y_done = m.sem("tanh_done"), m.sem("y_done")
        act_passed, pe_passed = m.sem("act_passed"), m.sem("pe_passed")
        small_in, wu_in, wd_in, setup = m.sem("small_in"), m.sem("wu_in"), m.sem("wd_in"), m.sem("setup")
        inner_ready, inner_done = m.count("inner_ready", 1), m.count("inner_done", 1)
        logit_ready, ranked = m.count("logit_ready", 1), m.count("ranked", 12)
        share_exp = m.count("share_exp", 1)
        turned, turned_out = m.count("turned", 1), m.count("turned_out", 1)
        up_ready = m.count("up_ready", NEH)
        tanh_u_done, lin_done, hid_done = m.count("tanh_u_done", NEH, 3), m.count("lin_done", NEH, 3), m.count("hid_done", NEH, 3)
        spread_ready, spread_done = m.count("spread_ready", NE, 3), m.count("spread_done", NE, 3)
        down_done = m.count("down_done", NEH, 3)
        extra_ready = m.count("extra_ready", 2, 1)
        rows_done, stored = m.count("rows_done", NT), m.count("stored", NT, 1, by=16)
        batch_done = m.count("batch_done", NT)
        load_y, act_y, dve_y = gate_all(xT, tanh_buf, y, tanh_done, y_done, ratio_in)
        block = ctx.enter_context(nc.Block())

        @block.sync
        def _(sp):
            stored.open(sp)
            load_y(sp, gate)
            sp.dma_start(wg1_sb[:, :, :], wg1T.rearrange("(c p) e -> p c e", p=P)).then_inc(small_in, 16)
            for dst, src in ((wg2_sb, wg2T), (bd_sb, bdown), (onehot_sb, onehot), (bup_t, bup)):
                sp.dma_start(dst[:, :], src).then_inc(small_in, 16)
            sp.dma_start(lower_t[:, :, :], lower).then_inc(small_in, 16)
            for c in range(NC_):
                sp.dma_start(wu_sb[:, c, :], wupT[c * P:(c + 1) * P, :]).then_inc(wu_in, 16)
            sp.dma_start(wd_sb[:, :, :], wdownT.rearrange("(t p) n -> p t n", p=P)).then_inc(wd_in, 16)
            with sp.Fori(0, B) as b:
                for t in range(NT):
                    rows_done.wait(sp, b, t + 1)
                    sp.dma_start(out[bass.ds(b, 1), t * P:(t + 1) * P, :].rearrange("o p c -> p (o c)"), rows[:, t, :]).then_inc(stored.sem, 16)
            stored.wait(sp, B, 0)

        @block.tensor
        def _(pe):
            for s in (inner_ready, logit_ready, turned, up_ready, spread_ready, down_done, batch_done):
                s.open(pe)
            pe.wait_ge(small_in, 16 * 6)
            with pe.Fori(0, B) as b:
                pe.wait_ge(y_done, b + 1)
                turned_out.wait(pe, b, 0)
                for c in range(NC_):
                    last = pe.matmul(pb[0][0:NE, :], wg1_sb[:, c, :], y[:, c, bass.ds(b * T, T)], start=c == 0, stop=c == NC_ - 1)
                last.then_inc(inner_ready.sem, 1)
                inner_done.wait(pe, b, 1)
                for t in range(NT):
                    last = pe.matmul(pb[1][:, t * NE:(t + 1) * NE], inner[:, t * P:(t + 1) * P], wg2_sb[:, :], start=True, stop=True)
                last.then_inc(logit_ready.sem, 1)
                ranked.wait(pe, b, 12)
                for t in range(NT):
                    last = pe.transpose(pb[0][0:NE, t * P:(t + 1) * P], share[:, t, :], ident[:, :])
                last.then_inc(turned.sem, 1)
            turned_out.wait(pe, B, 0)
            pe.wait_ge(wu_in, 16 * NC_)

            def up(b, i):
                lin_done.wait(pe, b, i - 1)
                tanh_u_done.wait(pe, b, i - 1)
                for c in range(NC_):
                    last = pe.matmul(pu[i % 2][:, :], wu_sb[:, c, i * P:(i + 1) * P], y[:, c, bass.ds(b * T, T)],
                                     start=c == 0, stop=c == NC_ - 1)
                last.then_inc(up_ready.sem, 1)

            def spread_scores(b, e):
                spread_done.wait(pe, b, e - 1)
                settle(pe, pe_passed)
                pe.matmul(pb[e % 2][:, :], onehot_sb[:, e * P:(e + 1) * P], scoreT[:, bass.ds(b * T, T)],
                          start=True, stop=True).then_inc(spread_ready.sem, 1)

            def down(b, i):
                hid_done.wait(pe, b, i + 1)
                for t in range(NT):
                    last = pe.matmul(pd[t][:, :], hid[:, i % 2, t * P:(t + 1) * P], wd_sb[:, i, :], start=False, stop=i == NEH - 1)
                    if i == NEH - 1:
                        last.then_inc(batch_done.sem, 1)
                if i < NEH - 1:
                    last.then_inc(down_done.sem, 1)
                else:
                    pe.sem_inc(down_done.sem, 1)

            def begin(b):
                extra_ready.wait(pe, b, 2)
                rows_done.wait(pe, b, 0)
                for t in range(NT):
                    pe.matmul(pd[t][:, :], score2[:, t * P:(t + 1) * P], bd_sb[:, :], start=True, stop=False)
                    for c in range(NC_):
                        pe.matmul(pd[t][:, c * P:(c + 1) * P], x2[:, c, t * P:(t + 1) * P], ident[:, :],
                                  start=False, stop=False, skip_group_check=True)

            with pe.Fori(0, B) as b:
                for e in range(NE):
                    spread_scores(b, e)
                    for i in (2 * e, 2 * e + 1):
                        up(b, i)
                        if i == 0:
                            begin(b)
                            pe.wait_ge(wd_in, 16)
                        else:
                            down(b, i - 1)
                down(b, NEH - 1)

        @block.scalar
        def _(act):
            for s in (inner_done, share_exp, turned_out, tanh_u_done, spread_done, extra_ready, rows_done):
                s.open(act)
            act_y(act)
            with act.Fori(0, B) as b:
                inner_ready.wait(act, b, 1)
                logit_ready.wait(act, b, 0)
                act.activation(inner[:, :], pb[0][0:NE, :], ACT.Tanh).then_inc(inner_done.sem, 1)
                ranked.wait(act, b, 8)
                act.activation(share[:, :, :], share[:, :, :], ACT.Exp).then_inc(share_exp.sem, 1)
                turned.wait(act, b, 1)
                settle(act, act_passed)
                act.activation(scoreT[:, bass.ds(b * T, T)], pb[0][0:NE, :], ACT.Copy).then_inc(turned_out.sem, 1)
            turned_out.wait(act, B, 0)
            act.wait_ge(setup, 1)

            def spread_copy(b, e):
                spread_ready.wait(act, b, e + 1)
                lin_done.wait(act, b, 2 * (e - 1))
                act.activation(spread[:, e % 2, :], pb[e % 2][:, :], ACT.Copy).then_inc(spread_done.sem, 1)

            with act.Fori(0, B) as b:
                batch_done.wait(act, b, 0)
                settle(act, act_passed)
                act.activation(score2[:, :], scoreT[:, bass.ds(b * T, T)], ACT.Copy, scale=2.0).then_inc(extra_ready.sem, 1)
                act.activation(x2[:, :, :], xT[:, :, bass.ds(b * T, T)], ACT.Copy, scale=2.0).then_inc(extra_ready.sem, 1)
                for e in range(NE):
                    spread_copy(b, e)
                    for i in (2 * e, 2 * e + 1):
                        up_ready.wait(act, b, i + 1)
                        hid_done.wait(act, b, i - 1)
                        act.activation(tanh_u[:, i % 2, :], pu[i % 2][:, :], ACT.Tanh, scale=0.5,
                                       bias=half_bup[:, i:i + 1]).then_inc(tanh_u_done.sem, 1)
                stored.wait(act, b, 0)
                for t in range(NT):
                    batch_done.wait(act, b, t + 1)
                    act.activation(rows[:, t, :], pd[t][:, :], ACT.Copy, scale=0.5).then_inc(rows_done.sem, 1)

        @block.vector
        def _(dve):
            for s in (ranked, lin_done, hid_done):
                s.open(dve)
            dve.wait_ge(small_in, 16 * 6)
            dve.tensor_scalar(half_bup[:, :], bup_t[:, :], 0.5, None, ALU.mult).then_inc(setup, 1)
            dve_y(dve)
            with dve.Fori(0, B) as b:
                own, rival = [P, NT, NE, NE], [P, NT, NE, NE]
                step = [0]

                def did(ins):
                    step[0] += 1
                    ins.then_inc(ranked.sem, 1)
                    ranked.wait(dve, b, step[0])

                logit_ready.wait(dve, b, 1)
                turned.wait(dve, b, 0)
                did(dve.tensor_copy(logit[:, :, :], pb[1][:, 0:NT * NE].rearrange("p (t e) -> p t e", e=NE)))
                mine = logit[:, :, :].rearrange("p t (e o) -> p t e o", o=1).to_broadcast(own)
                theirs = logit[:, :, :].rearrange("p t (o e) -> p t o e", o=1).to_broadcast(rival)
                did(dve.tensor_tensor(above[:, :, :, :], theirs, mine, ALU.is_gt))
                did(dve.tensor_tensor(equal[:, :, :, :], theirs, mine, ALU.is_equal))
                did(dve.tensor_tensor(equal[:, :, :, :], equal[:, :, :, :],
                                      lower_t[:, :, :].rearrange("p (o e) f -> p o e f", o=1).to_broadcast(own), ALU.mult))
                did(dve.tensor_tensor(above[:, :, :, :], above[:, :, :, :], equal[:, :, :, :], ALU.add))
                did(dve.tensor_reduce(rank[:, :, :], above[:, :, :, :], AX_X, ALU.add))
                did(dve.tensor_reduce(top[:, :], logit[:, :, :], AX_X, ALU.max))
                did(dve.tensor_tensor(share[:, :, :], logit[:, :, :], top[:, :].rearrange("p (t o) -> p t o", o=1).to_broadcast([P, NT, NE]),
                                      ALU.subtract))
                share_exp.wait(dve, b, 1)
                did(dve.scalar_tensor_tensor(share[:, :, :], rank[:, :, :], 2.0, share[:, :, :], ALU.is_lt, ALU.mult))
                did(dve.tensor_reduce(denom[:, :], share[:, :, :], AX_X, ALU.add))
                did(dve.reciprocal(denom[:, :], denom[:, :]))
                did(dve.tensor_tensor(share[:, :, :], share[:, :, :], denom[:, :].rearrange("p (t o) -> p t o", o=1).to_broadcast([P, NT, NE]),
                                      ALU.mult))
            with dve.Fori(0, B) as b:
                for i in range(NEH):
                    e = i // 2
                    tanh_u_done.wait(dve, b, i + 1)
                    spread_done.wait(dve, b, e + 1)
                    hid_done.wait(dve, b, i)
                    dve.scalar_tensor_tensor(lin[:, :], pu[i % 2][:, :], bup_t[:, i:i + 1], spread[:, e % 2, :],
                                             ALU.add, ALU.mult).then_inc(lin_done.sem, 1)
                    lin_done.wait(dve, b, i + 1)
                    down_done.wait(dve, b, i - 1)
                    dve.scalar_tensor_tensor(hid[:, i % 2, :], tanh_u[:, i % 2, :], 1.0, lin[:, :],
                                             ALU.add, ALU.mult).then_inc(hid_done.sem, 1)


def build(nc, a, out):
    gates = nc.dram_tensor("gates", (NCOND, B, P, NC_, T), F32, kind="Internal").ap()
    with ExitStack() as ctx:
        ident = ctx.enter_context(nc.sbuf_tensor("ident", [P, P], F32))
        xT = ctx.enter_context(nc.sbuf_tensor("xT", [P, NC_, B * T], F32))
        ident_done = ctx.enter_context(nc.semaphore("ident_done"))
        with nc.Block() as block:
            @block.gpsimd
            def _(pool):
                pool.memset(ident[:, :], 0.0).then_inc(ident_done, 1)
                pool.wait_ge(ident_done, 1)
                pool.affine_select(out=ident[:, :], in_=ident[:, :], compare_op=ALU.not_equal, fill=1.0, base=0,
                                   pattern=[[-1, P]], channel_multiplier=1).then_inc(ident_done, 1)
                pool.wait_ge(ident_done, 2)
        prepare(nc, a["x"], a["fside"], a["cond"], a["w"], a["u"], ident, xT, gates)
        attention(nc, ident, xT, gates[0], (a["wq"], a["wk"], a["wv"]), a["wo"], a["sink"], (a["cos"], a["sin"]), a["mask"], a["perm"])
        sparse_ffn(nc, xT, gates[1], a["ffn_gate"], a["ffn_up"], a["ffn_down"])
        fourier_attention(nc, xT, gates[2], a["fft_q"], a["fft_kv"], a["fft_oT"], a["dft"], a["idftT"], a["norm"], a["dc"])
        expert_ffn(nc, ident, xT, gates[3], a["g1T"], a["g2T"], a["upT"], a["bup"], a["downT"], a["bdown"], a["lower"], a["onehot"], out)


def constants():
    c = {}
    freq = np.float32(1.0 / 1024.0) ** np.linspace(0, 1, HD // 4, dtype=np.float32)
    freq = np.concatenate([freq.astype(np.float32), np.zeros(HD // 4, np.float32)])
    theta = np.arange(T, dtype=np.float32)[None, :] * freq[:, None]
    c["cos"] = np.tile(np.cos(theta), (4, 1)).astype(np.float32)
    c["sin"] = np.concatenate([np.sin(theta), -np.sin(theta)] * 2).astype(np.float32)
    off = np.arange(MW)[None, :] - (NT - 1) * P - np.arange(P)[:, None]
    c["mask"] = np.where((off <= 0) & (off > -128), MASKED, 0.0).astype(np.float32)
    r = np.arange(P)
    c["perm"] = (r[:, None] == (r ^ (HD // 2))[None, :]).astype(np.float32)
    n, s = np.arange(2 * BINS)[:, None], np.arange(BINS)[None, :]
    theta = np.pi * n * s / BINS
    re, im = np.cos(theta), -np.sin(theta)
    im[:, 0] = (-1.0) ** n[:, 0]
    weight = np.where(s == 0, 1.0, 2.0)
    dft, idft = np.zeros((C, 2, NCH, BINS)), np.zeros((C, 2, NCH, BINS))
    for h in range(NCH):
        rows = slice(2 * BINS * h, 2 * BINS * (h + 1))
        for plane, f in ((0, re), (1, im)):
            dft[rows, plane, h] = f
            idft[rows, plane, h] = f * weight / (2 * BINS)
    c["dft"], c["idftT"] = (d.reshape(C, C).astype(np.float32) for d in (dft, idft))
    c["norm"] = ((r[:, None] // BINS == r[None, :] // BINS) * np.where(r[:, None] % BINS == 0, 1.0, 2.0)).astype(np.float32)
    c["dc"] = np.stack([r % BINS != 0, r % BINS == 0, r >= 0], 1).astype(np.float32)
    e = np.arange(NE)
    c["lower"] = np.tile((e[None, :] < e[:, None]).astype(np.float32)[None], (P, 1, 1))
    c["onehot"] = np.repeat(np.eye(NE, dtype=np.float32), P, axis=1)
    return c


def layouts(v):
    def columns(names):
        return np.stack([v[n] for n in names]).reshape(NCOND, NC_, P).transpose(2, 0, 1).reshape(P, NCOND * NC_)

    def hidden_last(w):
        return w.reshape(C, NG, P, 4).transpose(0, 1, 3, 2).reshape(C, NHID * P)

    conds = ["L0_cond", "L0_cond2", "L1_cond", "L1_cond2"]
    wqkv, nq = v["L0_attn_W_qkv"], NKV * QM * HD
    return {
        "x": v["x"], "fside": v["fside_BxSxS_0"], "cond": v["cond_512"],
        "w": columns([n + "_w" for n in conds]), "u": columns([n + "_u" for n in conds]),
        "wq": wqkv[:, :nq].reshape(C, NPAIR, 2, QM, HD).transpose(0, 1, 3, 2, 4).reshape(C, nq),
        "wk": wqkv[:, nq:nq + NKV * HD], "wv": wqkv[:, nq + NKV * HD:],
        "wo": v["L0_attn_W_out"].reshape(NPAIR, 2, QM, HD, C).transpose(0, 2, 1, 3, 4).reshape(nq, C),
        "sink": v["L0_attn_s"].reshape(NPAIR, 2, QM).transpose(0, 2, 1).reshape(1, NHEAD),
        "ffn_gate": hidden_last(v["L0_ffn_w_gate"]), "ffn_up": hidden_last(v["L0_ffn_w_up"]),
        "ffn_down": v["L0_ffn_w_down"].reshape(NG, P, 4, C).transpose(0, 2, 1, 3).reshape(NHID * P, C),
        "fft_q": v["L1_attn_W_q"], "fft_kv": v["L1_attn_W_kv"], "fft_oT": v["L1_attn_W_o"].T,
        "g1T": v["L1_ffn_Wg1"].T, "g2T": v["L1_ffn_Wg2"].T, "upT": v["L1_ffn_Wup"].reshape(NE * HE, C).T,
        "bup": v["L1_ffn_bup"].reshape(NEH, P).T,
        "downT": v["L1_ffn_Wdown"].transpose(0, 2, 1).reshape(NE * HE, C), "bdown": v["L1_ffn_bdown"],
    }


def kernel(**inputs):
    import concourse.bacc as bacc
    from concourse.bass_utils import run_bass_kernel_spmd

    nc = bacc.Bacc("TRN2", target_bir_lowering=False, num_devices=1)
    arrays, aps = {}, {}
    for name, a in {**layouts(inputs), **constants()}.items():
        a = np.ascontiguousarray(a)
        arrays[f"in_{name}"] = a
        aps[name] = nc.dram_tensor(f"in_{name}", a.shape, mybir.dt.from_np(a.dtype), kind="ExternalInput").ap()
    out = nc.dram_tensor("out", (B, T, C), F32, kind="ExternalOutput").ap()
    build(nc, aps, out)
    r = run_bass_kernel_spmd(nc, [arrays], core_ids=[0])
    return r.results[0]["out"]
```

```python
from contextlib import ExitStack

import numpy as np
import concourse.bass as bass
from concourse import mybir

F32 = mybir.dt.float32
BF16 = mybir.dt.bfloat16
F32R = mybir.dt.float32r
ALU = mybir.AluOpType
ACT = mybir.ActivationFunctionType
AX_X = mybir.AxisListType.X

P = 128
B, T, C = 4, 512, 512
NC_ = C // P
NT = T // P
TD = 128
NCOND = 4
E30 = float(np.exp(np.float32(30.0)))



class Count:

    def __init__(self, sem, per, credit, by):
        self.sem, self.per, self.credit, self.by = sem, per, credit, by

    def open(self, eng):
        eng.sem_inc(self.sem, self.credit)

    def wait(self, eng, turn, n):
        assert n * self.by + self.credit > 0, self.sem
        eng.wait_ge(self.sem, turn * (self.per * self.by) + (n * self.by + self.credit))


def settle(eng, passed):
    eng.sem_inc(passed, 1)


class Space:

    def __init__(self, nc, ctx, tag):
        self.nc, self.ctx, self.tag = nc, ctx, tag

    def sb(self, name, shape, dt=F32):
        return self.ctx.enter_context(self.nc.sbuf_tensor(f"{self.tag}_{name}", shape, dt))

    def ps(self, name, shape, dt=F32):
        return self.ctx.enter_context(self.nc.psum_tensor(f"{self.tag}_{name}", shape, dt))

    def sem(self, name):
        return self.ctx.enter_context(self.nc.semaphore(f"{self.tag}_{name}"))

    def count(self, name, per, credit=1, by=1):
        return Count(self.sem(name), per, credit, by)


def prepare(nc, x, fside, cond, ws, us, ident, xT, gates):
    with ExitStack() as ctx:
        m = Space(nc, ctx, "prep")
        xin, fin = m.sb("xin", [P, NT, C]), m.sb("fin", [P, NT, C])
        fT, ek, ekv = m.sb("fT", [P, NC_, T]), m.sb("ek", [P, NC_, T]), m.sb("ekv", [P, NC_, T])
        fwd_n, fwd_d = m.sb("fwd_n", [P, 2, NC_, T]), m.sb("fwd_d", [P, NC_, T])
        bwd_n, bwd_d = m.sb("bwd_n", [P, 2, NC_, T + 1]), m.sb("bwd_d", [P, NC_, T + 1])
        euk, eukv = m.sb("euk", [P, 2, NC_, T]), m.sb("eukv", [P, 2, NC_, T])
        ratio = m.sb("ratio", [P, 2, NC_, T])
        wcol, ucol = m.sb("wcol", [P, NCOND * NC_]), m.sb("ucol", [P, NCOND * NC_])
        emb = m.sb("emb", [P, B, TD])
        embsum, embtanh = m.sb("embsum", [P, B]), m.sb("embtanh", [P, B])
        half, lngain = m.sb("half", [P, B]), m.sb("lngain", [P, B])
        decay = m.sb("decay", [P, B, NCOND * NC_])
        tp = m.ps("tp", [P, 8, T])

        params_in, par_act, par_dve, par_pool = m.sem("params_in"), m.sem("par_act"), m.sem("par_dve"), m.sem("par_pool")
        loaded = m.count("loaded", 2, by=16)
        act_passed = m.sem("act_passed")
        stored = [m.count(f"stored{h}", NCOND // 2, 17, by=16) for h in range(2)]
        f_turned, x_turned = m.count("f_turned", NC_), m.count("x_turned", NC_)
        f_copied, x_copied = m.count("f_copied", NC_), m.count("x_copied", NC_)
        ek_done, ekv_done = m.count("ek_done", 1), m.count("ekv_done", 2)
        euk_done = m.count("euk_done", NCOND * NC_)
        scans = m.count("scans", NCOND * 4 * NC_)
        eukv_done = m.count("eukv_done", NCOND, 3)
        den_done = m.count("den_done", 3 * NCOND, 1)
        rden_done = m.count("rden_done", 2 * NCOND)
        num_done = m.count("num_done", 2 * NCOND, 5)
        ratio_done = m.count("ratio_done", NCOND, 3)
        block = ctx.enter_context(nc.Block())

        @block.sync
        def _(sp):
            loaded.open(sp)
            for s in stored:
                s.open(sp)
            sp.dma_start(wcol[:, :], ws).then_inc(params_in, 16)
            sp.dma_start(ucol[:, :], us).then_inc(params_in, 16)
            sp.dma_start(emb[:, :, :], cond.rearrange("(o b) d -> o b d", o=1).to_broadcast([P, B, TD])).then_inc(params_in, 16)
            with sp.Fori(0, B) as b:
                f_turned.wait(sp, b, 0)
                x_turned.wait(sp, b, 0)
                sp.dma_start(fin[:, :, :], fside[bass.ds(b, 1)].rearrange("o (t p) c -> p (o t) c", p=P)).then_inc(loaded.sem, 16)
                sp.dma_start(xin[:, :, :], x[bass.ds(b, 1)].rearrange("o (t p) c -> p (o t) c", p=P)).then_inc(loaded.sem, 16)
                for i in range(NCOND):
                    ratio_done.wait(sp, b, i + 1)
                    sp.dma_start(gates[i, bass.ds(b, 1)].rearrange("o p c t -> p (o c) t"), ratio[:, i % 2]).then_inc(stored[i % 2].sem, 16)
            for s in stored:
                s.wait(sp, B, 0)

        @block.tensor
        def _(pe):
            f_turned.open(pe)
            x_turned.open(pe)
            with pe.Fori(0, B) as b:
                for n, (src, bank, copied, turned) in enumerate(((fin, 0, f_copied, f_turned), (xin, NC_, x_copied, x_turned))):
                    loaded.wait(pe, b, 2)
                    copied.wait(pe, b, 0)
                    for c in range(NC_):
                        for t in range(NT):
                            last = pe.transpose(tp[:, bank + c, t * P:(t + 1) * P], src[:, t, c * P:(c + 1) * P], ident[:, :])
                        last.then_inc(turned.sem, 1)

        @block.scalar
        def _(act):
            for s in (f_copied, ek_done, euk_done, rden_done):
                s.open(act)
            act.wait_ge(params_in, 16 * 3)
            act.activation(wcol[:, :], wcol[:, :], ACT.Exp).then_inc(par_act, 1)
            act.wait_ge(par_act, 1)
            act.activation(wcol[:, :], wcol[:, :], ACT.Exp, scale=-1.0).then_inc(par_act, 1)
            act.wait_ge(par_dve, 1)
            act.activation(embtanh[:, :], embsum[:, :], ACT.Tanh, scale=0.5).then_inc(par_act, 1)
            act.wait_ge(par_dve, 3)
            act.activation(lngain[:, :], lngain[:, :], ACT.Ln).then_inc(par_act, 1)
            act.wait_ge(par_act, 4)
            with act.Fori(0, B) as b:
                eukv_done.wait(act, b, 0)
                scans.wait(act, b, 0)
                euk_done.wait(act, b, 0)
                ekv_done.wait(act, b, 0)
                for c in range(NC_):
                    f_turned.wait(act, b, c + 1)
                    act.activation(fT[:, c, :], tp[:, c, :], ACT.Copy).then_inc(f_copied.sem, 1)
                f_copied.wait(act, b, NC_)
                act.activation(ek[:, :, :], fT[:, :, :], ACT.Exp).then_inc(ek_done.sem, 1)
                for i in range(NCOND + 1):
                    if i < NCOND:
                        ratio_done.wait(act, b, i - 1)
                        eukv_done.wait(act, b, i - 1)
                        for c in range(NC_):
                            act.activation(euk[:, i % 2, c, :], fT[:, c, :], ACT.Exp,
                                           bias=ucol[:, i * NC_ + c:i * NC_ + c + 1]).then_inc(euk_done.sem, 1)
                    if i >= 1:
                        j = i - 1
                        den_done.wait(act, b, 3 * j + 3)
                        act.activation(euk[:, j % 2], euk[:, j % 2], ACT.Ln).then_inc(rden_done.sem, 1)
                        rden_done.wait(act, b, 2 * j + 1)
                        settle(act, act_passed)
                        act.activation(euk[:, j % 2], euk[:, j % 2], ACT.Exp, scale=-1.0,
                                       bias=lngain[:, bass.ds(b, 1)]).then_inc(rden_done.sem, 1)

        @block.vector
        def _(dve):
            for s in (x_copied, ekv_done, scans, eukv_done, den_done):
                s.open(dve)
            dve.wait_ge(params_in, 16 * 3)
            dve.tensor_reduce(embsum[:, :], emb[:, :, :], AX_X, ALU.add).then_inc(par_dve, 1)
            dve.wait_ge(par_act, 3)
            dve.tensor_scalar(half[:, :], embtanh[:, :], 0.25, 0.75, ALU.mult, ALU.add).then_inc(par_dve, 1)
            dve.tensor_scalar(lngain[:, :], embtanh[:, :], 0.05, 0.45, ALU.mult, ALU.add).then_inc(par_dve, 1)
            dve.wait_ge(par_dve, 3)
            for b in range(B):
                dve.tensor_scalar(decay[:, b, :], wcol[:, :], half[:, b:b + 1], None, ALU.mult).then_inc(par_dve, 1)
            for h in range(2):
                dve.memset(bwd_n[:, h, :, T:T + 1], 0.0).then_inc(par_dve, 1)
            dve.memset(bwd_d[:, :, T:T + 1], 0.0).then_inc(par_dve, 1)
            dve.wait_ge(par_dve, 3 + B + 3)
            with dve.Fori(0, B) as b:
                for c in range(NC_):
                    x_turned.wait(dve, b, c + 1)
                    dve.tensor_copy(xT[:, c, bass.ds(b * T, T)], tp[:, NC_ + c, :]).then_inc(x_copied.sem, 1)
                ek_done.wait(dve, b, 1)
                dve.tensor_scalar(ek[:, :, :], ek[:, :, :], E30, None, ALU.min).then_inc(ekv_done.sem, 1)
                ekv_done.wait(dve, b, 1)
                dve.tensor_tensor(ekv[:, :, :], ek[:, :, :], fT[:, :, :], ALU.mult).then_inc(ekv_done.sem, 1)
                ekv_done.wait(dve, b, 2)
                for i in range(NCOND):
                    h = i % 2
                    ratio_done.wait(dve, b, i - 1)
                    den_done.wait(dve, b, 3 * i)
                    for c in range(NC_):
                        d = decay[:, bass.ds(b, 1), i * NC_ + c:i * NC_ + c + 1].rearrange("p o k -> p (o k)").to_broadcast([P, T])
                        for fwd, bwd, v in ((fwd_n[:, h], bwd_n[:, h], ekv), (fwd_d, bwd_d, ek)):
                            dve.tensor_tensor_scan(fwd[:, c, :], d, v[:, c, :], 0.0, ALU.mult, ALU.add).then_inc(scans.sem, 1)
                            dve.tensor_tensor_scan(bwd[:, c, 0:T][:, ::-1], v[:, c, ::-1], d, 0.0, ALU.add, ALU.mult).then_inc(scans.sem, 1)
                    euk_done.wait(dve, b, (i + 1) * NC_)
                    dve.scalar_tensor_tensor(eukv[:, h], euk[:, h], E30, fT[:, :, :], ALU.min, ALU.mult).then_inc(eukv_done.sem, 1)
                    scans.wait(dve, b, (i + 1) * 4 * NC_)
                    eukv_done.wait(dve, b, i + 1)
                    dve.scalar_tensor_tensor(euk[:, h], euk[:, h], E30, fwd_d[:, :, :], ALU.min, ALU.add).then_inc(den_done.sem, 1)
                    den_done.wait(dve, b, 3 * i + 1)
                    dve.tensor_tensor(euk[:, h], euk[:, h], bwd_d[:, :, 1:T + 1], ALU.add).then_inc(den_done.sem, 1)
                    den_done.wait(dve, b, 3 * i + 2)
                    dve.tensor_scalar(euk[:, h], euk[:, h], 1e-8, None, ALU.max).then_inc(den_done.sem, 1)

        @block.gpsimd
        def _(pool):
            for s in (num_done, ratio_done):
                s.open(pool)
            with pool.Fori(0, B) as b:
                for i in range(NCOND):
                    h = i % 2
                    scans.wait(pool, b, (i + 1) * 4 * NC_)
                    pool.tensor_tensor(fwd_n[:, h], fwd_n[:, h], bwd_n[:, h, :, 1:T + 1], ALU.add).then_inc(num_done.sem, 1)
                    num_done.wait(pool, b, 2 * i + 1)
                    eukv_done.wait(pool, b, i + 1)
                    pool.tensor_tensor(fwd_n[:, h], fwd_n[:, h], eukv[:, h], ALU.add).then_inc(num_done.sem, 1)
                    num_done.wait(pool, b, 2 * i + 2)
                    rden_done.wait(pool, b, 2 * i + 2)
                    stored[h].wait(pool, b, i // 2)
                    pool.tensor_tensor(ratio[:, h], fwd_n[:, h], euk[:, h], ALU.mult).then_inc(ratio_done.sem, 1)


def product(pe, bank, a_hi, a_lo, b_hi, b_lo, start, stop):
    pe.matmul(bank, a_hi, b_hi, start=start, stop=False)
    pe.matmul(bank, a_hi, b_lo, start=False, stop=False)
    return pe.matmul(bank, a_lo, b_hi, start=False, stop=stop)


NKV, QM, HD = 8, 4, 64
NPAIR = NKV // 2
NTILE = NPAIR * QM
NHEAD = 2 * NTILE
MASKED = -1e30
MW = T + (NT - 1) * P
RAWS, SPLITS = 3, 2
AHEAD = 2


def attention_jobs():
    jobs = [("k", 0), ("v", 0), ("ks", 0), ("v", 1), ("q", 0), ("v", 2), ("qs", 0), ("v", 3), ("q", 1), ("qs", 1)]
    for n in range(NHEAD):
        jobs += side_jobs(n) + [(kind + "s", i) for kind, i in side_jobs(n) if kind != "o"]
    jobs += [("o", (NPAIR - 1) * NC_ + oc) for oc in range(NC_)]
    return jobs


def side_jobs(n):
    t, h = divmod(n, 2)
    p, j = divmod(t, QM)
    jobs = [("o", (p - 1) * NC_ + 2 * h + i) for i in range(2) if p > 0 and j == 0]
    if h == 0 and t + 2 < NTILE:
        jobs.append(("q", t + 2))
    if h == 1 and j == 1 and p + 1 < NPAIR:
        jobs.append(("k", p + 1))
    return jobs


def attention(nc, ident, xT, gate, weights, wv, sink, tables, mask, perm):
    with ExitStack() as ctx:
        m = Space(nc, ctx, "att")
        wraw = m.sb("wraw", [P, RAWS, NC_, P])
        w_hi, w_lo = m.sb("w_hi", [P, SPLITS, NC_, P], F32R), m.sb("w_lo", [P, SPLITS, NC_, P], F32R)
        wv_sb = m.sb("wv", [P, NC_, NKV * HD])
        y = m.sb("y", [P, NC_, T])
        y_hi, y_lo = m.sb("y_hi", [P, NC_, T], F32R), m.sb("y_lo", [P, NC_, T], F32R)
        v_hi, v_lo = m.sb("v_hi", [P, NT, NKV * HD], F32R), m.sb("v_lo", [P, NT, NKV * HD], F32R)
        kz_hi, kz_lo = m.sb("kz_hi", [P, 2, 2, T], F32R), m.sb("kz_lo", [P, 2, 2, T], F32R)
        q_hi, q_lo = m.sb("q_hi", [P, 2, T], F32R), m.sb("q_lo", [P, 2, T], F32R)
        cos_t, sin_t, mask_t = m.sb("cos", [P, T]), m.sb("sin", [P, T]), m.sb("mask", [P, MW])
        perm_t = m.sb("perm", [P, P])
        sink_t, nsink_t = m.sb("sink", [P, NHEAD]), m.sb("nsink", [P, NHEAD])
        raw, rcos, rsin, rsum = m.sb("raw", [P, 2, T]), m.sb("rcos", [P, T]), m.sb("rsin", [P, T]), m.sb("rsum", [P, T])
        probs = m.sb("probs", [P, AHEAD + 1, NT, T])
        pT_hi, pT_lo = m.sb("pT_hi", [P, NT, T], F32R), m.sb("pT_lo", [P, NT, T], F32R)
        negmax, rowsum = m.sb("negmax", [P, AHEAD + 1, NT]), m.sb("rowsum", [P, AHEAD + 1, NT])
        sinkexp, rinv = m.sb("sinkexp", [P, AHEAD + 1, NT]), m.sb("rinv", [P, AHEAD + 1, NT])
        heads_hi, heads_lo = m.sb("heads_hi", [P, QM, T], F32R), m.sb("heads_lo", [P, QM, T], F32R)
        pj = [m.ps(f"pj{i}", [P, T]) for i in range(2)]
        sc = [m.ps(f"sc{i}", [P, T]) for i in range(3)]
        pt = [m.ps(f"pt{i}", [P, T]) for i in range(2)]
        po = m.ps("po", [P, T])

        RING = AHEAD + 1
        jobs = attention_jobs()
        where = {job: n for n, job in enumerate(jobs)}
        ropes = [j for j in jobs if j[0] in ("k", "q")]
        by_dve = [j for j in jobs if j[0] in ("ks", "qs", "v", "o")]
        weighted = [j for j in jobs if j[0] in ("k", "q", "o")]
        NJ, NR, NW = len(jobs), len(ropes), len(weighted)
        assert NJ % 2 == 0 and NR % 2 == 0 and NW % RAWS == 0 and NW % SPLITS == 0
        rounds = np.cumsum([2 if kind == "k" else 1 for kind, _ in ropes]).tolist()
        before = lambda r: rounds[r - 1] if r > 0 else 0

        act_passed, dve_passed, pool_passed = m.sem("act_passed"), m.sem("dve_passed"), m.sem("pool_passed")
        wv_in, small_in, zeroed, setup = m.sem("wv_in"), m.sem("small_in"), m.sem("zeroed"), m.sem("setup")
        w_in = [m.count(f"w_in{s}", NW // RAWS, 16, by=16) for s in range(RAWS)]
        w_hi_done, w_lo_done = m.count("w_hi_done", NW, RAWS), m.count("w_lo_done", NW, RAWS)
        ratio_in = m.count("ratio_in", 1, by=16)
        tanh_done, y_done = m.count("tanh_done", 1), m.count("y_done", NC_)
        y_hi_done, y_lo_done = m.count("y_hi_done", NC_), m.count("y_lo_done", NC_)
        pj_ready = m.count("pj_ready", NJ, NJ)
        raw_done, pj_dve = m.count("raw_done", NR, 3), m.count("pj_dve", len(by_dve), 3)
        v_hi_done = m.count("v_hi_done", NT)
        rcos_done, rsum_done = m.count("rcos_done", NR, 2), m.count("rsum_done", NR, 2)
        rope_hi, rope_lo = m.count("rope_hi", rounds[-1], 3), m.count("rope_lo", rounds[-1], 3)
        sc_ready, masked = m.count("sc_ready", NHEAD * NT, NHEAD * NT + 8), m.count("masked", NHEAD * NT, 4)
        exp_done, sink_done = m.count("exp_done", NHEAD * NT), m.count("sink_done", NHEAD)
        den_done = m.count("den_done", 2 * NHEAD)
        normed = m.count("normed", NHEAD * NT)
        pt_ready = m.count("pt_ready", NHEAD * NT, 5)
        pt_hi, pt_lo = m.count("pt_hi", NHEAD * NT, 3), m.count("pt_lo", NHEAD * NT, 3)
        pv_done = m.count("pv_done", NHEAD * NT, 5)
        head_hi, head_lo = m.count("head_hi", NHEAD), m.count("head_lo", NHEAD)
        block = ctx.enter_context(nc.Block())

        def wait_job(eng, b, job, ago=0):
            pj_ready.wait(eng, b, where[job] + 1 - ago * NJ)

        def wait_emptied(eng, b, n):
            job, ago = jobs[(n - 2) % NJ], 0 if n >= 2 else 1
            if job in ropes:
                raw_done.wait(eng, b, ropes.index(job) + 1 - ago * NR)
            else:
                pj_dve.wait(eng, b, by_dve.index(job) + 1 - ago * len(by_dve))

        def wait_heads_free(eng, b, n):
            p = n // (2 * QM)
            wait_job(eng, b, ("o", (p - 1) % NPAIR * NC_ + NC_ - 1), 0 if p > 0 else 1)

        @block.sync
        def _(sp):
            ratio_in.open(sp)
            for s in w_in:
                s.open(sp)
            sp.dma_start(wv_sb[:, :, :], wv.rearrange("(c p) n -> p c n", p=P)).then_inc(wv_in, 16)
            for dst, src in ((cos_t, tables[0]), (sin_t, tables[1]), (mask_t, mask), (perm_t, perm)):
                sp.dma_start(dst[:, :], src).then_inc(small_in, 16)
            sp.dma_start(sink_t[:, :], sink.to_broadcast([P, NHEAD])).then_inc(small_in, 16)
            with sp.Fori(0, B) as b:
                wait_job(sp, b, ("v", NT - 1), 1)
                y_hi_done.wait(sp, b, 0)
                y_lo_done.wait(sp, b, 0)
                sp.dma_start(y[:, :, :], gate[bass.ds(b, 1)].rearrange("o p c t -> p (o c) t")).then_inc(ratio_in.sem, 16)
                for w in range(NW):
                    w_hi_done.wait(sp, b, w - RAWS + 1)
                    w_lo_done.wait(sp, b, w - RAWS + 1)
                    sp.dma_start(wraw[:, w % RAWS], weights[w].rearrange("p (c n) -> p c n", c=NC_)).then_inc(w_in[w % RAWS].sem, 16)

        @block.gpsimd
        def _(pool):
            for s in (w_lo_done, rcos_done, rsum_done, rope_lo, normed):
                s.open(pool)
            pool.wait_ge(small_in, 16 * 5)

            def weight_lo(b, w):
                w_hi_done.wait(pool, b, w + 1)
                pool.tensor_tensor(w_lo[:, w % SPLITS], wraw[:, w % RAWS], w_hi[:, w % SPLITS].bitcast(F32),
                                   ALU.subtract).then_inc(w_lo_done.sem, 1)

            def after_job(b, job):
                w = weighted.index(job) + SPLITS
                if w < NW:
                    weight_lo(b, w)

            def rope(b, job):
                r = ropes.index(job)
                raw_done.wait(pool, b, r + 1)
                rsum_done.wait(pool, b, r)
                pool.tensor_tensor(rcos[:, :], raw[:, r % 2, :], cos_t[:, :], ALU.mult).then_inc(rcos_done.sem, 1)
                rcos_done.wait(pool, b, r + 1)
                pj_dve.wait(pool, b, by_dve.index((job[0] + "s", job[1])) + 1)
                rope_lo.wait(pool, b, before(r))
                pool.tensor_tensor(rsum[:, :], rcos[:, :], rsin[:, :], ALU.add).then_inc(rsum_done.sem, 1)

            def rope_low(b, job):
                kind, i = job
                r = ropes.index(job)
                if kind == "q":
                    rope_hi.wait(pool, b, before(r) + 1)
                    pool.tensor_tensor(q_lo[:, i % 2, :], rsum[:, :], q_hi[:, i % 2, :].bitcast(F32), ALU.subtract).then_inc(rope_lo.sem, 1)
                else:
                    for h in range(2):
                        rows = slice(h * HD, (h + 1) * HD)
                        rope_hi.wait(pool, b, before(r) + h + 1)
                        rsum_done.wait(pool, b, r + 1)
                        if i > 0:
                            normed.wait(pool, b, (2 * QM * (i - 1) + 3 + AHEAD) * NT)
                        pool.tensor_tensor(kz_lo[rows, i % 2, h, :], rsum[rows, :], kz_hi[rows, i % 2, h, :].bitcast(F32),
                                           ALU.subtract).then_inc(rope_lo.sem, 1)
                        rope_lo.wait(pool, b, before(r) + h + 1)

            def norm(b, n):
                den_done.wait(pool, b, 2 * n + 2)
                settle(pool, pool_passed)
                for q in range(NT):
                    pool.tensor_scalar(probs[:, n % RING, q, :], probs[:, n % RING, q, :], rinv[:, n % RING, q:q + 1], 1.0,
                                       ALU.mult, ALU.mult).then_inc(normed.sem, 1)

            pool.wait_ge(zeroed, 5)
            with pool.Fori(0, B) as b:
                for w in range(SPLITS):
                    weight_lo(b, w)
                for job in ropes[:3]:
                    after_job(b, job)
                    rope(b, job)
                    rope_low(b, job)
                for n in range(AHEAD):
                    norm(b, n)
                for n in range(NHEAD):
                    for job in side_jobs(n):
                        after_job(b, job)
                        if job in ropes:
                            rope(b, job)
                            rope_low(b, job)
                    if n + AHEAD < NHEAD:
                        norm(b, n + AHEAD)
                for oc in range(NC_):
                    after_job(b, ("o", (NPAIR - 1) * NC_ + oc))

        @block.tensor
        def _(pe):
            for s in (pj_ready, sc_ready, pt_ready, pv_done):
                s.open(pe)
            pe.wait_ge(wv_in, 16)
            pe.wait_ge(small_in, 16 * 5)
            pe.wait_ge(zeroed, 5)

            def run(b, kind, i):
                n = where[kind, i]
                bank = pj[n % 2][:, :]
                wait_emptied(pe, b, n)
                if (kind, i) in weighted:
                    w = weighted.index((kind, i))
                    w_lo_done.wait(pe, b, w + 1)
                    if kind == "o":
                        p = i // NC_
                        head_lo.wait(pe, b, (p + 1) * 2 * QM)
                    a_hi, a_lo = (heads_hi, heads_lo) if kind == "o" else (y_hi, y_lo)
                    for c in range(NC_):
                        if kind != "o":
                            y_lo_done.wait(pe, b, c + 1)
                        last = product(pe, bank, w_hi[:, w % SPLITS, c, :], w_lo[:, w % SPLITS, c, :], a_hi[:, c, :], a_lo[:, c, :],
                                       start=c == 0, stop=c == NC_ - 1)
                elif kind == "v":
                    for c in range(NC_):
                        last = pe.matmul(bank, y[:, c, i * P:(i + 1) * P], wv_sb[:, c, :], start=c == 0, stop=c == NC_ - 1)
                else:
                    r = ropes.index((kind[0], i))
                    raw_done.wait(pe, b, r + 1)
                    last = pe.matmul(bank, perm_t[:, :], raw[:, r % 2, :], start=True, stop=True)
                last.then_inc(pj_ready.sem, 1)

            def scores(b, n, q):
                t, h = divmod(n, 2)
                p = t // QM
                s = n * NT + q
                if q == 0:
                    rope_lo.wait(pe, b, rounds[ropes.index(("q", t))])
                    rope_lo.wait(pe, b, rounds[ropes.index(("k", p))])
                masked.wait(pe, b, max(s - 2, 0))
                tokens = slice(q * P, (q + 1) * P)
                product(pe, sc[s % 3][:, :], q_hi[:, t % 2, tokens], q_lo[:, t % 2, tokens], kz_hi[:, p % 2, h, :], kz_lo[:, p % 2, h, :],
                        start=True, stop=True).then_inc(sc_ready.sem, 1)

            def turn(b, n, k):
                if k == 0:
                    normed.wait(pe, b, (n + 1) * NT)
                pt_lo.wait(pe, b, n * NT + k - 1)
                for q in range(NT):
                    last = pe.transpose(pt[k % 2][:, q * P:(q + 1) * P], probs[:, n % RING, q, k * P:(k + 1) * P], ident[:, :])
                last.then_inc(pt_ready.sem, 1)

            def values(b, n, k):
                p = n // (2 * QM)
                if k == 0:
                    head_lo.wait(pe, b, n)
                pt_lo.wait(pe, b, n * NT + k + 1)
                both = slice(p * P, (p + 1) * P)
                product(pe, po[:, :], v_hi[:, k, both], v_lo[:, k, both], pT_hi[:, k, :], pT_lo[:, k, :],
                        start=k == 0, stop=k == NT - 1).then_inc(pv_done.sem, 1)

            with pe.Fori(0, B) as b:
                for kind, i in jobs[:10]:
                    run(b, kind, i)
                pj_dve.wait(pe, b, by_dve.index(("v", NT - 1)) + 1)
                for n in range(AHEAD):
                    for q in range(NT):
                        scores(b, n, q)
                for n in range(NHEAD):
                    more = n + AHEAD < NHEAD
                    for k in range(NT):
                        if more:
                            scores(b, n + AHEAD, k)
                        turn(b, n, k)
                        if k == 1:
                            for kind, i in side_jobs(n):
                                run(b, kind, i)
                    for kind, i in side_jobs(n):
                        if kind != "o":
                            run(b, kind + "s", i)
                    for k in range(NT):
                        values(b, n, k)
                for oc in range(NC_):
                    run(b, "o", (NPAIR - 1) * NC_ + oc)

        @block.scalar
        def _(act):
            for s in (w_hi_done, tanh_done, y_hi_done, raw_done, v_hi_done, rope_hi, exp_done, sink_done, pt_hi, head_hi):
                s.open(act)
            act.wait_ge(small_in, 16 * 5)
            act.wait_ge(zeroed, 5)

            def weight_hi(b, w):
                w_in[w % RAWS].wait(act, b, w // RAWS + 1)
                act.activation(w_hi[:, w % SPLITS], wraw[:, w % RAWS], ACT.Copy).then_inc(w_hi_done.sem, 1)

            def after_job(b, job):
                w = weighted.index(job) + SPLITS
                if w < NW:
                    wait_job(act, b, job)
                    weight_hi(b, w)

            def copy_raw(b, job):
                r = ropes.index(job)
                wait_job(act, b, job)
                rcos_done.wait(act, b, r - 1)
                kind, i = ropes[(r - 2) % NR]
                wait_job(act, b, (kind + "s", i), 0 if r >= 2 else 1)
                act.activation(raw[:, r % 2, :], pj[where[job] % 2][:, :], ACT.Copy).then_inc(raw_done.sem, 1)

            def copy_values(b, i):
                wait_job(act, b, ("v", i))
                pv_done.wait(act, b, 0)
                act.activation(v_hi[:, i, :], pj[where["v", i] % 2][:, :], ACT.Copy).then_inc(v_hi_done.sem, 1)

            def rope_high(b, job):
                kind, i = job
                rsum_done.wait(act, b, ropes.index(job) + 1)
                if kind == "q":
                    sc_ready.wait(act, b, (i - 1) * 2 * NT)
                    act.activation(q_hi[:, i % 2, :], rsum[:, :], ACT.Copy).then_inc(rope_hi.sem, 1)
                else:
                    sc_ready.wait(act, b, (i - 1) * QM * 2 * NT)
                    for h in range(2):
                        rows = slice(h * HD, (h + 1) * HD)
                        act.activation(kz_hi[rows, i % 2, h, :], rsum[rows, :], ACT.Copy).then_inc(rope_hi.sem, 1)

            def exps(b, n, q):
                s = n * NT + q
                masked.wait(act, b, s + 1)
                act.activation(probs[:, n % RING, q, :], probs[:, n % RING, q, :], ACT.Exp, scale=-1.0,
                               bias=negmax[:, n % RING, q:q + 1], accum_out=rowsum[:, n % RING, q:q + 1]).then_inc(exp_done.sem, 1)

            def sinks(b, n):
                act.activation(sinkexp[:, n % RING, :], negmax[:, n % RING, :], ACT.Exp, bias=sink_t[:, n:n + 1]).then_inc(sink_done.sem, 1)

            def turned_high(b, n, k):
                pt_ready.wait(act, b, n * NT + k + 1)
                pv_done.wait(act, b, (n - 1) * NT + k + 1)
                act.activation(pT_hi[:, k, :], pt[k % 2][:, :], ACT.Copy).then_inc(pt_hi.sem, 1)

            def head_high(b, n):
                t, h = divmod(n, 2)
                rows = slice(h * HD, (h + 1) * HD)
                pv_done.wait(act, b, (n + 1) * NT)
                if t % QM == 0:
                    wait_heads_free(act, b, n)
                act.activation(heads_hi[rows, t % QM, :], po[rows, :], ACT.Copy).then_inc(head_hi.sem, 1)

            with act.Fori(0, B) as b:
                pt_ready.wait(act, b, -NT)
                settle(act, act_passed)
                act.activation(probs[:, 0], xT[:, :, bass.ds(b * T, T)], ACT.Tanh, scale=0.5).then_inc(tanh_done.sem, 1)
                wait_job(act, b, ("o", NPAIR * NC_ - 1), 1)
                for w in range(SPLITS):
                    weight_hi(b, w)
                for c in range(NC_):
                    y_done.wait(act, b, c + 1)
                    act.activation(y_hi[:, c, :], y[:, c, :], ACT.Copy).then_inc(y_hi_done.sem, 1)
                copy_raw(b, ("k", 0))
                after_job(b, ("k", 0))
                copy_values(b, 0)
                copy_values(b, 1)
                rope_high(b, ("k", 0))
                copy_raw(b, ("q", 0))
                after_job(b, ("q", 0))
                copy_values(b, 2)
                rope_high(b, ("q", 0))
                copy_values(b, 3)
                copy_raw(b, ("q", 1))
                after_job(b, ("q", 1))
                rope_high(b, ("q", 1))
                for n in range(AHEAD):
                    for q in range(NT):
                        exps(b, n, q)
                    sinks(b, n)
                for n in range(NHEAD):
                    more = n + AHEAD < NHEAD
                    for k in range(NT):
                        turned_high(b, n, k)
                        if more:
                            exps(b, n + AHEAD, k)
                        if k == 1:
                            for job in side_jobs(n):
                                if job in ropes:
                                    copy_raw(b, job)
                                after_job(b, job)
                    if more:
                        sinks(b, n + AHEAD)
                    for job in side_jobs(n):
                        if job in ropes:
                            rope_high(b, job)
                    head_high(b, n)
                for oc in range(NC_):
                    after_job(b, ("o", (NPAIR - 1) * NC_ + oc))

        @block.vector
        def _(dve):
            for s in (y_done, y_lo_done, pj_dve, masked, den_done, pt_lo, head_lo):
                s.open(dve)
            dve.memset(rsin[:, :], 0.0).then_inc(zeroed, 1)
            dve.wait_ge(zeroed, 1)
            for kz in (kz_hi, kz_lo):
                for h in range(2):
                    rows = slice((1 - h) * HD, (2 - h) * HD)
                    zeros = rsin[rows, :].rearrange("p (o t) -> p o t", o=1).to_broadcast([HD, 2, T])
                    dve.tensor_copy(kz[rows, :, h, :], zeros).then_inc(zeroed, 1)
            dve.wait_ge(small_in, 16 * 5)
            dve.tensor_scalar(nsink_t[:, :], sink_t[:, :], -1.0, None, ALU.mult).then_inc(setup, 1)
            dve.wait_ge(setup, 1)
            dve.wait_ge(zeroed, 5)

            def gate_y(b, c):
                dve.scalar_tensor_tensor(y[:, c, :], probs[:, 0, c, :], 1.0, y[:, c, :], ALU.add, ALU.mult).then_inc(y_done.sem, 1)

            def gate_low(b, c):
                y_hi_done.wait(dve, b, c + 1)
                dve.tensor_tensor(y_lo[:, c, :], y[:, c, :], y_hi[:, c, :].bitcast(F32), ALU.subtract).then_inc(y_lo_done.sem, 1)

            def rot_sin(b, job):
                r = ropes.index(job)
                swap = (job[0] + "s", job[1])
                wait_job(dve, b, swap)
                rsum_done.wait(dve, b, r)
                dve.tensor_tensor(rsin[:, :], pj[where[swap] % 2][:, :], sin_t[:, :], ALU.mult).then_inc(pj_dve.sem, 1)

            def values_low(b, i):
                v_hi_done.wait(dve, b, i + 1)
                dve.tensor_tensor(v_lo[:, i, :], pj[where["v", i] % 2][:, :], v_hi[:, i, :].bitcast(F32), ALU.subtract).then_inc(pj_dve.sem, 1)

            def add_out(b, i):
                oc = i % NC_
                wait_job(dve, b, ("o", i))
                if i >= NC_:
                    pj_dve.wait(dve, b, by_dve.index(("o", i - NC_)) + 1)
                x_oc = xT[:, oc, bass.ds(b * T, T)]
                dve.tensor_tensor(x_oc, x_oc, pj[where["o", i] % 2][:, :], ALU.add).then_inc(pj_dve.sem, 1)

            def masking(b, n, q):
                s = n * NT + q
                sc_ready.wait(dve, b, s + 1)
                if q == 0:
                    pt_ready.wait(dve, b, max(n - RING + 1, 0) * NT if n > 0 else -NT)
                    sink_done.wait(dve, b, max(n - RING + 1, 0))
                settle(dve, dve_passed)
                dve.tensor_tensor_reduce(out=probs[:, n % RING, q, :], in0=sc[s % 3][:, :],
                                         in1=mask_t[:, (NT - 1 - q) * P:(NT - 1 - q) * P + T],
                                         scale=-HD ** -0.5, scalar=nsink_t[:, n:n + 1], op0=ALU.add, op1=ALU.min,
                                         accum_out=negmax[:, n % RING, q:q + 1]).then_inc(masked.sem, 1)

            def denominators(b, n):
                exp_done.wait(dve, b, (n + 1) * NT)
                sink_done.wait(dve, b, n + 1)
                normed.wait(dve, b, max(n - RING + 1, 0) * NT)
                dve.tensor_tensor(sinkexp[:, n % RING, :], sinkexp[:, n % RING, :], rowsum[:, n % RING, :], ALU.add).then_inc(den_done.sem, 1)
                den_done.wait(dve, b, 2 * n + 1)
                dve.reciprocal(rinv[:, n % RING, :], sinkexp[:, n % RING, :]).then_inc(den_done.sem, 1)

            def turned_low(b, n, k):
                pt_hi.wait(dve, b, n * NT + k + 1)
                pv_done.wait(dve, b, (n - 1) * NT + k + 1)
                dve.tensor_tensor(pT_lo[:, k, :], pt[k % 2][:, :], pT_hi[:, k, :].bitcast(F32), ALU.subtract).then_inc(pt_lo.sem, 1)

            def head_low(b, n):
                t, h = divmod(n, 2)
                rows = slice(h * HD, (h + 1) * HD)
                head_hi.wait(dve, b, n + 1)
                if t % QM == 0:
                    wait_heads_free(dve, b, n)
                dve.tensor_tensor(heads_lo[rows, t % QM, :], po[rows, :], heads_hi[rows, t % QM, :].bitcast(F32),
                                  ALU.subtract).then_inc(head_lo.sem, 1)

            with dve.Fori(0, B) as b:
                tanh_done.wait(dve, b, 1)
                ratio_in.wait(dve, b, 1)
                gate_y(b, 0)
                for c in range(1, NC_):
                    gate_y(b, c)
                    gate_low(b, c - 1)
                gate_low(b, NC_ - 1)
                values_low(b, 0)
                rot_sin(b, ("k", 0))
                values_low(b, 1)
                values_low(b, 2)
                rot_sin(b, ("q", 0))
                values_low(b, 3)
                rot_sin(b, ("q", 1))
                for n in range(AHEAD):
                    for q in range(NT):
                        masking(b, n, q)
                    denominators(b, n)
                for n in range(NHEAD):
                    more = n + AHEAD < NHEAD
                    for k in range(NT):
                        if more:
                            masking(b, n + AHEAD, k)
                        turned_low(b, n, k)
                        if k == 1:
                            for kind, i in side_jobs(n):
                                if kind == "o":
                                    add_out(b, i)
                    for job in side_jobs(n):
                        if job in ropes:
                            rot_sin(b, job)
                    if more:
                        denominators(b, n + AHEAD)
                    head_low(b, n)
                for oc in range(NC_):
                    add_out(b, (NPAIR - 1) * NC_ + oc)


def gate_all(xT, tanh_buf, y, tanh_done, y_done, ratio_in):

    def load(sp, gate):
        for b in range(B):
            sp.dma_start(y[:, :, b * T:(b + 1) * T], gate[b]).then_inc(ratio_in[b], 16)

    def scalar(act):
        for b in range(B):
            if b >= 2:
                act.wait_ge(y_done, b - 1)
            act.activation(tanh_buf[:, b % 2], xT[:, :, b * T:(b + 1) * T], ACT.Tanh, scale=0.5).then_inc(tanh_done, 1)

    def vector(dve):
        for b in range(B):
            dve.wait_ge(tanh_done, b + 1)
            dve.wait_ge(ratio_in[b], 16)
            y_b = y[:, :, b * T:(b + 1) * T]
            dve.scalar_tensor_tensor(y_b, tanh_buf[:, b % 2], 1.0, y_b, ALU.add, ALU.mult).then_inc(y_done, 1)

    return load, scalar, vector


def split_y(m, xT, y_hi, y_lo, stage, tanh_buf, pair=2):
    ratio_in = m.count("ratio_in", pair, by=16)
    tanh_done, y_done = m.count("tanh_done", pair), m.count("y_done", pair)
    hi_done, lo_done = m.count("y_hi_done", pair), m.count("y_lo_done", pair)
    passed = m.sem("y_passed")

    def x_of(turn, bi):
        return xT[:, :, bass.ds(turn * (pair * T) + bi * T, T)]

    def load(sp, turn, bi, gate):
        lo_done.wait(sp, turn, bi)
        hi_done.wait(sp, turn, bi)
        sp.dma_start(stage[:, :, :], gate[bass.ds(turn * pair + bi, 1)].rearrange("o p c t -> p (o c) t")).then_inc(ratio_in.sem, 16)

    def scalar_tanh(act, turn, bi):
        y_done.wait(act, turn, bi)
        settle(act, passed)
        act.activation(tanh_buf[:, :, :], x_of(turn, bi), ACT.Tanh, scale=0.5).then_inc(tanh_done.sem, 1)

    def scalar_hi(act, turn, bi):
        y_done.wait(act, turn, bi + 1)
        act.activation(y_hi[:, :, bi * T:(bi + 1) * T], stage[:, :, :], ACT.Copy).then_inc(hi_done.sem, 1)

    def vector_y(dve, turn, bi):
        tanh_done.wait(dve, turn, bi + 1)
        ratio_in.wait(dve, turn, bi + 1)
        dve.scalar_tensor_tensor(stage[:, :, :], tanh_buf[:, :, :], 1.0, stage[:, :, :], ALU.add, ALU.mult).then_inc(y_done.sem, 1)

    def vector_lo(dve, turn, bi):
        hi_done.wait(dve, turn, bi + 1)
        dve.tensor_tensor(y_lo[:, :, bi * T:(bi + 1) * T], stage[:, :, :], y_hi[:, :, bi * T:(bi + 1) * T].bitcast(F32),
                          ALU.subtract).then_inc(lo_done.sem, 1)

    class Parts:
        pass

    parts = Parts()
    parts.ratio_in, parts.tanh_done, parts.y_done, parts.hi_done, parts.lo_done = ratio_in, tanh_done, y_done, hi_done, lo_done
    parts.load, parts.scalar_tanh, parts.scalar_hi, parts.vector_y, parts.vector_lo = load, scalar_tanh, scalar_hi, vector_y, vector_lo
    return parts


NG = 4
NHID = 4 * NG
PAIR = 2
UNITS = NG * PAIR


def sparse_ffn(nc, xT, gate, weights):
    with ExitStack() as ctx:
        m = Space(nc, ctx, "ffn")
        raw = m.sb("raw", [P, 2, 3, C])
        gu_hi, gu_lo = m.sb("gu_hi", [P, 4, 2, NC_, P], F32R), m.sb("gu_lo", [P, 4, 2, NC_, P], F32R)
        wd_hi, wd_lo = m.sb("wd_hi", [P, 2, 4, C], F32R), m.sb("wd_lo", [P, 2, 4, C], F32R)
        y_hi, y_lo = m.sb("y_hi", [P, NC_, PAIR * T], F32R), m.sb("y_lo", [P, NC_, PAIR * T], F32R)
        stage = m.sb("stage", [P, NC_, T])
        tanh_g, hid, size = m.sb("tanh_g", [P, 2, T]), m.sb("hid", [P, 4, T]), m.sb("size", [P, 4, T])
        beats, votes = m.sb("beats", [P, 6, T], BF16), m.sb("votes", [P, 4, T], BF16)
        hs_hi, hs_lo = m.sb("hs_hi", [P, 4, T], F32R), m.sb("hs_lo", [P, 4, T], F32R)
        pg = [m.ps(f"pg{i}", [P, T]) for i in range(2)]
        pu = [m.ps(f"pu{i}", [P, T]) for i in range(2)]
        pd = [m.ps(f"pd{i}", [P, T]) for i in range(NC_)]

        NTL = 4 * UNITS
        raw_in = [m.count(f"raw_in{s}", NHID // 2, by=16) for s in range(2)]
        w_hi_done, w_lo_done = m.count("w_hi_done", 2 * NHID, 4), m.count("w_lo_done", 2 * NHID, 4)
        g_ready, u_ready = m.count("g_ready", NTL, 9), m.count("u_ready", NTL, 9)
        tanh_g_done = m.count("tanh_g_done", NTL)
        silu_done, hid_done = m.count("silu_done", NTL, 3), m.count("hid_done", NTL, 3)
        size_done = m.count("size_done", NTL, 5)
        beats_done, votes_done = m.count("beats_done", 3 * UNITS, 4), m.count("votes_done", 4 * UNITS, 5)
        sparse_done = m.count("sparse_done", NTL, 5)
        hs_hi_done, hs_lo_done = m.count("hs_hi_done", NTL, 5), m.count("hs_lo_done", NTL, 5)
        down_done, added = m.count("down_done", NTL, 14), m.count("added", NC_ * UNITS, 9)
        yp = split_y(m, xT, y_hi, y_lo, stage, size, PAIR)
        block = ctx.enter_context(nc.Block())

        def weights_free(eng, bp, t, part):
            g, j = divmod(t, 4)
            if part == "gu":
                u_ready.wait(eng, bp, 8 * (g - 1) + 4 + j + 1)
            else:
                down_done.wait(eng, bp, 8 * (g - 2) + 4 + j + 1)

        def load_raw(sp, bp, t):
            w_lo_done.wait(sp, bp, 2 * (t - 1))
            w_hi_done.wait(sp, bp, 2 * (t - 1))
            sp.dma_start(raw[:, t % 2], weights[t]).then_inc(raw_in[t % 2].sem, 16)

        @block.sync
        def _(sp):
            for s in (yp.ratio_in, *raw_in):
                s.open(sp)
            with sp.Fori(0, B // PAIR) as bp:
                for bi in range(PAIR):
                    if bi == 1:
                        load_raw(sp, bp, 0)
                        load_raw(sp, bp, 1)
                    yp.load(sp, bp, bi, gate)
                for t in range(2, NHID):
                    load_raw(sp, bp, t)

        @block.tensor
        def _(pe):
            for s in (g_ready, u_ready, down_done):
                s.open(pe)

            def up(bp, v, j):
                g, bi = divmod(v, PAIR)
                i = 4 * v + j
                if bi == 0:
                    w_lo_done.wait(pe, bp, 2 * (4 * g + j) + 1)
                if v < PAIR and j == 0:
                    yp.lo_done.wait(pe, bp, bi + 1)
                for w, (bank, ready, free) in enumerate(((pg, g_ready, silu_done), (pu, u_ready, hid_done))):
                    free.wait(pe, bp, i - 1)
                    cols = slice(bi * T, (bi + 1) * T)
                    for c in range(NC_):
                        last = product(pe, bank[i % 2][:, :], gu_hi[:, j, w, c, :], gu_lo[:, j, w, c, :],
                                       y_hi[:, c, cols], y_lo[:, c, cols], c == 0, c == NC_ - 1)
                    last.then_inc(ready.sem, 1)

            def down(bp, v, j):
                g, bi = divmod(v, PAIR)
                hs_lo_done.wait(pe, bp, 4 * v + j + 1)
                if bi == 0:
                    w_lo_done.wait(pe, bp, 2 * (4 * g + j) + 2)
                for oc in range(NC_):
                    if j == 0:
                        added.wait(pe, bp, NC_ * (v - 1) + oc + 1)
                    cols = slice(oc * P, (oc + 1) * P)
                    last = product(pe, pd[oc][:, :], wd_hi[:, g % 2, j, cols], wd_lo[:, g % 2, j, cols],
                                   hs_hi[:, j, :], hs_lo[:, j, :], j == 0, j == 3)
                last.then_inc(down_done.sem, 1)

            with pe.Fori(0, B // PAIR) as bp:
                for v in range(UNITS):
                    up(bp, v, 0)
                    up(bp, v, 1)
                    for j in range(2):
                        if v > 0:
                            down(bp, v - 1, j)
                        up(bp, v, j + 2)
                    if v > 0:
                        down(bp, v - 1, 2)
                        down(bp, v - 1, 3)
                for j in range(4):
                    down(bp, UNITS - 1, j)

        @block.scalar
        def _(act):
            for s in (yp.tanh_done, yp.hi_done, w_hi_done, tanh_g_done, size_done, hs_hi_done):
                s.open(act)

            def weight_hi(bp, t):
                g, j = divmod(t, 4)
                raw_in[t % 2].wait(act, bp, t // 2 + 1)
                weights_free(act, bp, t, "gu")
                act.activation(gu_hi[:, j].rearrange("p w c n -> p (w c n)"), raw[:, t % 2, 0:2, :].rearrange("p w n -> p (w n)"),
                               ACT.Copy).then_inc(w_hi_done.sem, 1)
                weights_free(act, bp, t, "down")
                act.activation(wd_hi[:, g % 2, j, :], raw[:, t % 2, 2, :], ACT.Copy).then_inc(w_hi_done.sem, 1)

            def tanh_of(bp, i):
                g_ready.wait(act, bp, i + 1)
                hid_done.wait(act, bp, i - 1)
                act.activation(tanh_g[:, i % 2, :], pg[i % 2][:, :], ACT.Tanh, scale=0.5).then_inc(tanh_g_done.sem, 1)

            def sizes(bp, i):
                hid_done.wait(act, bp, i + 1)
                beats_done.wait(act, bp, 3 * (i // 4))
                act.activation(size[:, i % 4, :], hid[:, i % 4, :], ACT.Abs).then_inc(size_done.sem, 1)

            def sparse_hi(bp, v):
                for j in range(4):
                    i = 4 * v + j
                    sparse_done.wait(act, bp, i + 1)
                    down_done.wait(act, bp, i - 3)
                    hs_lo_done.wait(act, bp, i - 3)
                    act.activation(hs_hi[:, j, :], hid[:, j, :], ACT.Copy).then_inc(hs_hi_done.sem, 1)

            with act.Fori(0, B // PAIR) as bp:
                size_free = UNITS * 3
                beats_done.wait(act, bp, 0)
                yp.scalar_tanh(act, bp, 0)
                weight_hi(bp, 0)
                yp.scalar_hi(act, bp, 0)
                yp.scalar_tanh(act, bp, 1)
                weight_hi(bp, 1)
                yp.scalar_hi(act, bp, 1)
                weight_hi(bp, 2)
                weight_hi(bp, 3)
                for v in range(UNITS):
                    for j in range(4):
                        tanh_of(bp, 4 * v + j)
                        if v == 0 and j == 0:
                            yp.y_done.wait(act, bp, 2)
                        sizes(bp, 4 * v + j)
                        if v % PAIR == 1 and v < UNITS - 1 and j >= 1:
                            weight_hi(bp, 4 * (v // PAIR + 1) + j - 1)
                    sparse_hi(bp, v)
                    if v % PAIR == 1 and v < UNITS - 1:
                        weight_hi(bp, 4 * (v // PAIR + 1) + 3)

        @block.gpsimd
        def _(pool):
            w_lo_done.open(pool)
            with pool.Fori(0, B // PAIR) as bp:
                for t in range(NHID):
                    g, j = divmod(t, 4)
                    w_hi_done.wait(pool, bp, 2 * t + 1)
                    weights_free(pool, bp, t, "gu")
                    pool.tensor_tensor(gu_lo[:, j].rearrange("p w c n -> p (w c n)"), raw[:, t % 2, 0:2, :].rearrange("p w n -> p (w n)"),
                                       gu_hi[:, j].rearrange("p w c n -> p (w c n)").bitcast(F32), ALU.subtract).then_inc(w_lo_done.sem, 1)
                    w_hi_done.wait(pool, bp, 2 * t + 2)
                    weights_free(pool, bp, t, "down")
                    pool.tensor_tensor(wd_lo[:, g % 2, j, :], raw[:, t % 2, 2, :], wd_hi[:, g % 2, j, :].bitcast(F32),
                                       ALU.subtract).then_inc(w_lo_done.sem, 1)

        @block.vector
        def _(dve):
            for s in (yp.y_done, yp.lo_done, silu_done, hid_done, beats_done, votes_done, sparse_done, hs_lo_done, added):
                s.open(dve)

            def hidden(bp, i):
                tanh_g_done.wait(dve, bp, i + 1)
                dve.scalar_tensor_tensor(tanh_g[:, i % 2, :], tanh_g[:, i % 2, :], 1.0, pg[i % 2][:, :],
                                         ALU.add, ALU.mult).then_inc(silu_done.sem, 1)
                u_ready.wait(dve, bp, i + 1)
                silu_done.wait(dve, bp, i + 1)
                hs_lo_done.wait(dve, bp, i - 3)
                dve.tensor_tensor(hid[:, i % 4, :], tanh_g[:, i % 2, :], pu[i % 2][:, :], ALU.mult).then_inc(hid_done.sem, 1)

            def sparsify(bp, v):
                size_done.wait(dve, bp, 4 * (v + 1))
                sparse_done.wait(dve, bp, 4 * v)
                for i, (lo, n) in enumerate(((0, 3), (3, 2), (5, 1))):
                    dve.tensor_tensor(beats[:, lo:lo + n, :], size[:, i:i + 1, :].to_broadcast([P, n, T]), size[:, i + 1:4, :],
                                      ALU.is_ge).then_inc(beats_done.sem, 1)
                beats_done.wait(dve, bp, 3 * (v + 1))
                dve.tensor_tensor(votes[:, 0:2, :], beats[:, 0:6:3, :], beats[:, 1:6:3, :], ALU.add).then_inc(votes_done.sem, 1)
                dve.tensor_tensor(votes[:, 2:4, :], beats[:, 1:3, :], beats[:, 3:5, :], ALU.add).then_inc(votes_done.sem, 1)
                votes_done.wait(dve, bp, 4 * v + 2)
                dve.tensor_tensor(votes[:, 0:4:3, :], votes[:, 0:4:3, :], beats[:, 2:6:3, :], ALU.add).then_inc(votes_done.sem, 1)
                dve.tensor_tensor(votes[:, 1:3, :], votes[:, 1:3, :], beats[:, 0:6:5, :], ALU.subtract).then_inc(votes_done.sem, 1)
                votes_done.wait(dve, bp, 4 * v + 4)
                for j, (op, limit) in enumerate(((ALU.is_ge, 2.0), (ALU.is_ge, 1.0), (ALU.is_le, 0.0), (ALU.is_le, 1.0))):
                    dve.scalar_tensor_tensor(hid[:, j, :], votes[:, j, :], limit, hid[:, j, :], op, ALU.mult).then_inc(sparse_done.sem, 1)
                for j in range(4):
                    hs_hi_done.wait(dve, bp, 4 * v + j + 1)
                    dve.tensor_tensor(hs_lo[:, j, :], hid[:, j, :], hs_hi[:, j, :].bitcast(F32), ALU.subtract).then_inc(hs_lo_done.sem, 1)

            def add_out(bp, v):
                bi = v % PAIR
                down_done.wait(dve, bp, 4 * (v + 1))
                for oc in range(NC_):
                    x_oc = xT[:, oc, bass.ds(bp * (PAIR * T) + bi * T, T)]
                    dve.scalar_tensor_tensor(x_oc, pd[oc][:, :], 0.5, x_oc, ALU.mult, ALU.add).then_inc(added.sem, 1)

            with dve.Fori(0, B // PAIR) as bp:
                for bi in range(PAIR):
                    yp.vector_y(dve, bp, bi)
                    yp.vector_lo(dve, bp, bi)
                for v in range(UNITS):
                    for j in range(4):
                        hidden(bp, 4 * v + j)
                    sparsify(bp, v)
                    if v > 0:
                        add_out(bp, v - 1)
                add_out(bp, UNITS - 1)


NCH = 16
BINS = 16


def fourier_attention(nc, xT, gate, wq, wkv, woT, dft, idftT, norm_mat, dc_cols):
    with ExitStack() as ctx:
        m = Space(nc, ctx, "fft")
        raw_w = [m.sb(f"raw_{n}", [P, NC_, C]) for n in ("q", "kv", "o")]
        f_sb, fi_sb = m.sb("dft", [P, NC_, C]), m.sb("idft", [P, NC_, C])
        fold = [m.sb(f"fold_{n}", [P, NC_, C]) for n in ("kv", "q", "o")]
        norm_t, dc_t = m.sb("norm", [P, P]), m.sb("dc", [P, 3])
        y, tanh_buf = m.sb("y", [P, NC_, B * T]), m.sb("tanh_buf", [P, 2, NC_, T])
        square, rnorm = m.sb("square", [P, 2, 2, T]), m.sb("rnorm", [P, 2, T])
        hat_k, hat_q = m.sb("hat_k", [P, 2, T]), m.sb("hat_q", [P, 2, T])
        total = m.sb("total", [P, 2, T])
        other = m.sb("other", [P, 3, T])
        parts = m.sb("parts", [P, 4, T])
        prod = m.sb("prod", [P, 1, 4, T])
        pl = [m.ps(f"pl{i}", [P, T]) for i in range(4)]
        pn = [m.ps(f"pn{i}", [P, T]) for i in range(2)]
        pd = [m.ps(f"pd{i}", [P, T]) for i in range(2)]

        ratio_in = [m.sem(f"ratio_in{b}") for b in range(B)]
        tanh_done, y_done, w_in = m.sem("tanh_done"), m.sem("y_done"), m.sem("w_in")
        folded, fold_copied = m.sem("folded"), m.sem("fold_copied")
        planes = m.count("planes", 8, 5)
        squared, norm_ready = m.count("squared", 8, 5), m.count("norm_ready", 4, 3)
        rnormed, hatted = m.count("rnormed", 8, 5), m.count("hatted", 8, 5)
        summed, others = m.count("summed", 4, 3), m.count("others", 6, 4)
        dve_parts, pool_parts = m.count("dve_parts", 4, 3), m.count("pool_parts", 4, 3)
        prod_re, prod_im = m.count("prod_re", 2, 3), m.count("prod_im", 2, 3)
        out_ready, added = m.count("out_ready", NC_, 9), m.count("added", NC_, 9)
        load_y, act_y, dve_y = gate_all(xT, tanh_buf, y, tanh_done, y_done, ratio_in)
        block = ctx.enter_context(nc.Block())

        @block.sync
        def _(sp):
            for dst, src in ((raw_w[0], wq), (raw_w[1], wkv), (raw_w[2], woT), (f_sb, dft), (fi_sb, idftT)):
                sp.dma_start(dst[:, :, :], src.rearrange("(k p) n -> p k n", p=P)).then_inc(w_in, 16)
            sp.dma_start(norm_t[:, :], norm_mat).then_inc(w_in, 16)
            sp.dma_start(dc_t[:, :], dc_cols).then_inc(w_in, 16)
            load_y(sp, gate)

        @block.tensor
        def _(pe):
            for s in (planes, norm_ready, out_ready):
                s.open(pe)
            pe.wait_ge(w_in, 16 * 7)
            n = 0
            for w in (raw_w[1], raw_w[0]):
                for mc in range(NC_):
                    if n >= 4:
                        pe.wait_ge(fold_copied, n - 3)
                    for half in range(2):
                        for k in range(2):
                            last = pe.matmul(pl[n % 4][:, :].rearrange("p (r h s) -> p r h s", r=2, h=2)[:, :, half, :],
                                             w[:, 2 * half + k, mc * P:(mc + 1) * P],
                                             f_sb[:, 2 * half + k, :].rearrange("p (r h s) -> p r h s", r=2, h=2)[:, :, half, :],
                                             start=k == 0, stop=k == 1)
                    last.then_inc(folded, 1)
                    n += 1
            for ft in range(4):
                pe.wait_ge(fold_copied, n - 3)
                for k in range(2):
                    last = pe.matmul(pl[n % 4][:, :], fi_sb[:, 2 * (ft % 2) + k, ft * P:(ft + 1) * P],
                                     raw_w[2][:, 2 * (ft % 2) + k, :], start=k == 0, stop=k == 1)
                last.then_inc(folded, 1)
                n += 1
            pe.wait_ge(fold_copied, 12)

            def norm(b, u):
                squared.wait(pe, b, 2 * u + 2)
                rnormed.wait(pe, b, 2 * u - 3)
                for r in range(2):
                    last = pe.matmul(pn[u % 2][:, :], norm_t[:, :], square[:, u % 2, r, :], start=r == 0, stop=r == 1)
                last.then_inc(norm_ready.sem, 1)

            def out(b, oc):
                added.wait(pe, b, oc - 1)
                if oc == 0:
                    prod_re.wait(pe, b, 2)
                    prod_im.wait(pe, b, 2)
                for ft in range(4):
                    last = pe.matmul(pd[oc % 2][:, :], fold[2][:, ft, oc * P:(oc + 1) * P], prod[:, 0, ft, :],
                                     start=ft == 0, stop=ft == 3)
                last.then_inc(out_ready.sem, 1)

            def unit(b, u):
                kind, half = u % 2, u // 2
                for r in range(2):
                    tile = 2 * r + half
                    hatted.wait(pe, b, 2 * u + r - 3)
                    squared.wait(pe, b, 2 * u + r - 3)
                    for c in range(NC_):
                        last = pe.matmul(pl[2 * (u % 2) + r][:, :], fold[kind][:, c, tile * P:(tile + 1) * P],
                                         y[:, c, bass.ds(b * T, T)], start=c == 0, stop=c == NC_ - 1)
                    last.then_inc(planes.sem, 1)

            with pe.Fori(0, B) as b:
                pe.wait_ge(y_done, b + 1)
                for u in range(4):
                    unit(b, u)
                    if u >= 1:
                        norm(b, u - 1)
                norm(b, 3)
                for oc in range(NC_):
                    out(b, oc)

        @block.scalar
        def _(act):
            squared.open(act)
            rnormed.open(act)
            for n in range(12):
                act.wait_ge(folded, n + 1)
                act.activation(fold[n // 4][:, n % 4, :], pl[n % 4][:, :], ACT.Copy).then_inc(fold_copied, 1)
            act_y(act)

            def rnorm_of(b, u):
                norm_ready.wait(act, b, u + 1)
                hatted.wait(act, b, 2 * u - 2)
                act.activation(rnorm[:, u % 2, :], pn[u % 2][:, :], ACT.Ln).then_inc(rnormed.sem, 1)
                rnormed.wait(act, b, 2 * u + 1)
                act.activation(rnorm[:, u % 2, :], rnorm[:, u % 2, :], ACT.Exp, scale=-0.5).then_inc(rnormed.sem, 1)

            with act.Fori(0, B) as b:
                for u in range(4):
                    norm_ready.wait(act, b, u - 1)
                    for r in range(2):
                        planes.wait(act, b, 2 * u + r + 1)
                        act.activation(square[:, u % 2, r, :], pl[2 * (u % 2) + r][:, :], ACT.Square).then_inc(squared.sem, 1)
                    if u >= 1:
                        rnorm_of(b, u - 1)
                rnorm_of(b, 3)

        @block.vector
        def _(dve):
            for s in (hatted, summed, others, dve_parts, prod_im, added):
                s.open(dve)
            dve.wait_ge(w_in, 16 * 7)
            dve_y(dve)

            def hat(b, u):
                kind, half = u % 2, u // 2
                hat_t = hat_k if kind == 0 else hat_q
                rnormed.wait(dve, b, 2 * u + 2)
                if kind == 0:
                    summed.wait(dve, b, 2 * half)
                else:
                    pool_parts.wait(dve, b, 2 * half)
                    dve_parts.wait(dve, b, 2 * half)
                for r in range(2):
                    dve.tensor_tensor(hat_t[:, r, :], pl[2 * (u % 2) + r][:, :], rnorm[:, u % 2, :], ALU.mult).then_inc(hatted.sem, 1)

            def sums(b, half):
                hatted.wait(dve, b, 4 * half + 2)
                pool_parts.wait(dve, b, 2 * half)
                others.wait(dve, b, 3 * half)
                for r in range(2):
                    dve.tensor_tensor_scan(total[:, r, :], dc_t[:, 2:3].to_broadcast([P, T]), hat_k[:, r, :], 0.0,
                                           ALU.mult, ALU.add).then_inc(summed.sem, 1)
                summed.wait(dve, b, 2 * half + 2)
                dve_parts.wait(dve, b, 2 * half)
                dve.tensor_scalar(other[:, 0, :], total[:, 1, :], dc_t[:, 0:1], None, ALU.mult).then_inc(others.sem, 1)
                dve.tensor_scalar(other[:, 1, :], total[:, 0, :], dc_t[:, 0:1], None, ALU.mult).then_inc(others.sem, 1)
                others.wait(dve, b, 3 * half + 2)
                dve.scalar_tensor_tensor(other[:, 2, :], total[:, 1, :], dc_t[:, 1:2], other[:, 1, :],
                                         ALU.mult, ALU.add).then_inc(others.sem, 1)

            def product_im(b, half):
                hatted.wait(dve, b, 4 * half + 4)
                others.wait(dve, b, 3 * half + 3)
                prod_im.wait(dve, b, half)
                dve.tensor_tensor(parts[:, 2, :], hat_q[:, 0, :], other[:, 0, :], ALU.mult).then_inc(dve_parts.sem, 1)
                dve.tensor_tensor(parts[:, 3, :], hat_q[:, 1, :], other[:, 2, :], ALU.mult).then_inc(dve_parts.sem, 1)
                dve_parts.wait(dve, b, 2 * half + 2)
                out_ready.wait(dve, b, 0)
                dve.tensor_tensor(prod[:, 0, 2 + half, :], parts[:, 2, :], parts[:, 3, :], ALU.add).then_inc(prod_im.sem, 1)

            with dve.Fori(0, B) as b:
                hat(b, 0)
                sums(b, 0)
                hat(b, 1)
                product_im(b, 0)
                hat(b, 2)
                sums(b, 1)
                hat(b, 3)
                product_im(b, 1)
                for oc in range(NC_):
                    out_ready.wait(dve, b, oc + 1)
                    x_oc = xT[:, oc, bass.ds(b * T, T)]
                    dve.tensor_tensor(x_oc, x_oc, pd[oc % 2][:, :], ALU.add).then_inc(added.sem, 1)

        @block.gpsimd
        def _(pool):
            pool_parts.open(pool)
            prod_re.open(pool)
            with pool.Fori(0, B) as b:
                for half in range(2):
                    hatted.wait(pool, b, 4 * half + 4)
                    others.wait(pool, b, 3 * half + 1)
                    prod_re.wait(pool, b, half)
                    pool.tensor_tensor(parts[:, 0, :], hat_q[:, 0, :], total[:, 0, :], ALU.mult).then_inc(pool_parts.sem, 1)
                    pool.tensor_tensor(parts[:, 1, :], hat_q[:, 1, :], other[:, 0, :], ALU.mult).then_inc(pool_parts.sem, 1)
                    pool_parts.wait(pool, b, 2 * half + 2)
                    out_ready.wait(pool, b, 0)
                    pool.tensor_tensor(prod[:, 0, half, :], parts[:, 0, :], parts[:, 1, :], ALU.subtract).then_inc(prod_re.sem, 1)


NE, HE = 8, 256
NEH = NE * HE // P


def expert_ffn(nc, ident, xT, gate, wg1T, wg2T, wupT, bup, wdownT, bdown, lower, onehot, out):
    with ExitStack() as ctx:
        m = Space(nc, ctx, "moe")
        wu_sb, wd_sb = m.sb("wu", [P, NC_, NE * HE]), m.sb("wd", [P, NEH, C])
        wg1_sb, wg2_sb = m.sb("wg1", [P, NC_, NE]), m.sb("wg2", [NE, NE])
        bd_sb, onehot_sb = m.sb("bd", [NE, C]), m.sb("onehot", [NE, NE * P])
        bup_t, half_bup, lower_t = m.sb("bup", [P, NEH]), m.sb("half_bup", [P, NEH]), m.sb("lower", [P, NE, NE])
        y, tanh_buf = m.sb("y", [P, NC_, B * T]), m.sb("tanh_buf", [P, 2, NC_, T])
        inner, logit = m.sb("inner", [NE, T]), m.sb("logit", [P, NT, NE])
        above, equal = m.sb("above", [P, NT, NE, NE]), m.sb("equal", [P, NT, NE, NE])
        rank, top, share = m.sb("rank", [P, NT, NE]), m.sb("top", [P, NT]), m.sb("share", [P, NT, NE])
        denom = m.sb("denom", [P, NT])
        scoreT, score2 = m.sb("scoreT", [NE, B * T]), m.sb("score2", [NE, T])
        spread, tanh_u = m.sb("spread", [P, 2, T]), m.sb("tanh_u", [P, 2, T])
        lin, hid = m.sb("lin", [P, T]), m.sb("hid", [P, 2, T])
        x2, rows = m.sb("x2", [P, NC_, T]), m.sb("rows", [P, NT, C])
        pu = [m.ps(f"pu{i}", [P, T]) for i in range(2)]
        pb = [m.ps(f"pb{i}", [P, T]) for i in range(2)]
        pd = [m.ps(f"pd{i}", [P, T]) for i in range(NT)]

        ratio_in = [m.sem(f"ratio_in{b}") for b in range(B)]
        tanh_done, y_done = m.sem("tanh_done"), m.sem("y_done")
        act_passed, pe_passed = m.sem("act_passed"), m.sem("pe_passed")
        small_in, wu_in, wd_in, setup = m.sem("small_in"), m.sem("wu_in"), m.sem("wd_in"), m.sem("setup")
        inner_ready, inner_done = m.count("inner_ready", 1), m.count("inner_done", 1)
        logit_ready, ranked = m.count("logit_ready", 1), m.count("ranked", 12)
        share_exp = m.count("share_exp", 1)
        turned, turned_out = m.count("turned", 1), m.count("turned_out", 1)
        up_ready = m.count("up_ready", NEH)
        tanh_u_done, lin_done, hid_done = m.count("tanh_u_done", NEH, 3), m.count("lin_done", NEH, 3), m.count("hid_done", NEH, 3)
        spread_ready, spread_done = m.count("spread_ready", NE, 3), m.count("spread_done", NE, 3)
        down_done = m.count("down_done", NEH, 3)
        extra_ready = m.count("extra_ready", 2, 1)
        rows_done, stored = m.count("rows_done", NT), m.count("stored", NT, 1, by=16)
        batch_done = m.count("batch_done", NT)
        load_y, act_y, dve_y = gate_all(xT, tanh_buf, y, tanh_done, y_done, ratio_in)
        block = ctx.enter_context(nc.Block())

        @block.sync
        def _(sp):
            stored.open(sp)
            load_y(sp, gate)
            sp.dma_start(wg1_sb[:, :, :], wg1T.rearrange("(c p) e -> p c e", p=P)).then_inc(small_in, 16)
            for dst, src in ((wg2_sb, wg2T), (bd_sb, bdown), (onehot_sb, onehot), (bup_t, bup)):
                sp.dma_start(dst[:, :], src).then_inc(small_in, 16)
            sp.dma_start(lower_t[:, :, :], lower).then_inc(small_in, 16)
            for c in range(NC_):
                sp.dma_start(wu_sb[:, c, :], wupT[c * P:(c + 1) * P, :]).then_inc(wu_in, 16)
            sp.dma_start(wd_sb[:, :, :], wdownT.rearrange("(t p) n -> p t n", p=P)).then_inc(wd_in, 16)
            with sp.Fori(0, B) as b:
                for t in range(NT):
                    rows_done.wait(sp, b, t + 1)
                    sp.dma_start(out[bass.ds(b, 1), t * P:(t + 1) * P, :].rearrange("o p c -> p (o c)"), rows[:, t, :]).then_inc(stored.sem, 16)
            stored.wait(sp, B, 0)

        @block.tensor
        def _(pe):
            for s in (inner_ready, logit_ready, turned, up_ready, spread_ready, down_done, batch_done):
                s.open(pe)
            pe.wait_ge(small_in, 16 * 6)
            with pe.Fori(0, B) as b:
                pe.wait_ge(y_done, b + 1)
                turned_out.wait(pe, b, 0)
                for c in range(NC_):
                    last = pe.matmul(pb[0][0:NE, :], wg1_sb[:, c, :], y[:, c, bass.ds(b * T, T)], start=c == 0, stop=c == NC_ - 1)
                last.then_inc(inner_ready.sem, 1)
                inner_done.wait(pe, b, 1)
                for t in range(NT):
                    last = pe.matmul(pb[1][:, t * NE:(t + 1) * NE], inner[:, t * P:(t + 1) * P], wg2_sb[:, :], start=True, stop=True)
                last.then_inc(logit_ready.sem, 1)
                ranked.wait(pe, b, 12)
                for t in range(NT):
                    last = pe.transpose(pb[0][0:NE, t * P:(t + 1) * P], share[:, t, :], ident[:, :])
                last.then_inc(turned.sem, 1)
            turned_out.wait(pe, B, 0)
            pe.wait_ge(wu_in, 16 * NC_)

            def up(b, i):
                lin_done.wait(pe, b, i - 1)
                tanh_u_done.wait(pe, b, i - 1)
                for c in range(NC_):
                    last = pe.matmul(pu[i % 2][:, :], wu_sb[:, c, i * P:(i + 1) * P], y[:, c, bass.ds(b * T, T)],
                                     start=c == 0, stop=c == NC_ - 1)
                last.then_inc(up_ready.sem, 1)

            def spread_scores(b, e):
                spread_done.wait(pe, b, e - 1)
                settle(pe, pe_passed)
                pe.matmul(pb[e % 2][:, :], onehot_sb[:, e * P:(e + 1) * P], scoreT[:, bass.ds(b * T, T)],
                          start=True, stop=True).then_inc(spread_ready.sem, 1)

            def down(b, i):
                hid_done.wait(pe, b, i + 1)
                for t in range(NT):
                    last = pe.matmul(pd[t][:, :], hid[:, i % 2, t * P:(t + 1) * P], wd_sb[:, i, :], start=False, stop=i == NEH - 1)
                    if i == NEH - 1:
                        last.then_inc(batch_done.sem, 1)
                if i < NEH - 1:
                    last.then_inc(down_done.sem, 1)
                else:
                    pe.sem_inc(down_done.sem, 1)

            def begin(b):
                extra_ready.wait(pe, b, 2)
                rows_done.wait(pe, b, 0)
                for t in range(NT):
                    pe.matmul(pd[t][:, :], score2[:, t * P:(t + 1) * P], bd_sb[:, :], start=True, stop=False)
                    for c in range(NC_):
                        pe.matmul(pd[t][:, c * P:(c + 1) * P], x2[:, c, t * P:(t + 1) * P], ident[:, :],
                                  start=False, stop=False, skip_group_check=True)

            with pe.Fori(0, B) as b:
                for e in range(NE):
                    spread_scores(b, e)
                    for i in (2 * e, 2 * e + 1):
                        up(b, i)
                        if i == 0:
                            begin(b)
                            pe.wait_ge(wd_in, 16)
                        else:
                            down(b, i - 1)
                down(b, NEH - 1)

        @block.scalar
        def _(act):
            for s in (inner_done, share_exp, turned_out, tanh_u_done, spread_done, extra_ready, rows_done):
                s.open(act)
            act_y(act)
            with act.Fori(0, B) as b:
                inner_ready.wait(act, b, 1)
                logit_ready.wait(act, b, 0)
                act.activation(inner[:, :], pb[0][0:NE, :], ACT.Tanh).then_inc(inner_done.sem, 1)
                ranked.wait(act, b, 8)
                act.activation(share[:, :, :], share[:, :, :], ACT.Exp).then_inc(share_exp.sem, 1)
                turned.wait(act, b, 1)
                settle(act, act_passed)
                act.activation(scoreT[:, bass.ds(b * T, T)], pb[0][0:NE, :], ACT.Copy).then_inc(turned_out.sem, 1)
            turned_out.wait(act, B, 0)
            act.wait_ge(setup, 1)

            def spread_copy(b, e):
                spread_ready.wait(act, b, e + 1)
                lin_done.wait(act, b, 2 * (e - 1))
                act.activation(spread[:, e % 2, :], pb[e % 2][:, :], ACT.Copy).then_inc(spread_done.sem, 1)

            with act.Fori(0, B) as b:
                batch_done.wait(act, b, 0)
                settle(act, act_passed)
                act.activation(score2[:, :], scoreT[:, bass.ds(b * T, T)], ACT.Copy, scale=2.0).then_inc(extra_ready.sem, 1)
                act.activation(x2[:, :, :], xT[:, :, bass.ds(b * T, T)], ACT.Copy, scale=2.0).then_inc(extra_ready.sem, 1)
                for e in range(NE):
                    spread_copy(b, e)
                    for i in (2 * e, 2 * e + 1):
                        up_ready.wait(act, b, i + 1)
                        hid_done.wait(act, b, i - 1)
                        act.activation(tanh_u[:, i % 2, :], pu[i % 2][:, :], ACT.Tanh, scale=0.5,
                                       bias=half_bup[:, i:i + 1]).then_inc(tanh_u_done.sem, 1)
                stored.wait(act, b, 0)
                for t in range(NT):
                    batch_done.wait(act, b, t + 1)
                    act.activation(rows[:, t, :], pd[t][:, :], ACT.Copy, scale=0.5).then_inc(rows_done.sem, 1)

        @block.vector
        def _(dve):
            for s in (ranked, lin_done, hid_done):
                s.open(dve)
            dve.wait_ge(small_in, 16 * 6)
            dve.tensor_scalar(half_bup[:, :], bup_t[:, :], 0.5, None, ALU.mult).then_inc(setup, 1)
            dve_y(dve)
            with dve.Fori(0, B) as b:
                own, rival = [P, NT, NE, NE], [P, NT, NE, NE]
                step = [0]

                def did(ins):
                    step[0] += 1
                    ins.then_inc(ranked.sem, 1)
                    ranked.wait(dve, b, step[0])

                logit_ready.wait(dve, b, 1)
                turned.wait(dve, b, 0)
                did(dve.tensor_copy(logit[:, :, :], pb[1][:, 0:NT * NE].rearrange("p (t e) -> p t e", e=NE)))
                mine = logit[:, :, :].rearrange("p t (e o) -> p t e o", o=1).to_broadcast(own)
                theirs = logit[:, :, :].rearrange("p t (o e) -> p t o e", o=1).to_broadcast(rival)
                did(dve.tensor_tensor(above[:, :, :, :], theirs, mine, ALU.is_gt))
                did(dve.tensor_tensor(equal[:, :, :, :], theirs, mine, ALU.is_equal))
                did(dve.tensor_tensor(equal[:, :, :, :], equal[:, :, :, :],
                                      lower_t[:, :, :].rearrange("p (o e) f -> p o e f", o=1).to_broadcast(own), ALU.mult))
                did(dve.tensor_tensor(above[:, :, :, :], above[:, :, :, :], equal[:, :, :, :], ALU.add))
                did(dve.tensor_reduce(rank[:, :, :], above[:, :, :, :], AX_X, ALU.add))
                did(dve.tensor_reduce(top[:, :], logit[:, :, :], AX_X, ALU.max))
                did(dve.tensor_tensor(share[:, :, :], logit[:, :, :], top[:, :].rearrange("p (t o) -> p t o", o=1).to_broadcast([P, NT, NE]),
                                      ALU.subtract))
                share_exp.wait(dve, b, 1)
                did(dve.scalar_tensor_tensor(share[:, :, :], rank[:, :, :], 2.0, share[:, :, :], ALU.is_lt, ALU.mult))
                did(dve.tensor_reduce(denom[:, :], share[:, :, :], AX_X, ALU.add))
                did(dve.reciprocal(denom[:, :], denom[:, :]))
                did(dve.tensor_tensor(share[:, :, :], share[:, :, :], denom[:, :].rearrange("p (t o) -> p t o", o=1).to_broadcast([P, NT, NE]),
                                      ALU.mult))
            with dve.Fori(0, B) as b:
                for i in range(NEH):
                    e = i // 2
                    tanh_u_done.wait(dve, b, i + 1)
                    spread_done.wait(dve, b, e + 1)
                    hid_done.wait(dve, b, i)
                    dve.scalar_tensor_tensor(lin[:, :], pu[i % 2][:, :], bup_t[:, i:i + 1], spread[:, e % 2, :],
                                             ALU.add, ALU.mult).then_inc(lin_done.sem, 1)
                    lin_done.wait(dve, b, i + 1)
                    down_done.wait(dve, b, i - 1)
                    dve.scalar_tensor_tensor(hid[:, i % 2, :], tanh_u[:, i % 2, :], 1.0, lin[:, :],
                                             ALU.add, ALU.mult).then_inc(hid_done.sem, 1)


def build(nc, a, out):
    gates = nc.dram_tensor("gates", (NCOND, B, P, NC_, T), F32, kind="Internal").ap()
    with ExitStack() as ctx:
        ident = ctx.enter_context(nc.sbuf_tensor("ident", [P, P], F32))
        xT = ctx.enter_context(nc.sbuf_tensor("xT", [P, NC_, B * T], F32))
        ident_done = ctx.enter_context(nc.semaphore("ident_done"))
        with nc.Block() as block:
            @block.gpsimd
            def _(pool):
                pool.memset(ident[:, :], 0.0).then_inc(ident_done, 1)
                pool.wait_ge(ident_done, 1)
                pool.affine_select(out=ident[:, :], in_=ident[:, :], compare_op=ALU.not_equal, fill=1.0, base=0,
                                   pattern=[[-1, P]], channel_multiplier=1).then_inc(ident_done, 1)
                pool.wait_ge(ident_done, 2)
        prepare(nc, a["x"], a["fside"], a["cond"], a["w"], a["u"], ident, xT, gates)
        attention(nc, ident, xT, gates[0], a["att"], a["wv"], a["sink"], (a["cos"], a["sin"]), a["mask"], a["perm"])
        sparse_ffn(nc, xT, gates[1], a["ffn"])
        fourier_attention(nc, xT, gates[2], a["fft_q"], a["fft_kv"], a["fft_oT"], a["dft"], a["idftT"], a["norm"], a["dc"])
        expert_ffn(nc, ident, xT, gates[3], a["g1T"], a["g2T"], a["upT"], a["bup"], a["downT"], a["bdown"], a["lower"], a["onehot"], out)


def constants():
    c = {}
    freq = np.float32(1.0 / 1024.0) ** np.linspace(0, 1, HD // 4, dtype=np.float32)
    freq = np.concatenate([freq.astype(np.float32), np.zeros(HD // 4, np.float32)])
    theta = np.arange(T, dtype=np.float32)[None, :] * freq[:, None]
    c["cos"] = np.tile(np.cos(theta), (4, 1)).astype(np.float32)
    c["sin"] = np.concatenate([np.sin(theta), -np.sin(theta)] * 2).astype(np.float32)
    off = np.arange(MW)[None, :] - (NT - 1) * P - np.arange(P)[:, None]
    c["mask"] = np.where((off <= 0) & (off > -128), MASKED, 0.0).astype(np.float32)
    r = np.arange(P)
    c["perm"] = (r[:, None] == (r ^ (HD // 2))[None, :]).astype(np.float32)
    n, s = np.arange(2 * BINS)[:, None], np.arange(BINS)[None, :]
    theta = np.pi * n * s / BINS
    re, im = np.cos(theta), -np.sin(theta)
    im[:, 0] = (-1.0) ** n[:, 0]
    weight = np.where(s == 0, 1.0, 2.0)
    dft, idft = np.zeros((C, 2, NCH, BINS)), np.zeros((C, 2, NCH, BINS))
    for h in range(NCH):
        rows = slice(2 * BINS * h, 2 * BINS * (h + 1))
        for plane, f in ((0, re), (1, im)):
            dft[rows, plane, h] = f
            idft[rows, plane, h] = f * weight / (2 * BINS)
    c["dft"], c["idftT"] = (d.reshape(C, C).astype(np.float32) for d in (dft, idft))
    c["norm"] = ((r[:, None] // BINS == r[None, :] // BINS) * np.where(r[:, None] % BINS == 0, 1.0, 2.0)).astype(np.float32)
    c["dc"] = np.stack([r % BINS != 0, r % BINS == 0, r >= 0], 1).astype(np.float32)
    e = np.arange(NE)
    c["lower"] = np.tile((e[None, :] < e[:, None]).astype(np.float32)[None], (P, 1, 1))
    c["onehot"] = np.repeat(np.eye(NE, dtype=np.float32), P, axis=1)
    return c


def layouts(v):
    def columns(names):
        return np.stack([v[n] for n in names]).reshape(NCOND, NC_, P).transpose(2, 0, 1).reshape(P, NCOND * NC_)

    def hidden_tiles(w):
        return w.reshape(NC_, P, NG, P, 4).transpose(2, 4, 1, 0, 3).reshape(NHID, P, C)

    conds = ["L0_cond", "L0_cond2", "L1_cond", "L1_cond2"]
    wqkv, nq = v["L0_attn_W_qkv"], NKV * QM * HD
    wq = wqkv[:, :nq].reshape(C, NPAIR, 2, QM, HD).transpose(0, 1, 3, 2, 4).reshape(C, nq)
    wk = wqkv[:, nq:nq + NKV * HD]
    wo = v["L0_attn_W_out"].reshape(NPAIR, 2, QM, HD, C).transpose(0, 2, 1, 3, 4).reshape(nq, C)

    def attention_tile(kind, i):
        if kind == "o":
            p, oc = divmod(i, NC_)
            tile = wo[p * QM * P:(p + 1) * QM * P, oc * P:(oc + 1) * P]
        else:
            tile = (wk if kind == "k" else wq)[:, i * P:(i + 1) * P]
        return tile.reshape(NC_, P, P).transpose(1, 0, 2).reshape(P, C)

    return {
        "x": v["x"], "fside": v["fside_BxSxS_0"], "cond": v["cond_512"],
        "w": columns([n + "_w" for n in conds]), "u": columns([n + "_u" for n in conds]),
        "att": np.stack([attention_tile(*job) for job in attention_jobs() if job[0] in ("k", "q", "o")]),
        "wv": wqkv[:, nq + NKV * HD:],
        "sink": v["L0_attn_s"].reshape(NPAIR, 2, QM).transpose(0, 2, 1).reshape(1, NHEAD),
        "ffn": np.stack([hidden_tiles(v["L0_ffn_w_gate"]), hidden_tiles(v["L0_ffn_w_up"]),
                         v["L0_ffn_w_down"].reshape(NG, P, 4, C).transpose(0, 2, 1, 3).reshape(NHID, P, C)], 2),
        "fft_q": v["L1_attn_W_q"], "fft_kv": v["L1_attn_W_kv"], "fft_oT": v["L1_attn_W_o"].T,
        "g1T": v["L1_ffn_Wg1"].T, "g2T": v["L1_ffn_Wg2"].T, "upT": v["L1_ffn_Wup"].reshape(NE * HE, C).T,
        "bup": v["L1_ffn_bup"].reshape(NEH, P).T,
        "downT": v["L1_ffn_Wdown"].transpose(0, 2, 1).reshape(NE * HE, C), "bdown": v["L1_ffn_bdown"],
    }


def kernel(**inputs):
    import concourse.bacc as bacc
    from concourse.bass_utils import run_bass_kernel_spmd

    nc = bacc.Bacc("TRN2", target_bir_lowering=False, num_devices=1)
    arrays, aps = {}, {}
    for name, a in {**layouts(inputs), **constants()}.items():
        a = np.ascontiguousarray(a)
        arrays[f"in_{name}"] = a
        aps[name] = nc.dram_tensor(f"in_{name}", a.shape, mybir.dt.from_np(a.dtype), kind="ExternalInput").ap()
    out = nc.dram_tensor("out", (B, T, C), F32, kind="ExternalOutput").ap()
    build(nc, aps, out)
    r = run_bass_kernel_spmd(nc, [arrays], core_ids=[0])
    return r.results[0]["out"]
```

```python
from contextlib import ExitStack

import numpy as np
import concourse.bass as bass
from concourse import mybir

F32 = mybir.dt.float32
BF16 = mybir.dt.bfloat16
F32R = mybir.dt.float32r
ALU = mybir.AluOpType
ACT = mybir.ActivationFunctionType
AX_X = mybir.AxisListType.X

P = 128
B, T, C = 4, 512, 512
NC_ = C // P
NT = T // P
TD = 128
NCOND = 4
E30 = float(np.exp(np.float32(30.0)))



class Count:

    def __init__(self, sem, per, credit, by):
        self.sem, self.per, self.credit, self.by = sem, per, credit, by

    def open(self, eng):
        eng.sem_inc(self.sem, self.credit)

    def at(self, turn, n):
        assert n * self.by + self.credit > 0, self.sem
        return turn * (self.per * self.by) + (n * self.by + self.credit)


def settle(eng, passed):
    eng.sem_inc(passed, 1)


class Space:

    shared = {}

    def __init__(self, nc, ctx, tag):
        self.nc, self.ctx, self.tag = nc, ctx, tag

    def sb(self, name, shape, dt=F32):
        return self.ctx.enter_context(self.nc.sbuf_tensor(f"{self.tag}_{name}", shape, dt))

    def ps(self, name, shape, dt=F32):
        return self.ctx.enter_context(self.nc.psum_tensor(f"{self.tag}_{name}", shape, dt))

    def sem(self, name):
        return self.ctx.enter_context(self.nc.semaphore(f"{self.tag}_{name}"))

    def passed(self, engine):
        if (self.nc, engine) not in self.shared:
            self.shared[self.nc, engine] = self.nc.alloc_semaphore(name=f"{engine}_passed")
        return self.shared[self.nc, engine]

    def count(self, name, per, credit=1, by=1):
        return Count(self.sem(name), per, credit, by)


def prepare(nc, x, fside, cond, ws, us, ident, xT, sideT, gates, small):
    wcol, ucol, decay, lngain = small
    with ExitStack() as ctx:
        m = Space(nc, ctx, "prep")
        xin, fin = m.sb("xin", [P, NT, C]), m.sb("fin", [P, NT, C])
        fT, ek, ekv = m.sb("fT", [P, NC_, T]), m.sb("ek", [P, NC_, T]), m.sb("ekv", [P, NC_, T])
        fwd_n, fwd_d = m.sb("fwd_n", [P, NC_, T]), m.sb("fwd_d", [P, NC_, T])
        bwd_n, bwd_d = m.sb("bwd_n", [P, NC_, T + 1]), m.sb("bwd_d", [P, NC_, T + 1])
        euk, eukv, ratio = m.sb("euk", [P, NC_, T]), m.sb("eukv", [P, NC_, T]), m.sb("ratio", [P, NC_, T])
        emb = m.sb("emb", [P, B, TD])
        embsum, embtanh, half = m.sb("embsum", [P, B]), m.sb("embtanh", [P, B]), m.sb("half", [P, B])
        tp = m.ps("tp", [P, 2 * NC_, T])

        params_in, par_act, par_dve = m.sem("params_in"), m.sem("par_act"), m.sem("par_dve")
        sp_passed, act_passed, dve_passed = m.passed("sp"), m.passed("act"), m.passed("dve")
        f_in, x_in = m.count("f_in", 1, by=16), m.count("x_in", 1, by=16)
        side_stored, ratio_stored = m.count("side_stored", NC_, 17, by=16), m.count("ratio_stored", NC_, 17, by=16)
        f_turned, x_turned, x_copied = m.count("f_turned", NC_), m.count("x_turned", NC_), m.count("x_copied", NC_, 5)
        fT_done, ek_done, euk_done = m.count("fT_done", NC_), m.count("ek_done", NC_), m.count("euk_done", NC_, 5)
        ekv_done = m.count("ekv_done", 2 * NC_, 9)
        scans, eukv_done = m.count("scans", 4 * NC_, 17), m.count("eukv_done", NC_, 5)
        den_dve, den_pool = m.count("den_dve", 2 * NC_), m.count("den_pool", NC_, 5)
        rden_done, num_done, ratio_done = m.count("rden_done", 2 * NC_), m.count("num_done", 2 * NC_, 9), m.count("ratio_done", NC_, 5)
        block = ctx.enter_context(nc.Block())

        @block.sync
        def _(sp):
            for s in (f_in, x_in, side_stored, ratio_stored):
                s.open(sp)
            sp.dma_start(wcol[:, :], ws).then_inc(params_in, 16)
            sp.dma_start(ucol[:, :], us).then_inc(params_in, 16)
            sp.dma_start(emb[:, :, :], cond.rearrange("(o b) d -> o b d", o=1).to_broadcast([P, B, TD])).then_inc(params_in, 16)

            def load(b):
                sp.wait_ge(f_turned.sem, f_turned.at(b, 0))
                settle(sp, sp_passed)
                sp.dma_start(fin[:, :, :], fside[bass.ds(b, 1)].rearrange("o (t p) c -> p (o t) c", p=P)).then_inc(f_in.sem, 16)
                sp.wait_ge(x_turned.sem, x_turned.at(b, 0))
                settle(sp, sp_passed)
                sp.dma_start(xin[:, :, :], x[bass.ds(b, 1)].rearrange("o (t p) c -> p (o t) c", p=P)).then_inc(x_in.sem, 16)

            def store_sides(b):
                for c in range(NC_):
                    sp.wait_ge(fT_done.sem, fT_done.at(b, c + 1))
                    settle(sp, sp_passed)
                    sp.dma_start(sideT[bass.ds(b, 1), :, c, :].rearrange("o p t -> p (o t)"), fT[:, c, :]).then_inc(side_stored.sem, 16)

            def store_ratios(b):
                for c in range(NC_):
                    sp.wait_ge(ratio_done.sem, ratio_done.at(b, c + 1))
                    settle(sp, sp_passed)
                    sp.dma_start(gates[0, bass.ds(b, 1), :, c, :].rearrange("o p t -> p (o t)"), ratio[:, c, :]).then_inc(ratio_stored.sem, 16)

            load(0)
            with sp.Fori(0, B - 1) as b:
                store_sides(b)
                load(b + 1)
                store_ratios(b)
            store_sides(B - 1)
            store_ratios(B - 1)
            for s in (side_stored, ratio_stored):
                sp.wait_ge(s.sem, s.at(B, 0))

        @block.tensor
        def _(pe):
            f_turned.open(pe)
            x_turned.open(pe)
            with pe.Fori(0, B) as b:
                for c in range(NC_):
                    pe.wait_ge(f_in.sem, f_in.at(b, 1))
                    pe.wait_ge(euk_done.sem, euk_done.at(b, c + 1 - NC_))
                    for t in range(NT):
                        last = pe.transpose(tp[:, c, t * P:(t + 1) * P], fin[:, t, c * P:(c + 1) * P], ident[:, :])
                    last.then_inc(f_turned.sem, 1)
                for c in range(NC_):
                    pe.wait_ge(x_in.sem, x_in.at(b, 1))
                    pe.wait_ge(x_copied.sem, x_copied.at(b, c + 1 - NC_))
                    for t in range(NT):
                        last = pe.transpose(tp[:, NC_ + c, t * P:(t + 1) * P], xin[:, t, c * P:(c + 1) * P], ident[:, :])
                    last.then_inc(x_turned.sem, 1)

        @block.scalar
        def _(act):
            for s in (fT_done, ek_done, euk_done, rden_done):
                s.open(act)
            act.wait_ge(params_in, 16 * 3)
            act.activation(wcol[:, :], wcol[:, :], ACT.Exp).then_inc(par_act, 1)
            act.wait_ge(par_act, 1)
            act.activation(wcol[:, :], wcol[:, :], ACT.Exp, scale=-1.0).then_inc(par_act, 1)
            act.wait_ge(par_dve, 1)
            act.activation(embtanh[:, :], embsum[:, :], ACT.Tanh, scale=0.5).then_inc(par_act, 1)
            act.wait_ge(par_dve, 3)
            act.activation(lngain[:, :], lngain[:, :], ACT.Ln).then_inc(par_act, 1)
            act.wait_ge(par_act, 4)

            def exponentials(b, c):
                act.wait_ge(f_turned.sem, f_turned.at(b, c + 1))
                if c == 0:
                    act.wait_ge(side_stored.sem, side_stored.at(b, 0))
                act.wait_ge(eukv_done.sem, eukv_done.at(b, c + 1 - NC_))
                act.wait_ge(ekv_done.sem, ekv_done.at(b, 2 * (c + 1 - NC_)))
                act.activation(fT[:, c, :], tp[:, c, :], ACT.Copy).then_inc(fT_done.sem, 1)
                act.wait_ge(scans.sem, scans.at(b, 4 * (c + 1 - NC_)))
                act.activation(ek[:, c, :], tp[:, c, :], ACT.Exp).then_inc(ek_done.sem, 1)
                act.wait_ge(ratio_done.sem, ratio_done.at(b, c + 1 - NC_))
                act.activation(euk[:, c, :], tp[:, c, :], ACT.Exp, bias=ucol[:, c:c + 1]).then_inc(euk_done.sem, 1)

            def reciprocal(b, c):
                act.wait_ge(den_dve.sem, den_dve.at(b, 2 * c + 2))
                act.activation(euk[:, c, :], euk[:, c, :], ACT.Ln).then_inc(rden_done.sem, 1)
                act.wait_ge(rden_done.sem, rden_done.at(b, 2 * c + 1))
                settle(act, act_passed)
                act.activation(euk[:, c, :], euk[:, c, :], ACT.Exp, scale=-1.0, bias=lngain[:, bass.ds(b, 1)]).then_inc(rden_done.sem, 1)

            with act.Fori(0, B) as b:
                exponentials(b, 0)
                exponentials(b, 1)
                for c in range(NC_):
                    if c + 2 < NC_:
                        exponentials(b, c + 2)
                    reciprocal(b, c)

        @block.vector
        def _(dve):
            for s in (x_copied, ekv_done, scans, eukv_done, den_dve):
                s.open(dve)
            dve.wait_ge(params_in, 16 * 3)
            dve.tensor_reduce(embsum[:, :], emb[:, :, :], AX_X, ALU.add).then_inc(par_dve, 1)
            dve.wait_ge(par_act, 3)
            dve.tensor_scalar(half[:, :], embtanh[:, :], 0.25, 0.75, ALU.mult, ALU.add).then_inc(par_dve, 1)
            dve.tensor_scalar(lngain[:, :], embtanh[:, :], 0.05, 0.45, ALU.mult, ALU.add).then_inc(par_dve, 1)
            dve.wait_ge(par_dve, 3)
            for b in range(B):
                dve.tensor_scalar(decay[:, b, :], wcol[:, :], half[:, b:b + 1], None, ALU.mult).then_inc(par_dve, 1)
            dve.memset(bwd_n[:, :, T:T + 1], 0.0).then_inc(par_dve, 1)
            dve.memset(bwd_d[:, :, T:T + 1], 0.0).then_inc(par_dve, 1)
            dve.wait_ge(par_dve, 3 + B + 2)
            with dve.Fori(0, B) as b:
                for c in range(NC_):
                    dve.wait_ge(ek_done.sem, ek_done.at(b, c + 1))
                    dve.tensor_scalar(ek[:, c, :], ek[:, c, :], E30, None, ALU.min).then_inc(ekv_done.sem, 1)
                    dve.wait_ge(ekv_done.sem, ekv_done.at(b, 2 * c + 1))
                    dve.tensor_tensor(ekv[:, c, :], ek[:, c, :], fT[:, c, :], ALU.mult).then_inc(ekv_done.sem, 1)
                    dve.wait_ge(ekv_done.sem, ekv_done.at(b, 2 * c + 2))
                    dve.wait_ge(num_done.sem, num_done.at(b, 2 * (c + 1 - NC_)))
                    dve.wait_ge(den_pool.sem, den_pool.at(b, c + 1 - NC_))
                    dve.wait_ge(ratio_done.sem, ratio_done.at(b, c + 1 - NC_))
                    d = decay[:, bass.ds(b, 1), c:c + 1].rearrange("p o k -> p (o k)").to_broadcast([P, T])
                    for fwd, bwd, v in ((fwd_d, bwd_d, ek), (fwd_n, bwd_n, ekv)):
                        dve.tensor_tensor_scan(fwd[:, c, :], d, v[:, c, :], 0.0, ALU.mult, ALU.add).then_inc(scans.sem, 1)
                        dve.tensor_tensor_scan(bwd[:, c, 0:T][:, ::-1], v[:, c, ::-1], d, 0.0, ALU.add, ALU.mult).then_inc(scans.sem, 1)
                    dve.wait_ge(euk_done.sem, euk_done.at(b, c + 1))
                    dve.scalar_tensor_tensor(eukv[:, c, :], euk[:, c, :], E30, fT[:, c, :], ALU.min, ALU.mult).then_inc(eukv_done.sem, 1)
                    dve.wait_ge(eukv_done.sem, eukv_done.at(b, c + 1))
                    dve.wait_ge(scans.sem, scans.at(b, 4 * c + 1))
                    dve.scalar_tensor_tensor(euk[:, c, :], euk[:, c, :], E30, fwd_d[:, c, :], ALU.min, ALU.add).then_inc(den_dve.sem, 1)
                    dve.wait_ge(x_turned.sem, x_turned.at(b, c + 1))
                    settle(dve, dve_passed)
                    dve.tensor_copy(xT[:, c, bass.ds(b * T, T)], tp[:, NC_ + c, :]).then_inc(x_copied.sem, 1)
                    dve.wait_ge(den_pool.sem, den_pool.at(b, c + 1))
                    dve.tensor_scalar(euk[:, c, :], euk[:, c, :], 1e-8, None, ALU.max).then_inc(den_dve.sem, 1)

        @block.gpsimd
        def _(pool):
            for s in (den_pool, num_done, ratio_done):
                s.open(pool)

            def multiply(b, c):
                pool.wait_ge(rden_done.sem, rden_done.at(b, 2 * c + 2))
                pool.wait_ge(num_done.sem, num_done.at(b, 2 * c + 2))
                if c == 0:
                    pool.wait_ge(ratio_stored.sem, ratio_stored.at(b, 0))
                pool.tensor_tensor(ratio[:, c, :], fwd_n[:, c, :], euk[:, c, :], ALU.mult).then_inc(ratio_done.sem, 1)

            with pool.Fori(0, B) as b:
                for c in range(NC_):
                    pool.wait_ge(den_dve.sem, den_dve.at(b, 2 * c + 1))
                    pool.wait_ge(scans.sem, scans.at(b, 4 * c + 4))
                    pool.tensor_tensor(euk[:, c, :], euk[:, c, :], bwd_d[:, c, 1:T + 1], ALU.add).then_inc(den_pool.sem, 1)
                    pool.tensor_tensor(fwd_n[:, c, :], fwd_n[:, c, :], bwd_n[:, c, 1:T + 1], ALU.add).then_inc(num_done.sem, 1)
                    pool.wait_ge(num_done.sem, num_done.at(b, 2 * c + 1))
                    pool.wait_ge(eukv_done.sem, eukv_done.at(b, c + 1))
                    pool.tensor_tensor(fwd_n[:, c, :], fwd_n[:, c, :], eukv[:, c, :], ALU.add).then_inc(num_done.sem, 1)
                    if c >= 1:
                        multiply(b, c - 1)
                multiply(b, NC_ - 1)


def product(pe, bank, a_hi, a_lo, b_hi, b_lo, start, stop):
    pe.matmul(bank, a_hi, b_hi, start=start, stop=False)
    pe.matmul(bank, a_hi, b_lo, start=False, stop=False)
    return pe.matmul(bank, a_lo, b_hi, start=False, stop=stop)


NKV, QM, HD = 8, 4, 64
NPAIR = NKV // 2
NTILE = NPAIR * QM
NHEAD = 2 * NTILE
MASKED = -1e30
MW = T + (NT - 1) * P
RAWS, SPLITS = 3, 2
AHEAD = 2


def attention_jobs():
    jobs = [("k", 0), ("q", 0), ("ks", 0), ("qs", 0), ("q", 1), ("v", 0), ("qs", 1), ("v", 1), ("v", 2), ("v", 3)]
    for n in range(NHEAD):
        jobs += side_jobs(n) + [(kind + "s", i) for kind, i in side_jobs(n) if kind != "o"]
    jobs += [("o", (NPAIR - 1) * NC_ + oc) for oc in range(NC_)]
    return jobs


def side_jobs(n):
    t, h = divmod(n, 2)
    p, j = divmod(t, QM)
    jobs = [("o", (p - 1) * NC_ + oc) for oc in range(NC_) if p > 0 and j == h == 0]
    if h == 0 and t + 2 < NTILE:
        jobs.append(("q", t + 2))
    if h == 1 and j == 1 and p + 1 < NPAIR:
        jobs.append(("k", p + 1))
    return jobs


SLOT = NHEAD // NC_
LATER = NCOND - 1


def attention(nc, ident, xT, sideT, gates, small, weights, wv, sink, tables, mask, perm):
    with ExitStack() as ctx:
        m = Space(nc, ctx, "att")
        wraw = m.sb("wraw", [P, RAWS, NC_, P])
        w_hi, w_lo = m.sb("w_hi", [P, SPLITS, NC_, P], F32R), m.sb("w_lo", [P, SPLITS, NC_, P], F32R)
        wv_sb = m.sb("wv", [P, NC_, NKV * HD])
        g_work = m.sb("g_work", [P, NC_, T])
        g_den, g_eukv = g_work[:, 0:LATER, :], g_work[:, LATER, :]
        g_num, g_f = wv_sb[:, 0:LATER, :], wv_sb[:, LATER, :]
        g_ek, g_ekv, g_fwd = m.sb("g_ek", [P, T]), m.sb("g_ekv", [P, T]), m.sb("g_fwd", [P, T])
        g_bwd_n, g_bwd_d = m.sb("g_bwd_n", [P, T + 1]), m.sb("g_bwd_d", [P, T + 1])
        _, ucol, decay, lngain = small
        NU = NC_ * LATER
        y_hi, y_lo = m.sb("y_hi", [P, NC_, T], F32R), m.sb("y_lo", [P, NC_, T], F32R)
        v_hi, v_lo = m.sb("v_hi", [P, NT, NKV * HD], F32R), m.sb("v_lo", [P, NT, NKV * HD], F32R)
        kz_hi, kz_lo = m.sb("kz_hi", [P, 2, 2, T], F32R), m.sb("kz_lo", [P, 2, 2, T], F32R)
        q_hi, q_lo = m.sb("q_hi", [P, 2, T], F32R), m.sb("q_lo", [P, 2, T], F32R)
        cos_t, sin_t, mask_t = m.sb("cos", [P, T]), m.sb("sin", [P, T]), m.sb("mask", [P, MW])
        perm_t = m.sb("perm", [P, P])
        sink_t, nsink_t = m.sb("sink", [P, NHEAD]), m.sb("nsink", [P, NHEAD])
        raw, rcos, rsin, rsum = m.sb("raw", [P, 2, T]), m.sb("rcos", [P, T]), m.sb("rsin", [P, T]), m.sb("rsum", [P, T])
        probs = m.sb("probs", [P, AHEAD + 1, NT, T])
        y = probs[:, AHEAD]
        pT_hi, pT_lo = m.sb("pT_hi", [P, NT, T], F32R), m.sb("pT_lo", [P, NT, T], F32R)
        negmax, rowsum = m.sb("negmax", [P, AHEAD + 1, NT]), m.sb("rowsum", [P, AHEAD + 1, NT])
        sinkexp, rinv = m.sb("sinkexp", [P, AHEAD + 1, NT]), m.sb("rinv", [P, AHEAD + 1, NT])
        heads_hi, heads_lo = m.sb("heads_hi", [P, QM, T], F32R), m.sb("heads_lo", [P, QM, T], F32R)
        pj = [m.ps(f"pj{i}", [P, T]) for i in range(2)]
        sc = [m.ps(f"sc{i}", [P, T]) for i in range(3)]
        pt = [m.ps(f"pt{i}", [P, T]) for i in range(2)]
        po = m.ps("po", [P, T])

        RING = AHEAD + 1
        jobs = attention_jobs()
        where = {job: n for n, job in enumerate(jobs)}
        ropes = [j for j in jobs if j[0] in ("k", "q")]
        by_dve = [j for j in jobs if j[0] in ("ks", "qs", "v", "o")]
        weighted = [j for j in jobs if j[0] in ("k", "q", "o")]
        NJ, NR, NW = len(jobs), len(ropes), len(weighted)
        assert NJ % 2 == 0 and NR % 2 == 0 and NW % RAWS == 0 and NW % SPLITS == 0
        rounds = np.cumsum([2 if kind == "k" else 1 for kind, _ in ropes]).tolist()
        before = lambda r: rounds[r - 1] if r > 0 else 0

        sp_passed, act_passed = m.passed("sp"), m.passed("act")
        dve_passed, pool_passed = m.passed("dve"), m.passed("pool")
        wv_in, small_in, zeroed, setup = m.count("wv_in", 1, by=16), m.sem("small_in"), m.sem("zeroed"), m.sem("setup")
        w_in = [m.count(f"w_in{s}", NW // RAWS, 16, by=16) for s in range(RAWS)]
        w_hi_done, w_lo_done = m.count("w_hi_done", NW, RAWS), m.count("w_lo_done", NW, RAWS)
        ratio_in = m.count("ratio_in", 1, by=16)
        tanh_done, y_done = m.count("tanh_done", 1), m.count("y_done", NC_)
        y_hi_done, y_lo_done = m.count("y_hi_done", NC_), m.count("y_lo_done", NC_)
        pj_ready = m.count("pj_ready", NJ, NJ)
        raw_done, pj_dve = m.count("raw_done", NR, 3), m.count("pj_dve", len(by_dve), 3)
        v_hi_done = m.count("v_hi_done", NT)
        rcos_done, rsum_done = m.count("rcos_done", NR, 2), m.count("rsum_done", NR, 2)
        rope_hi, rope_lo = m.count("rope_hi", rounds[-1], 3), m.count("rope_lo", rounds[-1], 3)
        sc_ready, masked = m.count("sc_ready", NHEAD * NT, NHEAD * NT + 8), m.count("masked", NHEAD * NT, 4)
        exp_done, sink_done = m.count("exp_done", NHEAD * NT), m.count("sink_done", NHEAD)
        den_done = m.count("den_done", 2 * NHEAD)
        normed = m.count("normed", NHEAD * NT)
        pt_ready = m.count("pt_ready", NHEAD * NT, 9)
        pt_hi, pt_lo = m.count("pt_hi", NHEAD * NT, 3), m.count("pt_lo", NHEAD * NT, 3)
        pv_done = m.count("pv_done", NHEAD * NT, 5)
        head_hi, head_lo = m.count("head_hi", NHEAD), m.count("head_lo", NHEAD)
        g_f_in, g_stored = m.count("g_f_in", NC_, 16, by=16), m.count("g_stored", NC_, 16, by=16)
        g_ek_done, g_ekv_done, g_euk_done = m.count("g_ek_done", NC_), m.count("g_ekv_done", 2 * NC_), m.count("g_euk_done", NU)
        g_clipped, g_eukv_done, g_scans = m.count("g_clipped", NU), m.count("g_eukv_done", NU), m.count("g_scans", 4 * NU)
        g_den_done, g_max_done, g_num_done = m.count("g_den_done", 2 * NU), m.count("g_max_done", NU), m.count("g_num_done", 2 * NU)
        g_rden_done, g_ratio_done = m.count("g_rden_done", 2 * NC_), m.count("g_ratio_done", NU)
        block = ctx.enter_context(nc.Block())

        def job_done(b, job, ago=0):
            return pj_ready.at(b, where[job] + 1 - ago * NJ)

        def emptied(b, n):
            job, ago = jobs[(n - 2) % NJ], 0 if n >= 2 else 1
            if job in ropes:
                return raw_done.sem, raw_done.at(b, ropes.index(job) + 1 - ago * NR)
            return pj_dve.sem, pj_dve.at(b, by_dve.index(job) + 1 - ago * len(by_dve))

        def heads_free(b, n):
            p = n // (2 * QM)
            return job_done(b, ("o", (p - 1) % NPAIR * NC_ + NC_ - 1), 0 if p > 0 else 1)

        @block.sync
        def _(sp):
            ratio_in.open(sp)
            for s in w_in:
                s.open(sp)
            for s in (wv_in, g_f_in, g_stored):
                s.open(sp)
            for dst, src in ((cos_t, tables[0]), (sin_t, tables[1]), (mask_t, mask), (perm_t, perm)):
                sp.dma_start(dst[:, :], src).then_inc(small_in, 16)
            sp.dma_start(sink_t[:, :], sink.to_broadcast([P, NHEAD])).then_inc(small_in, 16)

            def load_weight(b, w):
                sp.wait_ge(w_hi_done.sem, w_hi_done.at(b, w - RAWS + 1))
                settle(sp, sp_passed)
                sp.wait_ge(w_lo_done.sem, w_lo_done.at(b, w - RAWS + 1))
                sp.dma_start(wraw[:, w % RAWS], weights[w].rearrange("p (c n) -> p c n", c=NC_)).then_inc(w_in[w % RAWS].sem, 16)

            def load_after(b, job):
                w = weighted.index(job) + SPLITS + RAWS
                if w < NW:
                    load_weight(b, w)

            def load_side(b, c):
                if c == 0:
                    sp.wait_ge(pj_ready.sem, job_done(b, ("v", NT - 1)))
                    settle(sp, sp_passed)
                sp.wait_ge(g_ek_done.sem, g_ek_done.at(b, c))
                settle(sp, sp_passed)
                sp.wait_ge(g_ekv_done.sem, g_ekv_done.at(b, 2 * c))
                settle(sp, sp_passed)
                sp.wait_ge(g_eukv_done.sem, g_eukv_done.at(b, c * LATER))
                settle(sp, sp_passed)
                sp.dma_start(g_f, sideT[bass.ds(b, 1), :, c, :].rearrange("o p t -> p (o t)")).then_inc(g_f_in.sem, 16)

            def store_ratios(b, c):
                sp.wait_ge(g_ratio_done.sem, g_ratio_done.at(b, (c + 1) * LATER))
                settle(sp, sp_passed)
                sp.dma_start(gates[1:NCOND, bass.ds(b, 1), :, c, :].rearrange("i o p t -> p (i o) t"), g_num).then_inc(g_stored.sem, 16)

            def load_ratio(b):
                sp.wait_ge(pt_ready.sem, pt_ready.at(b, -2 * NT))
                settle(sp, sp_passed)
                sp.dma_start(y, gates[0, bass.ds(b, 1)].rearrange("o p c t -> p (o c) t")).then_inc(ratio_in.sem, 16)

            def turn(b, last=False):
                for w in range(SPLITS + RAWS):
                    load_weight(b, w)
                    if w == RAWS - 1:
                        sp.wait_ge(g_stored.sem, g_stored.at(b, 0))
                        settle(sp, sp_passed)
                        sp.wait_ge(g_ek_done.sem, g_ek_done.at(b, 0))
                        settle(sp, sp_passed)
                        sp.wait_ge(g_ekv_done.sem, g_ekv_done.at(b, 0))
                        settle(sp, sp_passed)
                        sp.wait_ge(g_eukv_done.sem, g_eukv_done.at(b, 0))
                        settle(sp, sp_passed)
                        sp.dma_start(wv_sb[:, :, :], wv.rearrange("(c p) n -> p c n", p=P)).then_inc(wv_in.sem, 16)
                for job in ropes[:3]:
                    load_after(b, job)
                load_side(b, 0)
                for n in range(NHEAD):
                    c, step = divmod(n, SLOT)
                    if step == 1 and c > 0:
                        store_ratios(b, c - 1)
                    if step == 7 and c + 1 < NC_:
                        load_side(b, c + 1)
                    for job in side_jobs(n):
                        load_after(b, job)
                if not last:
                    load_ratio(b + 1)
                store_ratios(b, NC_ - 1)

            load_ratio(0)
            with sp.Fori(0, B - 1) as b:
                turn(b)
            turn(B - 1, last=True)
            sp.wait_ge(g_stored.sem, g_stored.at(B, 0))

        @block.gpsimd
        def _(pool):
            for s in (w_lo_done, rcos_done, rsum_done, normed, g_den_done, g_num_done, g_ratio_done):
                s.open(pool)
            pool.wait_ge(small_in, 16 * 5)

            def weight_lo(b, w):
                pool.wait_ge(w_hi_done.sem, w_hi_done.at(b, w + 1))
                pool.tensor_tensor(w_lo[:, w % SPLITS], wraw[:, w % RAWS], w_hi[:, w % SPLITS].bitcast(F32),
                                   ALU.subtract).then_inc(w_lo_done.sem, 1)

            def after_job(b, job):
                w = weighted.index(job) + SPLITS
                if w < NW:
                    weight_lo(b, w)

            def rope(b, job):
                r = ropes.index(job)
                pool.wait_ge(raw_done.sem, raw_done.at(b, r + 1))
                pool.wait_ge(rsum_done.sem, rsum_done.at(b, r))
                pool.tensor_tensor(rcos[:, :], raw[:, r % 2, :], cos_t[:, :], ALU.mult).then_inc(rcos_done.sem, 1)
                pool.wait_ge(rcos_done.sem, rcos_done.at(b, r + 1))
                pool.wait_ge(pj_dve.sem, pj_dve.at(b, by_dve.index((job[0] + "s", job[1])) + 1))
                pool.wait_ge(rope_lo.sem, rope_lo.at(b, before(r)))
                pool.tensor_tensor(rsum[:, :], rcos[:, :], rsin[:, :], ALU.add).then_inc(rsum_done.sem, 1)

            def query_low(b, job):
                r = ropes.index(job)
                slot = job[1] % 2
                pool.wait_ge(rope_hi.sem, rope_hi.at(b, before(r) + 1))
                pool.tensor_tensor(q_lo[:, slot, :], rsum[:, :], q_hi[:, slot, :].bitcast(F32), ALU.subtract).then_inc(rope_lo.sem, 1)

            def norm(b, n):
                pool.wait_ge(den_done.sem, den_done.at(b, 2 * n + 2))
                settle(pool, pool_passed)
                for q in range(NT):
                    pool.tensor_scalar(probs[:, n % RING, q, :], probs[:, n % RING, q, :], rinv[:, n % RING, q:q + 1], 1.0,
                                       ALU.mult, ALU.mult).then_inc(normed.sem, 1)

            def gate_sums(b, c, g):
                v = c * LATER + g
                pool.wait_ge(g_clipped.sem, g_clipped.at(b, v + 1))
                pool.wait_ge(g_scans.sem, g_scans.at(b, 4 * v + 4))
                pool.tensor_tensor(g_den[:, g, :], g_den[:, g, :], g_fwd[:, :], ALU.add).then_inc(g_den_done.sem, 1)
                pool.wait_ge(g_den_done.sem, g_den_done.at(b, 2 * v + 1))
                pool.wait_ge(g_eukv_done.sem, g_eukv_done.at(b, v + 1))
                pool.tensor_tensor(g_den[:, g, :], g_den[:, g, :], g_bwd_d[:, 1:T + 1], ALU.add).then_inc(g_den_done.sem, 1)
                pool.tensor_tensor(g_num[:, g, :], g_num[:, g, :], g_bwd_n[:, 1:T + 1], ALU.add).then_inc(g_num_done.sem, 1)
                pool.wait_ge(g_num_done.sem, g_num_done.at(b, 2 * v + 1))
                pool.tensor_tensor(g_num[:, g, :], g_num[:, g, :], g_eukv, ALU.add).then_inc(g_num_done.sem, 1)

            def gate_ratios(b, c):
                pool.wait_ge(g_rden_done.sem, g_rden_done.at(b, 2 * c + 2))
                pool.wait_ge(g_num_done.sem, g_num_done.at(b, 2 * (c + 1) * LATER))
                for g in range(LATER):
                    pool.tensor_tensor(g_num[:, g, :], g_num[:, g, :], g_den[:, g, :], ALU.mult).then_inc(g_ratio_done.sem, 1)

            pool.wait_ge(zeroed, 7)
            with pool.Fori(0, B) as b:
                for w in range(SPLITS):
                    weight_lo(b, w)
                for job in ropes[:3]:
                    after_job(b, job)
                    rope(b, job)
                    if job[0] == "q":
                        query_low(b, job)
                for n in range(AHEAD):
                    norm(b, n)
                for n in range(NHEAD):
                    for job in side_jobs(n):
                        after_job(b, job)
                        if job in ropes:
                            rope(b, job)
                        if job[0] == "q":
                            query_low(b, job)
                    c, step = divmod(n, SLOT)
                    if step in (3, 5, 7):
                        gate_sums(b, c, step // 2 - 1)
                    if n + AHEAD < NHEAD:
                        norm(b, n + AHEAD)
                    if step == 0 and c > 0:
                        gate_ratios(b, c - 1)
                for oc in range(NC_):
                    after_job(b, ("o", (NPAIR - 1) * NC_ + oc))
                gate_ratios(b, NC_ - 1)

        @block.tensor
        def _(pe):
            for s in (pj_ready, sc_ready, pt_ready, pv_done):
                s.open(pe)
            pe.wait_ge(small_in, 16 * 5)
            pe.wait_ge(zeroed, 7)

            def run(b, kind, i):
                n = where[kind, i]
                bank = pj[n % 2][:, :]
                pe.wait_ge(*emptied(b, n))
                if (kind, i) in weighted:
                    w = weighted.index((kind, i))
                    pe.wait_ge(w_lo_done.sem, w_lo_done.at(b, w + 1))
                    if kind == "o":
                        p = i // NC_
                        pe.wait_ge(head_lo.sem, head_lo.at(b, (p + 1) * 2 * QM))
                    a_hi, a_lo = (heads_hi, heads_lo) if kind == "o" else (y_hi, y_lo)
                    for c in range(NC_):
                        if kind != "o":
                            pe.wait_ge(y_lo_done.sem, y_lo_done.at(b, c + 1))
                        last = product(pe, bank, w_hi[:, w % SPLITS, c, :], w_lo[:, w % SPLITS, c, :], a_hi[:, c, :], a_lo[:, c, :],
                                       start=c == 0, stop=c == NC_ - 1)
                elif kind == "v":
                    pe.wait_ge(wv_in.sem, wv_in.at(b, 1))
                    for c in range(NC_):
                        last = pe.matmul(bank, y[:, c, i * P:(i + 1) * P], wv_sb[:, c, :], start=c == 0, stop=c == NC_ - 1)
                else:
                    r = ropes.index((kind[0], i))
                    pe.wait_ge(raw_done.sem, raw_done.at(b, r + 1))
                    last = pe.matmul(bank, perm_t[:, :], raw[:, r % 2, :], start=True, stop=True)
                last.then_inc(pj_ready.sem, 1)

            def scores(b, n, q):
                t, h = divmod(n, 2)
                p = t // QM
                s = n * NT + q
                if q == 0:
                    pe.wait_ge(rope_lo.sem, rope_lo.at(b, rounds[ropes.index(("q", t))]))
                    pe.wait_ge(rope_lo.sem, rope_lo.at(b, rounds[ropes.index(("k", p))]))
                pe.wait_ge(masked.sem, masked.at(b, max(s - 2, 0)))
                tokens = slice(q * P, (q + 1) * P)
                product(pe, sc[s % 3][:, :], q_hi[:, t % 2, tokens], q_lo[:, t % 2, tokens], kz_hi[:, p % 2, h, :], kz_lo[:, p % 2, h, :],
                        start=True, stop=True).then_inc(sc_ready.sem, 1)

            def turn(b, n, k):
                if k == 0:
                    pe.wait_ge(normed.sem, normed.at(b, (n + 1) * NT))
                pe.wait_ge(pt_lo.sem, pt_lo.at(b, n * NT + k - 1))
                for q in range(NT):
                    last = pe.transpose(pt[k % 2][:, q * P:(q + 1) * P], probs[:, n % RING, q, k * P:(k + 1) * P], ident[:, :])
                last.then_inc(pt_ready.sem, 1)

            def values(b, n, k):
                p = n // (2 * QM)
                if k == 0:
                    pe.wait_ge(head_lo.sem, head_lo.at(b, n))
                pe.wait_ge(pt_lo.sem, pt_lo.at(b, n * NT + k + 1))
                both = slice(p * P, (p + 1) * P)
                product(pe, po[:, :], v_hi[:, k, both], v_lo[:, k, both], pT_hi[:, k, :], pT_lo[:, k, :],
                        start=k == 0, stop=k == NT - 1).then_inc(pv_done.sem, 1)

            with pe.Fori(0, B) as b:
                for kind, i in jobs[:10]:
                    run(b, kind, i)
                for n in range(AHEAD):
                    for q in range(NT):
                        scores(b, n, q)
                pe.wait_ge(pj_dve.sem, pj_dve.at(b, by_dve.index(("v", NT - 1)) + 1))
                for n in range(NHEAD):
                    more = n + AHEAD < NHEAD
                    for k in range(NT):
                        if more:
                            scores(b, n + AHEAD, k)
                        turn(b, n, k)
                        if k == 1:
                            for kind, i in side_jobs(n):
                                run(b, kind, i)
                    for kind, i in side_jobs(n):
                        if kind != "o":
                            run(b, kind + "s", i)
                    for k in range(NT):
                        values(b, n, k)
                for oc in range(NC_):
                    run(b, "o", (NPAIR - 1) * NC_ + oc)

        @block.scalar
        def _(act):
            for s in (w_hi_done, tanh_done, y_hi_done, raw_done, v_hi_done, rope_hi, exp_done, sink_done, pt_hi, head_hi,
                      g_ek_done, g_euk_done, g_rden_done):
                s.open(act)
            act.wait_ge(small_in, 16 * 5)
            act.wait_ge(zeroed, 7)

            def weight_hi(b, w):
                act.wait_ge(w_in[w % RAWS].sem, w_in[w % RAWS].at(b, w // RAWS + 1))
                act.activation(w_hi[:, w % SPLITS], wraw[:, w % RAWS], ACT.Copy).then_inc(w_hi_done.sem, 1)

            def after_job(b, job):
                w = weighted.index(job) + SPLITS
                if w < NW:
                    act.wait_ge(pj_ready.sem, job_done(b, job))
                    weight_hi(b, w)

            def copy_raw(b, job):
                r = ropes.index(job)
                act.wait_ge(pj_ready.sem, job_done(b, job))
                act.wait_ge(rcos_done.sem, rcos_done.at(b, r - 1))
                kind, i = ropes[(r - 2) % NR]
                act.wait_ge(pj_ready.sem, job_done(b, (kind + "s", i), 0 if r >= 2 else 1))
                act.activation(raw[:, r % 2, :], pj[where[job] % 2][:, :], ACT.Copy).then_inc(raw_done.sem, 1)

            def copy_values(b, i):
                act.wait_ge(pj_ready.sem, job_done(b, ("v", i)))
                act.wait_ge(pv_done.sem, pv_done.at(b, 0))
                act.activation(v_hi[:, i, :], pj[where["v", i] % 2][:, :], ACT.Copy).then_inc(v_hi_done.sem, 1)

            def rope_high(b, job):
                kind, i = job
                act.wait_ge(rsum_done.sem, rsum_done.at(b, ropes.index(job) + 1))
                if kind == "q":
                    act.wait_ge(sc_ready.sem, sc_ready.at(b, (i - 1) * 2 * NT))
                    act.activation(q_hi[:, i % 2, :], rsum[:, :], ACT.Copy).then_inc(rope_hi.sem, 1)
                else:
                    act.wait_ge(sc_ready.sem, sc_ready.at(b, (i - 1) * QM * 2 * NT))
                    for h in range(2):
                        rows = slice(h * HD, (h + 1) * HD)
                        act.activation(kz_hi[rows, i % 2, h, :], rsum[rows, :], ACT.Copy).then_inc(rope_hi.sem, 1)

            def exps(b, n, q):
                s = n * NT + q
                act.wait_ge(masked.sem, masked.at(b, s + 1))
                act.activation(probs[:, n % RING, q, :], probs[:, n % RING, q, :], ACT.Exp, scale=-1.0,
                               bias=negmax[:, n % RING, q:q + 1], accum_out=rowsum[:, n % RING, q:q + 1]).then_inc(exp_done.sem, 1)

            def sinks(b, n):
                act.activation(sinkexp[:, n % RING, :], negmax[:, n % RING, :], ACT.Exp, bias=sink_t[:, n:n + 1]).then_inc(sink_done.sem, 1)

            def turned_high(b, n, k):
                act.wait_ge(pt_ready.sem, pt_ready.at(b, n * NT + k + 1))
                act.wait_ge(pv_done.sem, pv_done.at(b, (n - 1) * NT + k + 1))
                act.activation(pT_hi[:, k, :], pt[k % 2][:, :], ACT.Copy).then_inc(pt_hi.sem, 1)

            def head_high(b, n):
                t, h = divmod(n, 2)
                rows = slice(h * HD, (h + 1) * HD)
                act.wait_ge(pv_done.sem, pv_done.at(b, (n + 1) * NT))
                if t % QM == 0:
                    act.wait_ge(pj_ready.sem, heads_free(b, n))
                act.activation(heads_hi[rows, t % QM, :], po[rows, :], ACT.Copy).then_inc(head_hi.sem, 1)

            def gate_ek(b, c):
                act.wait_ge(g_f_in.sem, g_f_in.at(b, c + 1))
                act.wait_ge(g_scans.sem, g_scans.at(b, 4 * c * LATER))
                act.activation(g_ek[:, :], g_f, ACT.Exp).then_inc(g_ek_done.sem, 1)

            def gate_euk(b, c, g):
                act.wait_ge(g_ratio_done.sem, g_ratio_done.at(b, c * LATER))
                u = (1 + g) * NC_ + c
                act.activation(g_den[:, g, :], g_f, ACT.Exp, bias=ucol[:, u:u + 1]).then_inc(g_euk_done.sem, 1)

            def gate_ln(b, c):
                act.wait_ge(g_max_done.sem, g_max_done.at(b, (c + 1) * LATER))
                act.activation(g_den, g_den, ACT.Ln).then_inc(g_rden_done.sem, 1)

            def gate_reciprocal(b, c):
                act.wait_ge(g_rden_done.sem, g_rden_done.at(b, 2 * c + 1))
                settle(act, act_passed)
                act.activation(g_den, g_den, ACT.Exp, scale=-1.0, bias=lngain[:, bass.ds(b, 1)]).then_inc(g_rden_done.sem, 1)

            with act.Fori(0, B) as b:
                act.wait_ge(pt_ready.sem, pt_ready.at(b, -NT))
                settle(act, act_passed)
                act.activation(probs[:, 0], xT[:, :, bass.ds(b * T, T)], ACT.Tanh, scale=0.5).then_inc(tanh_done.sem, 1)
                act.wait_ge(pj_ready.sem, job_done(b, weighted[NW - SPLITS], 1))
                weight_hi(b, 0)
                for c in range(NC_):
                    act.wait_ge(y_done.sem, y_done.at(b, c + 1))
                    act.activation(y_hi[:, c, :], y[:, c, :], ACT.Copy).then_inc(y_hi_done.sem, 1)
                act.wait_ge(pj_ready.sem, job_done(b, weighted[NW - 1], 1))
                weight_hi(b, 1)
                copy_raw(b, ("k", 0))
                after_job(b, ("k", 0))
                copy_raw(b, ("q", 0))
                after_job(b, ("q", 0))
                rope_high(b, ("k", 0))
                copy_raw(b, ("q", 1))
                after_job(b, ("q", 1))
                rope_high(b, ("q", 0))
                copy_values(b, 0)
                rope_high(b, ("q", 1))
                for i in range(1, NT):
                    copy_values(b, i)
                for n in range(AHEAD):
                    for q in range(NT):
                        exps(b, n, q)
                    sinks(b, n)
                for n in range(NHEAD):
                    more = n + AHEAD < NHEAD
                    slot, step = divmod(n, SLOT)
                    for k in range(NT):
                        turned_high(b, n, k)
                        if more:
                            exps(b, n + AHEAD, k)
                        if k == 1:
                            for job in side_jobs(n):
                                if job in ropes:
                                    copy_raw(b, job)
                                after_job(b, job)
                                if step == 0 and job == ("o", (slot - 1) * NC_):
                                    gate_ln(b, slot - 1)
                                if step == 0 and job == ("o", (slot - 1) * NC_ + 2):
                                    gate_reciprocal(b, slot - 1)
                    if more:
                        sinks(b, n + AHEAD)
                    for job in side_jobs(n):
                        if job in ropes:
                            rope_high(b, job)
                    if step == 0:
                        gate_ek(b, slot)
                    if step in (1, 3, 5):
                        gate_euk(b, slot, step // 2)
                    head_high(b, n)
                gate_ln(b, NC_ - 1)
                after_job(b, ("o", (NPAIR - 1) * NC_))
                gate_reciprocal(b, NC_ - 1)
                for oc in range(1, NC_):
                    after_job(b, ("o", (NPAIR - 1) * NC_ + oc))

        @block.vector
        def _(dve):
            for s in (y_done, y_lo_done, pj_dve, rope_lo, masked, den_done, pt_lo, head_lo,
                      g_ekv_done, g_clipped, g_eukv_done, g_scans, g_max_done):
                s.open(dve)
            dve.memset(rsin[:, :], 0.0).then_inc(zeroed, 1)
            dve.wait_ge(zeroed, 1)
            for kz in (kz_hi, kz_lo):
                for h in range(2):
                    rows = slice((1 - h) * HD, (2 - h) * HD)
                    zeros = rsin[rows, :].rearrange("p (o t) -> p o t", o=1).to_broadcast([HD, 2, T])
                    dve.tensor_copy(kz[rows, :, h, :], zeros).then_inc(zeroed, 1)
            dve.memset(g_bwd_n[:, T:T + 1], 0.0).then_inc(zeroed, 1)
            dve.memset(g_bwd_d[:, T:T + 1], 0.0).then_inc(zeroed, 1)
            dve.wait_ge(small_in, 16 * 5)
            dve.tensor_scalar(nsink_t[:, :], sink_t[:, :], -1.0, None, ALU.mult).then_inc(setup, 1)
            dve.wait_ge(setup, 1)
            dve.wait_ge(zeroed, 7)

            def gate_y(b, c):
                dve.scalar_tensor_tensor(y[:, c, :], probs[:, 0, c, :], 1.0, y[:, c, :], ALU.add, ALU.mult).then_inc(y_done.sem, 1)

            def gate_low(b, c):
                dve.wait_ge(y_hi_done.sem, y_hi_done.at(b, c + 1))
                dve.tensor_tensor(y_lo[:, c, :], y[:, c, :], y_hi[:, c, :].bitcast(F32), ALU.subtract).then_inc(y_lo_done.sem, 1)

            def rot_sin(b, job):
                r = ropes.index(job)
                swap = (job[0] + "s", job[1])
                dve.wait_ge(pj_ready.sem, job_done(b, swap))
                dve.wait_ge(rsum_done.sem, rsum_done.at(b, r))
                dve.tensor_tensor(rsin[:, :], pj[where[swap] % 2][:, :], sin_t[:, :], ALU.mult).then_inc(pj_dve.sem, 1)

            def keys_low(b, job):
                r, slot = ropes.index(job), job[1] % 2
                for h in range(2):
                    rows = slice(h * HD, (h + 1) * HD)
                    dve.wait_ge(rope_hi.sem, rope_hi.at(b, before(r) + h + 1))
                    dve.tensor_tensor(kz_lo[rows, slot, h, :], rsum[rows, :], kz_hi[rows, slot, h, :].bitcast(F32),
                                      ALU.subtract).then_inc(rope_lo.sem, 1)

            def values_low(b, i):
                dve.wait_ge(v_hi_done.sem, v_hi_done.at(b, i + 1))
                dve.tensor_tensor(v_lo[:, i, :], pj[where["v", i] % 2][:, :], v_hi[:, i, :].bitcast(F32), ALU.subtract).then_inc(pj_dve.sem, 1)

            def add_out(b, i):
                oc = i % NC_
                dve.wait_ge(pj_ready.sem, job_done(b, ("o", i)))
                if i >= NC_:
                    dve.wait_ge(pj_dve.sem, pj_dve.at(b, by_dve.index(("o", i - NC_)) + 1))
                x_oc = xT[:, oc, bass.ds(b * T, T)]
                dve.tensor_tensor(x_oc, x_oc, pj[where["o", i] % 2][:, :], ALU.add).then_inc(pj_dve.sem, 1)

            def masking(b, n, q):
                s = n * NT + q
                dve.wait_ge(sc_ready.sem, sc_ready.at(b, s + 1))
                if q == 0:
                    dve.wait_ge(pt_ready.sem, pt_ready.at(b, max(n - RING + 1, 0) * NT if n > 0 else -NT))
                    dve.wait_ge(sink_done.sem, sink_done.at(b, max(n - RING + 1, 0)))
                settle(dve, dve_passed)
                dve.tensor_tensor_reduce(out=probs[:, n % RING, q, :], in0=sc[s % 3][:, :],
                                         in1=mask_t[:, (NT - 1 - q) * P:(NT - 1 - q) * P + T],
                                         scale=-HD ** -0.5, scalar=nsink_t[:, n:n + 1], op0=ALU.add, op1=ALU.min,
                                         accum_out=negmax[:, n % RING, q:q + 1]).then_inc(masked.sem, 1)

            def denominators(b, n):
                dve.wait_ge(exp_done.sem, exp_done.at(b, (n + 1) * NT))
                dve.wait_ge(sink_done.sem, sink_done.at(b, n + 1))
                dve.wait_ge(normed.sem, normed.at(b, max(n - RING + 1, 0) * NT))
                dve.tensor_tensor(sinkexp[:, n % RING, :], sinkexp[:, n % RING, :], rowsum[:, n % RING, :], ALU.add).then_inc(den_done.sem, 1)
                dve.wait_ge(den_done.sem, den_done.at(b, 2 * n + 1))
                dve.reciprocal(rinv[:, n % RING, :], sinkexp[:, n % RING, :]).then_inc(den_done.sem, 1)

            def turned_low(b, n, k):
                dve.wait_ge(pt_hi.sem, pt_hi.at(b, n * NT + k + 1))
                dve.wait_ge(pv_done.sem, pv_done.at(b, (n - 1) * NT + k + 1))
                dve.tensor_tensor(pT_lo[:, k, :], pt[k % 2][:, :], pT_hi[:, k, :].bitcast(F32), ALU.subtract).then_inc(pt_lo.sem, 1)

            def head_low(b, n):
                t, h = divmod(n, 2)
                rows = slice(h * HD, (h + 1) * HD)
                dve.wait_ge(head_hi.sem, head_hi.at(b, n + 1))
                if t % QM == 0:
                    dve.wait_ge(pj_ready.sem, heads_free(b, n))
                dve.tensor_tensor(heads_lo[rows, t % QM, :], po[rows, :], heads_hi[rows, t % QM, :].bitcast(F32),
                                  ALU.subtract).then_inc(head_lo.sem, 1)

            def gate_ekv(b, c):
                dve.wait_ge(g_ek_done.sem, g_ek_done.at(b, c + 1))
                dve.tensor_scalar(g_ek[:, :], g_ek[:, :], E30, None, ALU.min).then_inc(g_ekv_done.sem, 1)
                dve.wait_ge(g_ekv_done.sem, g_ekv_done.at(b, 2 * c + 1))
                dve.tensor_tensor(g_ekv[:, :], g_ek[:, :], g_f, ALU.mult).then_inc(g_ekv_done.sem, 1)

            def gate_own(b, c, g):
                v = c * LATER + g
                dve.wait_ge(g_euk_done.sem, g_euk_done.at(b, v + 1))
                dve.tensor_scalar(g_den[:, g, :], g_den[:, g, :], E30, None, ALU.min).then_inc(g_clipped.sem, 1)
                dve.wait_ge(g_clipped.sem, g_clipped.at(b, v + 1))
                dve.wait_ge(g_num_done.sem, g_num_done.at(b, 2 * v))
                dve.tensor_tensor(g_eukv, g_den[:, g, :], g_f, ALU.mult).then_inc(g_eukv_done.sem, 1)

            def gate_scans(b, c, g, fwd, bwd, val):
                u = (1 + g) * NC_ + c
                d = decay[:, bass.ds(b, 1), u:u + 1].rearrange("p o k -> p (o k)").to_broadcast([P, T])
                dve.tensor_tensor_scan(fwd, d, val[:, :], 0.0, ALU.mult, ALU.add).then_inc(g_scans.sem, 1)
                dve.tensor_tensor_scan(bwd[:, 0:T][:, ::-1], val[:, ::-1], d, 0.0, ALU.add, ALU.mult).then_inc(g_scans.sem, 1)

            def gate_floor(b, c, g):
                v = c * LATER + g
                dve.wait_ge(g_den_done.sem, g_den_done.at(b, 2 * v + 2))
                dve.tensor_scalar(g_den[:, g, :], g_den[:, g, :], 1e-8, None, ALU.max).then_inc(g_max_done.sem, 1)

            def gate_beside_jobs(b, n):
                c, step = divmod(n, SLOT)
                if step == 1:
                    gate_ekv(b, c)
                if step in (2, 4, 6):
                    g = step // 2 - 1
                    gate_own(b, c, g)
                    dve.wait_ge(g_ekv_done.sem, g_ekv_done.at(b, 2 * c + 2))
                    dve.wait_ge(g_num_done.sem, g_num_done.at(b, 2 * (c * LATER + g)))
                    dve.wait_ge(g_stored.sem, g_stored.at(b, c))
                    gate_scans(b, c, g, g_num[:, g, :], g_bwd_n, g_ekv)

            def gate_beside_values(b, n):
                c, step = divmod(n, SLOT)
                if step in (2, 4, 6):
                    g = step // 2 - 1
                    dve.wait_ge(g_den_done.sem, g_den_done.at(b, 2 * (c * LATER + g)))
                    gate_scans(b, c, g, g_fwd[:, :], g_bwd_d, g_ek)
                    if g > 0:
                        gate_floor(b, c, g - 1)

            with dve.Fori(0, B) as b:
                dve.wait_ge(tanh_done.sem, tanh_done.at(b, 1))
                dve.wait_ge(ratio_in.sem, ratio_in.at(b, 1))
                gate_y(b, 0)
                for c in range(1, NC_):
                    gate_y(b, c)
                    gate_low(b, c - 1)
                gate_low(b, NC_ - 1)
                rot_sin(b, ("k", 0))
                rot_sin(b, ("q", 0))
                keys_low(b, ("k", 0))
                values_low(b, 0)
                rot_sin(b, ("q", 1))
                for i in range(1, NT):
                    values_low(b, i)
                for n in range(AHEAD):
                    for q in range(NT):
                        masking(b, n, q)
                    denominators(b, n)
                for n in range(NHEAD):
                    more = n + AHEAD < NHEAD
                    for k in range(NT):
                        if more:
                            masking(b, n + AHEAD, k)
                        turned_low(b, n, k)
                        if k == 1:
                            if n % SLOT == 0 and n > 0:
                                gate_floor(b, n // SLOT - 1, LATER - 1)
                            for kind, i in side_jobs(n):
                                if kind == "o":
                                    add_out(b, i)
                            gate_beside_jobs(b, n)
                    for job in side_jobs(n):
                        if job in ropes:
                            rot_sin(b, job)
                    if more:
                        denominators(b, n + AHEAD)
                    gate_beside_values(b, n)
                    for job in side_jobs(n):
                        if job[0] == "k":
                            keys_low(b, job)
                    head_low(b, n)
                gate_floor(b, NC_ - 1, LATER - 1)
                for oc in range(NC_):
                    add_out(b, (NPAIR - 1) * NC_ + oc)


def gate_all(xT, tanh_buf, y, tanh_done, y_done, ratio_in):

    def load(sp, gate):
        for b in range(B):
            sp.dma_start(y[:, :, b * T:(b + 1) * T], gate[b]).then_inc(ratio_in[b], 16)

    def scalar(act):
        for b in range(B):
            if b >= 2:
                act.wait_ge(y_done, b - 1)
            act.activation(tanh_buf[:, b % 2], xT[:, :, b * T:(b + 1) * T], ACT.Tanh, scale=0.5).then_inc(tanh_done, 1)

    def vector(dve):
        for b in range(B):
            dve.wait_ge(tanh_done, b + 1)
            dve.wait_ge(ratio_in[b], 16)
            y_b = y[:, :, b * T:(b + 1) * T]
            dve.scalar_tensor_tensor(y_b, tanh_buf[:, b % 2], 1.0, y_b, ALU.add, ALU.mult).then_inc(y_done, 1)

    return load, scalar, vector


def split_y(m, xT, y_hi, y_lo, stage, tanh_buf, pair=2):
    ratio_in = m.count("ratio_in", pair, by=16)
    tanh_done, y_done = m.count("tanh_done", pair), m.count("y_done", pair)
    hi_done, lo_done = m.count("y_hi_done", pair), m.count("y_lo_done", pair)
    passed = m.passed("act")

    def x_of(turn, bi):
        return xT[:, :, bass.ds(turn * (pair * T) + bi * T, T)]

    def load(sp, turn, bi, gate):
        sp.wait_ge(lo_done.sem, lo_done.at(turn, bi))
        sp.wait_ge(hi_done.sem, hi_done.at(turn, bi))
        sp.dma_start(stage[:, :, :], gate[bass.ds(turn * pair + bi, 1)].rearrange("o p c t -> p (o c) t")).then_inc(ratio_in.sem, 16)

    def scalar_tanh(act, turn, bi):
        act.wait_ge(y_done.sem, y_done.at(turn, bi))
        settle(act, passed)
        act.activation(tanh_buf[:, :, :], x_of(turn, bi), ACT.Tanh, scale=0.5).then_inc(tanh_done.sem, 1)

    def scalar_hi(act, turn, bi):
        act.wait_ge(y_done.sem, y_done.at(turn, bi + 1))
        act.activation(y_hi[:, :, bi * T:(bi + 1) * T], stage[:, :, :], ACT.Copy).then_inc(hi_done.sem, 1)

    def vector_y(dve, turn, bi):
        dve.wait_ge(tanh_done.sem, tanh_done.at(turn, bi + 1))
        dve.wait_ge(ratio_in.sem, ratio_in.at(turn, bi + 1))
        dve.scalar_tensor_tensor(stage[:, :, :], tanh_buf[:, :, :], 1.0, stage[:, :, :], ALU.add, ALU.mult).then_inc(y_done.sem, 1)

    def vector_lo(dve, turn, bi):
        dve.wait_ge(hi_done.sem, hi_done.at(turn, bi + 1))
        dve.tensor_tensor(y_lo[:, :, bi * T:(bi + 1) * T], stage[:, :, :], y_hi[:, :, bi * T:(bi + 1) * T].bitcast(F32),
                          ALU.subtract).then_inc(lo_done.sem, 1)

    class Parts:
        pass

    parts = Parts()
    parts.ratio_in, parts.tanh_done, parts.y_done, parts.hi_done, parts.lo_done = ratio_in, tanh_done, y_done, hi_done, lo_done
    parts.load, parts.scalar_tanh, parts.scalar_hi, parts.vector_y, parts.vector_lo = load, scalar_tanh, scalar_hi, vector_y, vector_lo
    return parts


NG = 4
NHID = 4 * NG
PAIR = 2
UNITS = NG * PAIR


def sparse_ffn(nc, xT, gate, weights):
    with ExitStack() as ctx:
        m = Space(nc, ctx, "ffn")
        raw = m.sb("raw", [P, 2, 3, C])
        gu_hi, gu_lo = m.sb("gu_hi", [P, 4, 2, NC_, P], F32R), m.sb("gu_lo", [P, 4, 2, NC_, P], F32R)
        wd_hi, wd_lo = m.sb("wd_hi", [P, 2, 4, C], F32R), m.sb("wd_lo", [P, 2, 4, C], F32R)
        y_hi, y_lo = m.sb("y_hi", [P, NC_, PAIR * T], F32R), m.sb("y_lo", [P, NC_, PAIR * T], F32R)
        stage = m.sb("stage", [P, NC_, T])
        tanh_g, hid, size = m.sb("tanh_g", [P, 2, T]), m.sb("hid", [P, 4, T]), m.sb("size", [P, 4, T])
        beats, votes = m.sb("beats", [P, 6, T], BF16), m.sb("votes", [P, 4, T], BF16)
        hs_hi, hs_lo = m.sb("hs_hi", [P, 4, T], F32R), m.sb("hs_lo", [P, 4, T], F32R)
        pg = [m.ps(f"pg{i}", [P, T]) for i in range(2)]
        pu = [m.ps(f"pu{i}", [P, T]) for i in range(2)]
        pd = [m.ps(f"pd{i}", [P, T]) for i in range(NC_)]

        NTL = 4 * UNITS
        raw_in = [m.count(f"raw_in{s}", NHID // 2, by=16) for s in range(2)]
        w_hi_done, w_lo_done = m.count("w_hi_done", 2 * NHID, 4), m.count("w_lo_done", 2 * NHID, 4)
        g_ready, u_ready = m.count("g_ready", NTL, 9), m.count("u_ready", NTL, 9)
        tanh_g_done = m.count("tanh_g_done", NTL)
        silu_done, hid_done = m.count("silu_done", NTL, 3), m.count("hid_done", NTL, 3)
        size_done = m.count("size_done", NTL, 5)
        beats_done, votes_done = m.count("beats_done", 3 * UNITS, 4), m.count("votes_done", 4 * UNITS, 5)
        sparse_done = m.count("sparse_done", NTL, 5)
        hs_hi_done, hs_lo_done = m.count("hs_hi_done", NTL, 5), m.count("hs_lo_done", NTL, 5)
        down_done, added = m.count("down_done", NTL, 14), m.count("added", NC_ * UNITS, 9)
        yp = split_y(m, xT, y_hi, y_lo, stage, size, PAIR)
        block = ctx.enter_context(nc.Block())

        def gu_free(bp, t):
            g, j = divmod(t, 4)
            return u_ready.at(bp, 8 * (g - 1) + 4 + j + 1)

        def wd_free(bp, t):
            g, j = divmod(t, 4)
            return down_done.at(bp, 8 * (g - 2) + 4 + j + 1)

        def load_raw(sp, bp, t):
            sp.wait_ge(w_lo_done.sem, w_lo_done.at(bp, 2 * (t - 1)))
            sp.wait_ge(w_hi_done.sem, w_hi_done.at(bp, 2 * (t - 1)))
            sp.dma_start(raw[:, t % 2], weights[t]).then_inc(raw_in[t % 2].sem, 16)

        @block.sync
        def _(sp):
            for s in (yp.ratio_in, *raw_in):
                s.open(sp)
            with sp.Fori(0, B // PAIR) as bp:
                for bi in range(PAIR):
                    if bi == 1:
                        load_raw(sp, bp, 0)
                        load_raw(sp, bp, 1)
                    yp.load(sp, bp, bi, gate)
                for t in range(2, NHID):
                    load_raw(sp, bp, t)

        @block.tensor
        def _(pe):
            for s in (g_ready, u_ready, down_done):
                s.open(pe)

            def up(bp, v, j):
                g, bi = divmod(v, PAIR)
                i = 4 * v + j
                if bi == 0:
                    pe.wait_ge(w_lo_done.sem, w_lo_done.at(bp, 2 * (4 * g + j) + 1))
                if v < PAIR and j == 0:
                    pe.wait_ge(yp.lo_done.sem, yp.lo_done.at(bp, bi + 1))
                for w, (bank, ready, free) in enumerate(((pg, g_ready, silu_done), (pu, u_ready, hid_done))):
                    pe.wait_ge(free.sem, free.at(bp, i - 1))
                    cols = slice(bi * T, (bi + 1) * T)
                    for c in range(NC_):
                        last = product(pe, bank[i % 2][:, :], gu_hi[:, j, w, c, :], gu_lo[:, j, w, c, :],
                                       y_hi[:, c, cols], y_lo[:, c, cols], c == 0, c == NC_ - 1)
                    last.then_inc(ready.sem, 1)

            def down(bp, v, j):
                g, bi = divmod(v, PAIR)
                pe.wait_ge(hs_lo_done.sem, hs_lo_done.at(bp, 4 * v + j + 1))
                if bi == 0:
                    pe.wait_ge(w_lo_done.sem, w_lo_done.at(bp, 2 * (4 * g + j) + 2))
                for oc in range(NC_):
                    if j == 0:
                        pe.wait_ge(added.sem, added.at(bp, NC_ * (v - 1) + oc + 1))
                    cols = slice(oc * P, (oc + 1) * P)
                    last = product(pe, pd[oc][:, :], wd_hi[:, g % 2, j, cols], wd_lo[:, g % 2, j, cols],
                                   hs_hi[:, j, :], hs_lo[:, j, :], j == 0, j == 3)
                last.then_inc(down_done.sem, 1)

            with pe.Fori(0, B // PAIR) as bp:
                for v in range(UNITS):
                    up(bp, v, 0)
                    up(bp, v, 1)
                    for j in range(2):
                        if v > 0:
                            down(bp, v - 1, j)
                        up(bp, v, j + 2)
                    if v > 0:
                        down(bp, v - 1, 2)
                        down(bp, v - 1, 3)
                for j in range(4):
                    down(bp, UNITS - 1, j)

        @block.scalar
        def _(act):
            for s in (yp.tanh_done, yp.hi_done, w_hi_done, tanh_g_done, size_done, hs_hi_done):
                s.open(act)

            def weight_hi(bp, t):
                g, j = divmod(t, 4)
                act.wait_ge(raw_in[t % 2].sem, raw_in[t % 2].at(bp, t // 2 + 1))
                act.wait_ge(u_ready.sem, gu_free(bp, t))
                act.activation(gu_hi[:, j].rearrange("p w c n -> p (w c n)"), raw[:, t % 2, 0:2, :].rearrange("p w n -> p (w n)"),
                               ACT.Copy).then_inc(w_hi_done.sem, 1)
                act.wait_ge(down_done.sem, wd_free(bp, t))
                act.activation(wd_hi[:, g % 2, j, :], raw[:, t % 2, 2, :], ACT.Copy).then_inc(w_hi_done.sem, 1)

            def tanh_of(bp, i):
                act.wait_ge(g_ready.sem, g_ready.at(bp, i + 1))
                act.wait_ge(hid_done.sem, hid_done.at(bp, i - 1))
                act.activation(tanh_g[:, i % 2, :], pg[i % 2][:, :], ACT.Tanh, scale=0.5).then_inc(tanh_g_done.sem, 1)

            def sizes(bp, i):
                act.wait_ge(hid_done.sem, hid_done.at(bp, i + 1))
                act.wait_ge(beats_done.sem, beats_done.at(bp, 3 * (i // 4)))
                act.activation(size[:, i % 4, :], hid[:, i % 4, :], ACT.Abs).then_inc(size_done.sem, 1)

            def sparse_hi(bp, v):
                for j in range(4):
                    i = 4 * v + j
                    act.wait_ge(sparse_done.sem, sparse_done.at(bp, i + 1))
                    act.wait_ge(down_done.sem, down_done.at(bp, i - 3))
                    act.wait_ge(hs_lo_done.sem, hs_lo_done.at(bp, i - 3))
                    act.activation(hs_hi[:, j, :], hid[:, j, :], ACT.Copy).then_inc(hs_hi_done.sem, 1)

            with act.Fori(0, B // PAIR) as bp:
                act.wait_ge(beats_done.sem, beats_done.at(bp, 0))
                yp.scalar_tanh(act, bp, 0)
                weight_hi(bp, 0)
                yp.scalar_hi(act, bp, 0)
                yp.scalar_tanh(act, bp, 1)
                weight_hi(bp, 1)
                yp.scalar_hi(act, bp, 1)
                weight_hi(bp, 2)
                weight_hi(bp, 3)
                for v in range(UNITS):
                    for j in range(4):
                        tanh_of(bp, 4 * v + j)
                        if v == 0 and j == 0:
                            act.wait_ge(yp.y_done.sem, yp.y_done.at(bp, 2))
                        sizes(bp, 4 * v + j)
                        if v % PAIR == 1 and v < UNITS - 1 and j >= 1:
                            weight_hi(bp, 4 * (v // PAIR + 1) + j - 1)
                    sparse_hi(bp, v)
                    if v % PAIR == 1 and v < UNITS - 1:
                        weight_hi(bp, 4 * (v // PAIR + 1) + 3)

        @block.gpsimd
        def _(pool):
            w_lo_done.open(pool)
            with pool.Fori(0, B // PAIR) as bp:
                for t in range(NHID):
                    g, j = divmod(t, 4)
                    pool.wait_ge(w_hi_done.sem, w_hi_done.at(bp, 2 * t + 1))
                    pool.wait_ge(u_ready.sem, gu_free(bp, t))
                    pool.tensor_tensor(gu_lo[:, j].rearrange("p w c n -> p (w c n)"), raw[:, t % 2, 0:2, :].rearrange("p w n -> p (w n)"),
                                       gu_hi[:, j].rearrange("p w c n -> p (w c n)").bitcast(F32), ALU.subtract).then_inc(w_lo_done.sem, 1)
                    pool.wait_ge(w_hi_done.sem, w_hi_done.at(bp, 2 * t + 2))
                    pool.wait_ge(down_done.sem, wd_free(bp, t))
                    pool.tensor_tensor(wd_lo[:, g % 2, j, :], raw[:, t % 2, 2, :], wd_hi[:, g % 2, j, :].bitcast(F32),
                                       ALU.subtract).then_inc(w_lo_done.sem, 1)

        @block.vector
        def _(dve):
            for s in (yp.y_done, yp.lo_done, silu_done, hid_done, beats_done, votes_done, sparse_done, hs_lo_done, added):
                s.open(dve)

            def hidden(bp, i):
                dve.wait_ge(tanh_g_done.sem, tanh_g_done.at(bp, i + 1))
                dve.scalar_tensor_tensor(tanh_g[:, i % 2, :], tanh_g[:, i % 2, :], 1.0, pg[i % 2][:, :],
                                         ALU.add, ALU.mult).then_inc(silu_done.sem, 1)
                dve.wait_ge(u_ready.sem, u_ready.at(bp, i + 1))
                dve.wait_ge(silu_done.sem, silu_done.at(bp, i + 1))
                dve.wait_ge(hs_lo_done.sem, hs_lo_done.at(bp, i - 3))
                dve.tensor_tensor(hid[:, i % 4, :], tanh_g[:, i % 2, :], pu[i % 2][:, :], ALU.mult).then_inc(hid_done.sem, 1)

            def sparsify(bp, v):
                dve.wait_ge(size_done.sem, size_done.at(bp, 4 * (v + 1)))
                dve.wait_ge(sparse_done.sem, sparse_done.at(bp, 4 * v))
                for i, (lo, n) in enumerate(((0, 3), (3, 2), (5, 1))):
                    dve.tensor_tensor(beats[:, lo:lo + n, :], size[:, i:i + 1, :].to_broadcast([P, n, T]), size[:, i + 1:4, :],
                                      ALU.is_ge).then_inc(beats_done.sem, 1)
                dve.wait_ge(beats_done.sem, beats_done.at(bp, 3 * (v + 1)))
                dve.tensor_tensor(votes[:, 0:2, :], beats[:, 0:6:3, :], beats[:, 1:6:3, :], ALU.add).then_inc(votes_done.sem, 1)
                dve.tensor_tensor(votes[:, 2:4, :], beats[:, 1:3, :], beats[:, 3:5, :], ALU.add).then_inc(votes_done.sem, 1)
                dve.wait_ge(votes_done.sem, votes_done.at(bp, 4 * v + 2))
                dve.tensor_tensor(votes[:, 0:4:3, :], votes[:, 0:4:3, :], beats[:, 2:6:3, :], ALU.add).then_inc(votes_done.sem, 1)
                dve.tensor_tensor(votes[:, 1:3, :], votes[:, 1:3, :], beats[:, 0:6:5, :], ALU.subtract).then_inc(votes_done.sem, 1)
                dve.wait_ge(votes_done.sem, votes_done.at(bp, 4 * v + 4))
                for j, (op, limit) in enumerate(((ALU.is_ge, 2.0), (ALU.is_ge, 1.0), (ALU.is_le, 0.0), (ALU.is_le, 1.0))):
                    dve.scalar_tensor_tensor(hid[:, j, :], votes[:, j, :], limit, hid[:, j, :], op, ALU.mult).then_inc(sparse_done.sem, 1)
                for j in range(4):
                    dve.wait_ge(hs_hi_done.sem, hs_hi_done.at(bp, 4 * v + j + 1))
                    dve.tensor_tensor(hs_lo[:, j, :], hid[:, j, :], hs_hi[:, j, :].bitcast(F32), ALU.subtract).then_inc(hs_lo_done.sem, 1)

            def add_out(bp, v):
                bi = v % PAIR
                dve.wait_ge(down_done.sem, down_done.at(bp, 4 * (v + 1)))
                for oc in range(NC_):
                    x_oc = xT[:, oc, bass.ds(bp * (PAIR * T) + bi * T, T)]
                    dve.scalar_tensor_tensor(x_oc, pd[oc][:, :], 0.5, x_oc, ALU.mult, ALU.add).then_inc(added.sem, 1)

            with dve.Fori(0, B // PAIR) as bp:
                for bi in range(PAIR):
                    yp.vector_y(dve, bp, bi)
                    yp.vector_lo(dve, bp, bi)
                for v in range(UNITS):
                    for j in range(4):
                        hidden(bp, 4 * v + j)
                    sparsify(bp, v)
                    if v > 0:
                        add_out(bp, v - 1)
                add_out(bp, UNITS - 1)


NCH = 16
BINS = 16


def fourier_attention(nc, xT, gate, wq, wkv, woT, dft, idftT, norm_mat, dc_cols):
    with ExitStack() as ctx:
        m = Space(nc, ctx, "fft")
        raw_w = [m.sb(f"raw_{n}", [P, NC_, C]) for n in ("q", "kv", "o")]
        f_sb, fi_sb = m.sb("dft", [P, NC_, C]), m.sb("idft", [P, NC_, C])
        fold = [m.sb(f"fold_{n}", [P, NC_, C]) for n in ("kv", "q", "o")]
        norm_t, dc_t = m.sb("norm", [P, P]), m.sb("dc", [P, 3])
        y, tanh_buf = m.sb("y", [P, NC_, B * T]), m.sb("tanh_buf", [P, 2, NC_, T])
        square, rnorm = m.sb("square", [P, 2, 2, T]), m.sb("rnorm", [P, 2, T])
        hat_k, hat_q = m.sb("hat_k", [P, 2, T]), m.sb("hat_q", [P, 2, T])
        total = m.sb("total", [P, 2, T])
        other = m.sb("other", [P, 3, T])
        parts = m.sb("parts", [P, 4, T])
        prod = m.sb("prod", [P, 1, 4, T])
        pl = [m.ps(f"pl{i}", [P, T]) for i in range(4)]
        pn = [m.ps(f"pn{i}", [P, T]) for i in range(2)]
        pd = [m.ps(f"pd{i}", [P, T]) for i in range(2)]

        ratio_in = [m.sem(f"ratio_in{b}") for b in range(B)]
        tanh_done, y_done, w_in = m.sem("tanh_done"), m.sem("y_done"), m.sem("w_in")
        folded, fold_copied = m.sem("folded"), m.sem("fold_copied")
        dve_passed = m.passed("dve")
        planes = m.count("planes", 8, 5)
        squared, norm_ready = m.count("squared", 8, 5), m.count("norm_ready", 4, 3)
        rnormed, hatted = m.count("rnormed", 8, 5), m.count("hatted", 8, 5)
        summed, others = m.count("summed", 4, 3), m.count("others", 6, 4)
        dve_parts, pool_parts = m.count("dve_parts", 4, 3), m.count("pool_parts", 4, 3)
        prod_re, prod_im = m.count("prod_re", 2, 3), m.count("prod_im", 2, 3)
        out_ready, added = m.count("out_ready", NC_, 9), m.count("added", NC_, 9)
        load_y, act_y, dve_y = gate_all(xT, tanh_buf, y, tanh_done, y_done, ratio_in)
        block = ctx.enter_context(nc.Block())

        @block.sync
        def _(sp):
            for dst, src in ((raw_w[0], wq), (raw_w[1], wkv), (raw_w[2], woT), (f_sb, dft), (fi_sb, idftT)):
                sp.dma_start(dst[:, :, :], src.rearrange("(k p) n -> p k n", p=P)).then_inc(w_in, 16)
            sp.dma_start(norm_t[:, :], norm_mat).then_inc(w_in, 16)
            sp.dma_start(dc_t[:, :], dc_cols).then_inc(w_in, 16)
            load_y(sp, gate)

        @block.tensor
        def _(pe):
            for s in (planes, norm_ready, out_ready):
                s.open(pe)
            pe.wait_ge(w_in, 16 * 7)
            n = 0
            for w in (raw_w[1], raw_w[0]):
                for mc in range(NC_):
                    if n >= 4:
                        pe.wait_ge(fold_copied, n - 3)
                    for half in range(2):
                        for k in range(2):
                            last = pe.matmul(pl[n % 4][:, :].rearrange("p (r h s) -> p r h s", r=2, h=2)[:, :, half, :],
                                             w[:, 2 * half + k, mc * P:(mc + 1) * P],
                                             f_sb[:, 2 * half + k, :].rearrange("p (r h s) -> p r h s", r=2, h=2)[:, :, half, :],
                                             start=k == 0, stop=k == 1)
                    last.then_inc(folded, 1)
                    n += 1
            for ft in range(4):
                pe.wait_ge(fold_copied, n - 3)
                for k in range(2):
                    last = pe.matmul(pl[n % 4][:, :], fi_sb[:, 2 * (ft % 2) + k, ft * P:(ft + 1) * P],
                                     raw_w[2][:, 2 * (ft % 2) + k, :], start=k == 0, stop=k == 1)
                last.then_inc(folded, 1)
                n += 1
            pe.wait_ge(fold_copied, 12)

            def norm(b, u):
                pe.wait_ge(squared.sem, squared.at(b, 2 * u + 2))
                pe.wait_ge(rnormed.sem, rnormed.at(b, 2 * u - 3))
                for r in range(2):
                    last = pe.matmul(pn[u % 2][:, :], norm_t[:, :], square[:, u % 2, r, :], start=r == 0, stop=r == 1)
                last.then_inc(norm_ready.sem, 1)

            def out(b, oc):
                pe.wait_ge(added.sem, added.at(b, oc - 1))
                if oc == 0:
                    pe.wait_ge(prod_re.sem, prod_re.at(b, 2))
                    pe.wait_ge(prod_im.sem, prod_im.at(b, 2))
                for ft in range(4):
                    last = pe.matmul(pd[oc % 2][:, :], fold[2][:, ft, oc * P:(oc + 1) * P], prod[:, 0, ft, :],
                                     start=ft == 0, stop=ft == 3)
                last.then_inc(out_ready.sem, 1)

            def unit(b, u):
                kind, half = u % 2, u // 2
                for r in range(2):
                    tile = 2 * r + half
                    pe.wait_ge(hatted.sem, hatted.at(b, 2 * u + r - 3))
                    pe.wait_ge(squared.sem, squared.at(b, 2 * u + r - 3))
                    for c in range(NC_):
                        last = pe.matmul(pl[2 * (u % 2) + r][:, :], fold[kind][:, c, tile * P:(tile + 1) * P],
                                         y[:, c, bass.ds(b * T, T)], start=c == 0, stop=c == NC_ - 1)
                    last.then_inc(planes.sem, 1)

            def turn(b, first=False):
                def fill(oc):
                    if not first:
                        out(b - 1, oc)

                pe.wait_ge(y_done, b + 1)
                unit(b, 0)
                unit(b, 1)
                norm(b, 0)
                fill(0)
                norm(b, 1)
                unit(b, 2)
                fill(1)
                norm(b, 2)
                unit(b, 3)
                fill(2)
                fill(3)
                norm(b, 3)

            turn(0, first=True)
            with pe.Fori(1, B) as b:
                turn(b)
            for oc in range(NC_):
                out(B - 1, oc)

        @block.scalar
        def _(act):
            squared.open(act)
            rnormed.open(act)
            for n in range(12):
                act.wait_ge(folded, n + 1)
                act.activation(fold[n // 4][:, n % 4, :], pl[n % 4][:, :], ACT.Copy).then_inc(fold_copied, 1)
            act_y(act)

            def rnorm_of(b, u):
                act.wait_ge(norm_ready.sem, norm_ready.at(b, u + 1))
                act.wait_ge(hatted.sem, hatted.at(b, 2 * u - 2))
                act.activation(rnorm[:, u % 2, :], pn[u % 2][:, :], ACT.Ln).then_inc(rnormed.sem, 1)
                act.wait_ge(rnormed.sem, rnormed.at(b, 2 * u + 1))
                act.activation(rnorm[:, u % 2, :], rnorm[:, u % 2, :], ACT.Exp, scale=-0.5).then_inc(rnormed.sem, 1)

            def squares(b, u):
                act.wait_ge(norm_ready.sem, norm_ready.at(b, u - 1))
                for r in range(2):
                    act.wait_ge(planes.sem, planes.at(b, 2 * u + r + 1))
                    act.activation(square[:, u % 2, r, :], pl[2 * (u % 2) + r][:, :], ACT.Square).then_inc(squared.sem, 1)

            with act.Fori(0, B) as b:
                squares(b, 0)
                squares(b, 1)
                rnorm_of(b, 0)
                rnorm_of(b, 1)
                for u in range(2, 4):
                    squares(b, u)
                    rnorm_of(b, u)

        @block.vector
        def _(dve):
            for s in (hatted, summed, others, dve_parts, prod_im, added):
                s.open(dve)
            dve.wait_ge(w_in, 16 * 7)
            dve_y(dve)

            def hat(b, u):
                kind, half = u % 2, u // 2
                hat_t = hat_k if kind == 0 else hat_q
                dve.wait_ge(rnormed.sem, rnormed.at(b, 2 * u + 2))
                if kind == 0:
                    dve.wait_ge(summed.sem, summed.at(b, 2 * half))
                else:
                    dve.wait_ge(pool_parts.sem, pool_parts.at(b, 2 * half))
                    dve.wait_ge(dve_parts.sem, dve_parts.at(b, 2 * half))
                for r in range(2):
                    dve.tensor_tensor(hat_t[:, r, :], pl[2 * (u % 2) + r][:, :], rnorm[:, u % 2, :], ALU.mult).then_inc(hatted.sem, 1)

            def sums(b, half):
                dve.wait_ge(hatted.sem, hatted.at(b, 4 * half + 2))
                dve.wait_ge(pool_parts.sem, pool_parts.at(b, 2 * half))
                dve.wait_ge(others.sem, others.at(b, 3 * half))
                for r in range(2):
                    dve.tensor_tensor_scan(total[:, r, :], dc_t[:, 2:3].to_broadcast([P, T]), hat_k[:, r, :], 0.0,
                                           ALU.mult, ALU.add).then_inc(summed.sem, 1)
                dve.wait_ge(summed.sem, summed.at(b, 2 * half + 2))
                dve.wait_ge(dve_parts.sem, dve_parts.at(b, 2 * half))
                dve.tensor_scalar(other[:, 0, :], total[:, 1, :], dc_t[:, 0:1], None, ALU.mult).then_inc(others.sem, 1)
                dve.tensor_scalar(other[:, 1, :], total[:, 0, :], dc_t[:, 0:1], None, ALU.mult).then_inc(others.sem, 1)
                dve.wait_ge(others.sem, others.at(b, 3 * half + 2))
                dve.scalar_tensor_tensor(other[:, 2, :], total[:, 1, :], dc_t[:, 1:2], other[:, 1, :],
                                         ALU.mult, ALU.add).then_inc(others.sem, 1)

            def product_im(b, half):
                dve.wait_ge(hatted.sem, hatted.at(b, 4 * half + 4))
                dve.wait_ge(others.sem, others.at(b, 3 * half + 3))
                dve.wait_ge(prod_im.sem, prod_im.at(b, half))
                dve.tensor_tensor(parts[:, 2, :], hat_q[:, 0, :], other[:, 0, :], ALU.mult).then_inc(dve_parts.sem, 1)
                dve.tensor_tensor(parts[:, 3, :], hat_q[:, 1, :], other[:, 2, :], ALU.mult).then_inc(dve_parts.sem, 1)
                dve.wait_ge(dve_parts.sem, dve_parts.at(b, 2 * half + 2))
                dve.wait_ge(out_ready.sem, out_ready.at(b, 0))
                dve.tensor_tensor(prod[:, 0, 2 + half, :], parts[:, 2, :], parts[:, 3, :], ALU.add).then_inc(prod_im.sem, 1)

            def add_out(b, oc):
                dve.wait_ge(out_ready.sem, out_ready.at(b, oc + 1))
                settle(dve, dve_passed)
                x_oc = xT[:, oc, bass.ds(b * T, T)]
                dve.tensor_tensor(x_oc, x_oc, pd[oc % 2][:, :], ALU.add).then_inc(added.sem, 1)

            def turn(b, first=False):
                hat(b, 0)
                if not first:
                    add_out(b - 1, 0)
                sums(b, 0)
                hat(b, 1)
                if not first:
                    add_out(b - 1, 1)
                hat(b, 2)
                if not first:
                    add_out(b - 1, 2)
                    add_out(b - 1, 3)
                product_im(b, 0)
                sums(b, 1)
                hat(b, 3)
                product_im(b, 1)

            turn(0, first=True)
            with dve.Fori(1, B) as b:
                turn(b)
            for oc in range(NC_):
                add_out(B - 1, oc)

        @block.gpsimd
        def _(pool):
            pool_parts.open(pool)
            prod_re.open(pool)
            with pool.Fori(0, B) as b:
                for half in range(2):
                    pool.wait_ge(hatted.sem, hatted.at(b, 4 * half + 4))
                    pool.wait_ge(others.sem, others.at(b, 3 * half + 1))
                    pool.wait_ge(prod_re.sem, prod_re.at(b, half))
                    pool.tensor_tensor(parts[:, 0, :], hat_q[:, 0, :], total[:, 0, :], ALU.mult).then_inc(pool_parts.sem, 1)
                    pool.tensor_tensor(parts[:, 1, :], hat_q[:, 1, :], other[:, 0, :], ALU.mult).then_inc(pool_parts.sem, 1)
                    pool.wait_ge(pool_parts.sem, pool_parts.at(b, 2 * half + 2))
                    pool.wait_ge(out_ready.sem, out_ready.at(b, 0))
                    pool.tensor_tensor(prod[:, 0, half, :], parts[:, 0, :], parts[:, 1, :], ALU.subtract).then_inc(prod_re.sem, 1)


NE, HE = 8, 256
TPE = HE // P
NEH = NE * TPE


def expert_ffn(nc, ident, xT, gate, wg1T, wg2T, weights, bup, bdown, lower, onehot, out):
    with ExitStack() as ctx:
        m = Space(nc, ctx, "moe")
        wraw = m.sb("wraw", [P, TPE, 2, C])
        w_hi, w_lo = m.sb("w_hi", [P, 2, TPE, 2, C], F32R), m.sb("w_lo", [P, 2, TPE, 2, C], F32R)
        wg1_sb, wg2_sb = m.sb("wg1", [P, NC_, NE]), m.sb("wg2", [NE, NE])
        bd_sb = m.sb("bd", [NE, C])
        bup_t, half_bup, lower_t = m.sb("bup", [P, NEH]), m.sb("half_bup", [P, NEH]), m.sb("lower", [P, NE, NE])
        y = m.sb("y", [P, NC_, B * T])
        y_hi, y_lo = m.sb("y_hi", [P, NC_, PAIR * T], F32R), m.sb("y_lo", [P, NC_, PAIR * T], F32R)
        xsum = y[:, :, 0:PAIR * T]
        NTR = PAIR * NT
        h_hi, h_lo = m.sb("h_hi", [P, 4, T], F32R), m.sb("h_lo", [P, 4, T], F32R)
        rows = m.sb("rows", [P, NT, C])
        inner, onehot_sb = rows[0:NE, 0:2, :], rows[0:NE, 2:4, :].rearrange("p t c -> p (t c)")
        logit, share = m.sb("logit", [P, NTR, NE]), m.sb("share", [P, NTR, NE])
        above, equal = m.sb("above", [P, NTR, NE, NE]), m.sb("equal", [P, NTR, NE, NE])
        rank, top, denom = m.sb("rank", [P, NTR, NE]), m.sb("top", [P, NTR]), m.sb("denom", [P, NTR])
        scoreT = m.sb("scoreT", [NE, B * T])
        score_hi, score_lo = m.sb("score_hi", [NE, PAIR * T], F32R), m.sb("score_lo", [NE, PAIR * T], F32R)
        onehot_r = m.sb("onehot_r", [NE, NE * P], F32R)
        work = m.sb("work", [P, 2 * NC_, T])
        tanh_buf = work[:, :, :].rearrange("p (h c) t -> p h c t", h=2)
        tanh_u, hid, spread, lin = work[:, 0:2, :], work[:, 2:4, :], work[:, 4:6, :], work[:, 6, :]
        pu = [m.ps(f"pu{i}", [P, T]) for i in range(2)]
        pb = [m.ps(f"pb{i}", [P, T]) for i in range(2)]
        pd = [m.ps(f"pd{i}", [P, T]) for i in range(NT)]

        ratio_in = [m.sem(f"ratio_in{b}") for b in range(B)]
        tanh_done, y_done = m.sem("tanh_done"), m.sem("y_done")
        act_passed, pe_passed, dve_passed = m.passed("act"), m.passed("pe"), m.passed("dve")
        small_in, setup, sp_passed = m.sem("small_in"), m.sem("setup"), m.passed("sp")
        inner_ready, inner_done = m.count("inner_ready", PAIR), m.count("inner_done", PAIR)
        logit_ready, ranked = m.count("logit_ready", 1), m.count("ranked", 12)
        share_exp = m.count("share_exp", 1)
        turned, turned_out = m.count("turned", PAIR), m.count("turned_out", PAIR)
        NV, NI = NE * PAIR, NE * PAIR * TPE
        w_in = m.count("w_in", NE, by=16)
        w_hi_done, w_lo_done = m.count("w_hi_done", NE, 3), m.count("w_lo_done", NE, 3)
        y_hi_done, y_lo_done = m.count("y_hi_done", PAIR), m.count("y_lo_done", PAIR)
        up_ready = m.count("up_ready", NI)
        tanh_u_done, lin_done, hid_done = m.count("tanh_u_done", NI, 3), m.count("lin_done", NI, 3), m.count("hid_done", NI, 3)
        h_hi_done, h_lo_done = m.count("h_hi_done", NI, 5), m.count("h_lo_done", NI, 5)
        spread_ready, spread_done = m.count("spread_ready", NV, 3), m.count("spread_done", NV, 3)
        scores_hi, scores_lo = m.count("scores_hi", 1), m.count("scores_lo", 1)
        down_done, added = m.count("down_done", NV, 3), m.count("added", NV * NC_, 5)
        rows_ready, rows_done = m.count("rows_ready", PAIR * NT, 5), m.count("rows_done", PAIR * NT, 5)
        stored = [m.count(f"stored{t}", PAIR, 17, by=16) for t in range(NT)]
        load_y, act_y, dve_y = gate_all(xT, tanh_buf, y, tanh_done, y_done, ratio_in)
        block = ctx.enter_context(nc.Block())

        @block.sync
        def _(sp):
            for cnt in (w_in, *stored):
                cnt.open(sp)
            sp.dma_start(wg1_sb[:, :, :], wg1T.rearrange("(c p) e -> p c e", p=P)).then_inc(small_in, 16)
            for dst, src in ((wg2_sb, wg2T), (bd_sb, bdown), (onehot_sb, onehot), (bup_t, bup)):
                sp.dma_start(dst[:, :], src).then_inc(small_in, 16)
            sp.dma_start(lower_t[:, :, :], lower).then_inc(small_in, 16)
            load_y(sp, gate)

            def load_weights(bp, e):
                sp.wait_ge(w_lo_done.sem, w_lo_done.at(bp, e))
                sp.dma_start(wraw[:, :, :, :], weights[e]).then_inc(w_in.sem, 16)

            def turn(bp, last=False):
                for e in range(1, NE):
                    load_weights(bp, e)
                if not last:
                    load_weights(bp + 1, 0)
                for bi in range(PAIR):
                    for t in range(NT):
                        sp.wait_ge(rows_done.sem, rows_done.at(bp, bi * NT + t + 1))
                        settle(sp, sp_passed)
                        sp.dma_start(out[bass.ds(bp * PAIR + bi, 1), t * P:(t + 1) * P, :].rearrange("o p c -> p (o c)"),
                                     rows[:, t, :]).then_inc(stored[t].sem, 16)

            load_weights(0, 0)
            with sp.Fori(0, B // PAIR - 1) as bp:
                turn(bp)
            turn(B // PAIR - 1, last=True)
            for cnt in stored:
                sp.wait_ge(cnt.sem, cnt.at(B // PAIR, 0))

        @block.tensor
        def _(pe):
            for s in (inner_ready, logit_ready, turned, up_ready, spread_ready, down_done, rows_ready):
                s.open(pe)
            pe.wait_ge(small_in, 16 * 6)
            with pe.Fori(0, B // PAIR) as bp:
                pe.wait_ge(y_done, bp * PAIR + PAIR)
                pe.wait_ge(turned_out.sem, turned_out.at(bp, 0))
                for bi in range(PAIR):
                    for c in range(NC_):
                        last = pe.matmul(pb[bi][0:NE, :], wg1_sb[:, c, :], y[:, c, bass.ds(bp * (PAIR * T) + bi * T, T)],
                                         start=c == 0, stop=c == NC_ - 1)
                    last.then_inc(inner_ready.sem, 1)
                for bi in range(PAIR):
                    pe.wait_ge(inner_done.sem, inner_done.at(bp, bi + 1))
                    for t in range(NT):
                        q = bi * NT + t
                        last = pe.matmul(pu[0][:, q * NE:(q + 1) * NE], inner[:, bi, t * P:(t + 1) * P], wg2_sb[:, :], start=True, stop=True)
                last.then_inc(logit_ready.sem, 1)
                pe.wait_ge(ranked.sem, ranked.at(bp, 12))
                for bi in range(PAIR):
                    for t in range(NT):
                        last = pe.transpose(pb[bi][0:NE, t * P:(t + 1) * P], share[:, bi * NT + t, :], ident[:, :])
                    last.then_inc(turned.sem, 1)
            pe.wait_ge(turned_out.sem, turned_out.at(B // PAIR, 0))
            pe.wait_ge(setup, 3)

            def spread_score(bp, v):
                e, bi = divmod(v, PAIR)
                pe.wait_ge(spread_done.sem, spread_done.at(bp, v - 1))
                pe.wait_ge(scores_lo.sem, scores_lo.at(bp, 1))
                tokens = slice(bi * T, (bi + 1) * T)
                pe.matmul(pb[v % 2][:, :], onehot_r[:, e * P:(e + 1) * P], score_hi[:, tokens], start=True, stop=False)
                pe.matmul(pb[v % 2][:, :], onehot_r[:, e * P:(e + 1) * P], score_lo[:, tokens],
                          start=False, stop=True).then_inc(spread_ready.sem, 1)

            def up(bp, v, j):
                e, bi = divmod(v, PAIR)
                i = TPE * v + j
                pe.wait_ge(tanh_u_done.sem, tanh_u_done.at(bp, i - 1))
                pe.wait_ge(lin_done.sem, lin_done.at(bp, i - 1))
                if j == 0 and bi == 0:
                    pe.wait_ge(w_lo_done.sem, w_lo_done.at(bp, e + 1))
                if j == 0 and e == 0:
                    pe.wait_ge(y_lo_done.sem, y_lo_done.at(bp, bi + 1))
                cols = slice(bi * T, (bi + 1) * T)
                for c in range(NC_):
                    w = slice(c * P, (c + 1) * P)
                    last = product(pe, pu[i % 2][:, :], w_hi[:, e % 2, j, 0, w], w_lo[:, e % 2, j, 0, w],
                                   y_hi[:, c, cols], y_lo[:, c, cols], start=c == 0, stop=c == NC_ - 1)
                last.then_inc(up_ready.sem, 1)

            def down(bp, v):
                e, bi = divmod(v, PAIR)
                for j in range(TPE):
                    i = TPE * v + j
                    pe.wait_ge(h_lo_done.sem, h_lo_done.at(bp, i + 1))
                    for oc in range(NC_):
                        cols = slice(oc * P, (oc + 1) * P)
                        if j == 0:
                            pe.wait_ge(added.sem, added.at(bp, NC_ * (v - 1) + oc + 1))
                            if v == 0:
                                pe.wait_ge(rows_done.sem, rows_done.at(bp, 0))
                        if j == 0 and e == 0:
                            settle(pe, pe_passed)
                            pe.matmul(pd[oc][:, :], bd_sb[:, cols], scoreT[:, bass.ds(bp * (PAIR * T) + bi * T, T)], start=True, stop=False)
                        last = product(pe, pd[oc][:, :], w_hi[:, e % 2, j, 1, cols], w_lo[:, e % 2, j, 1, cols],
                                       h_hi[:, i % 4, :], h_lo[:, i % 4, :], start=j == 0 and e > 0, stop=j == TPE - 1)
                last.then_inc(down_done.sem, 1)

            def turn_back(bp, bi, t):
                q = bi * NT + t
                pe.wait_ge(added.sem, added.at(bp, NC_ * (NV - PAIR + bi + 1)))
                pe.wait_ge(rows_done.sem, rows_done.at(bp, q - NT + 1))
                if q < NT:
                    pe.wait_ge(added.sem, added.at(bp, NC_ * NV))
                for c in range(NC_):
                    last = pe.transpose(pd[t][:, c * P:(c + 1) * P], xsum[:, c, bi * T + t * P:bi * T + (t + 1) * P], ident[:, :])
                last.then_inc(rows_ready.sem, 1)

            with pe.Fori(0, B // PAIR) as bp:
                for v in range(NV):
                    spread_score(bp, v)
                    for j in range(TPE):
                        up(bp, v, j)
                    if v > 0:
                        down(bp, v - 1)
                down(bp, NV - 1)
                for bi in range(PAIR):
                    for t in range(NT):
                        turn_back(bp, bi, t)

        @block.scalar
        def _(act):
            for s in (inner_done, share_exp, turned_out, w_hi_done, y_hi_done, scores_hi, tanh_u_done, spread_done, h_hi_done):
                s.open(act)
            act_y(act)
            with act.Fori(0, B // PAIR) as bp:
                act.wait_ge(logit_ready.sem, logit_ready.at(bp, 0))
                for bi in range(PAIR):
                    act.wait_ge(inner_ready.sem, inner_ready.at(bp, bi + 1))
                    act.activation(inner[:, bi, :], pb[bi][0:NE, :], ACT.Tanh).then_inc(inner_done.sem, 1)
                act.wait_ge(ranked.sem, ranked.at(bp, 8))
                act.activation(share[:, :, :], share[:, :, :], ACT.Exp).then_inc(share_exp.sem, 1)
                for bi in range(PAIR):
                    act.wait_ge(turned.sem, turned.at(bp, bi + 1))
                    settle(act, act_passed)
                    act.activation(scoreT[:, bass.ds(bp * (PAIR * T) + bi * T, T)], pb[bi][0:NE, :], ACT.Copy).then_inc(turned_out.sem, 1)
            act.wait_ge(turned_out.sem, turned_out.at(B // PAIR, 0))
            act.activation(bd_sb[:, :], bd_sb[:, :], ACT.Copy, scale=2.0).then_inc(setup, 1)
            act.activation(onehot_r[:, :], onehot_sb[:, :], ACT.Copy).then_inc(setup, 1)
            act.wait_ge(setup, 3)

            def weights_high(bp, e):
                act.wait_ge(w_in.sem, w_in.at(bp, e + 1))
                act.wait_ge(down_done.sem, down_done.at(bp, PAIR * (e - 1)))
                act.activation(w_hi[:, e % 2].rearrange("p j w n -> p (j w n)"), wraw[:, :, :, :].rearrange("p j w n -> p (j w n)"),
                               ACT.Copy).then_inc(w_hi_done.sem, 1)

            def y_high(bp, bi):
                act.wait_ge(up_ready.sem, up_ready.at(bp, 0))
                settle(act, act_passed)
                act.activation(y_hi[:, :, bi * T:(bi + 1) * T], y[:, :, bass.ds(bp * (PAIR * T) + bi * T, T)], ACT.Copy).then_inc(y_hi_done.sem, 1)

            def hidden_high(bp, i):
                act.wait_ge(hid_done.sem, hid_done.at(bp, i + 1))
                act.wait_ge(down_done.sem, down_done.at(bp, i // TPE - 1))
                act.activation(h_hi[:, i % 4, :], hid[:, i % 2, :], ACT.Copy).then_inc(h_hi_done.sem, 1)

            with act.Fori(0, B // PAIR) as bp:
                weights_high(bp, 0)
                y_high(bp, 0)
                y_high(bp, 1)
                act.wait_ge(spread_ready.sem, spread_ready.at(bp, 0))
                settle(act, act_passed)
                act.activation(score_hi[:, :], scoreT[:, bass.ds(bp * (PAIR * T), PAIR * T)], ACT.Copy).then_inc(scores_hi.sem, 1)
                weights_high(bp, 1)
                for v in range(NV):
                    e, bi = divmod(v, PAIR)
                    act.wait_ge(spread_ready.sem, spread_ready.at(bp, v + 1))
                    act.wait_ge(lin_done.sem, lin_done.at(bp, TPE * (v - 1)))
                    act.activation(spread[:, v % 2, :], pb[v % 2][:, :], ACT.Copy).then_inc(spread_done.sem, 1)
                    for j in range(TPE):
                        i = TPE * v + j
                        act.wait_ge(up_ready.sem, up_ready.at(bp, i + 1))
                        act.wait_ge(hid_done.sem, hid_done.at(bp, i - 1))
                        act.activation(tanh_u[:, i % 2, :], pu[i % 2][:, :], ACT.Tanh, scale=0.5,
                                       bias=half_bup[:, TPE * e + j:TPE * e + j + 1]).then_inc(tanh_u_done.sem, 1)
                    for j in range(TPE):
                        hidden_high(bp, TPE * v + j)
                    if bi == 0 and 0 < e < NE - 1:
                        weights_high(bp, e + 1)

        @block.gpsimd
        def _(pool):
            w_lo_done.open(pool)
            with pool.Fori(0, B // PAIR) as bp:
                for e in range(NE):
                    pool.wait_ge(w_hi_done.sem, w_hi_done.at(bp, e + 1))
                    pool.tensor_tensor(w_lo[:, e % 2].rearrange("p j w n -> p (j w n)"), wraw[:, :, :, :].rearrange("p j w n -> p (j w n)"),
                                       w_hi[:, e % 2].rearrange("p j w n -> p (j w n)").bitcast(F32), ALU.subtract).then_inc(w_lo_done.sem, 1)

        @block.vector
        def _(dve):
            for s in (ranked, y_lo_done, scores_lo, lin_done, hid_done, h_lo_done, added, rows_done):
                s.open(dve)
            dve.wait_ge(small_in, 16 * 6)
            dve.tensor_scalar(half_bup[:, :], bup_t[:, :], 0.5, None, ALU.mult).then_inc(setup, 1)
            dve_y(dve)
            with dve.Fori(0, B // PAIR) as bp:
                own, rival = [P, NTR, NE, NE], [P, NTR, NE, NE]
                step = [0]

                def did(ins):
                    step[0] += 1
                    ins.then_inc(ranked.sem, 1)
                    dve.wait_ge(ranked.sem, ranked.at(bp, step[0]))

                dve.wait_ge(logit_ready.sem, logit_ready.at(bp, 1))
                dve.wait_ge(turned.sem, turned.at(bp, 0))
                did(dve.tensor_copy(logit[:, :, :], pu[0][:, 0:NTR * NE].rearrange("p (t e) -> p t e", e=NE)))
                mine = logit[:, :, :].rearrange("p t (e o) -> p t e o", o=1).to_broadcast(own)
                theirs = logit[:, :, :].rearrange("p t (o e) -> p t o e", o=1).to_broadcast(rival)
                did(dve.tensor_tensor(above[:, :, :, :], theirs, mine, ALU.is_gt))
                did(dve.tensor_tensor(equal[:, :, :, :], theirs, mine, ALU.is_equal))
                did(dve.tensor_tensor(equal[:, :, :, :], equal[:, :, :, :],
                                      lower_t[:, :, :].rearrange("p (o e) f -> p o e f", o=1).to_broadcast(own), ALU.mult))
                did(dve.tensor_tensor(above[:, :, :, :], above[:, :, :, :], equal[:, :, :, :], ALU.add))
                did(dve.tensor_reduce(rank[:, :, :], above[:, :, :, :], AX_X, ALU.add))
                did(dve.tensor_reduce(top[:, :], logit[:, :, :], AX_X, ALU.max))
                did(dve.tensor_tensor(share[:, :, :], logit[:, :, :], top[:, :].rearrange("p (t o) -> p t o", o=1).to_broadcast([P, NTR, NE]),
                                      ALU.subtract))
                dve.wait_ge(share_exp.sem, share_exp.at(bp, 1))
                did(dve.scalar_tensor_tensor(share[:, :, :], rank[:, :, :], 2.0, share[:, :, :], ALU.is_lt, ALU.mult))
                did(dve.tensor_reduce(denom[:, :], share[:, :, :], AX_X, ALU.add))
                did(dve.reciprocal(denom[:, :], denom[:, :]))
                did(dve.tensor_tensor(share[:, :, :], share[:, :, :], denom[:, :].rearrange("p (t o) -> p t o", o=1).to_broadcast([P, NTR, NE]),
                                      ALU.mult))

            def y_low(bp, bi):
                dve.wait_ge(y_hi_done.sem, y_hi_done.at(bp, bi + 1))
                settle(dve, dve_passed)
                cols = slice(bi * T, (bi + 1) * T)
                dve.tensor_tensor(y_lo[:, :, cols], y[:, :, bass.ds(bp * (PAIR * T) + bi * T, T)], y_hi[:, :, cols].bitcast(F32),
                                  ALU.subtract).then_inc(y_lo_done.sem, 1)

            def hidden(bp, v, j):
                i, et = TPE * v + j, TPE * (v // PAIR) + j
                dve.wait_ge(tanh_u_done.sem, tanh_u_done.at(bp, i + 1))
                dve.wait_ge(spread_done.sem, spread_done.at(bp, v + 1))
                dve.wait_ge(hid_done.sem, hid_done.at(bp, i))
                dve.scalar_tensor_tensor(lin, pu[i % 2][:, :], bup_t[:, et:et + 1], spread[:, v % 2, :],
                                         ALU.add, ALU.mult).then_inc(lin_done.sem, 1)
                dve.wait_ge(lin_done.sem, lin_done.at(bp, i + 1))
                dve.wait_ge(h_lo_done.sem, h_lo_done.at(bp, i - 1))
                dve.scalar_tensor_tensor(hid[:, i % 2, :], tanh_u[:, i % 2, :], 1.0, lin,
                                         ALU.add, ALU.mult).then_inc(hid_done.sem, 1)

            def hidden_low(bp, i):
                dve.wait_ge(h_hi_done.sem, h_hi_done.at(bp, i + 1))
                dve.wait_ge(down_done.sem, down_done.at(bp, i // TPE - 1))
                dve.tensor_tensor(h_lo[:, i % 4, :], hid[:, i % 2, :], h_hi[:, i % 4, :].bitcast(F32), ALU.subtract).then_inc(h_lo_done.sem, 1)

            def add(bp, v):
                e, bi = divmod(v, PAIR)
                dve.wait_ge(down_done.sem, down_done.at(bp, v + 1))
                if v == 0:
                    dve.wait_ge(rows_ready.sem, rows_ready.at(bp, 0))
                settle(dve, dve_passed)
                for oc in range(NC_):
                    if e == 0:
                        before = xT[:, oc, bass.ds(bp * (PAIR * T) + bi * T, T)]
                    else:
                        dve.wait_ge(added.sem, added.at(bp, NC_ * (v - PAIR) + oc + 1))
                        before = xsum[:, oc, bi * T:(bi + 1) * T]
                    dve.scalar_tensor_tensor(xsum[:, oc, bi * T:(bi + 1) * T], pd[oc][:, :], 0.5, before, ALU.mult, ALU.add).then_inc(added.sem, 1)

            with dve.Fori(0, B // PAIR) as bp:
                for bi in range(PAIR):
                    y_low(bp, bi)
                dve.wait_ge(scores_hi.sem, scores_hi.at(bp, 1))
                settle(dve, dve_passed)
                dve.tensor_tensor(score_lo[:, :], scoreT[:, bass.ds(bp * (PAIR * T), PAIR * T)], score_hi[:, :].bitcast(F32),
                                  ALU.subtract).then_inc(scores_lo.sem, 1)
                for v in range(NV):
                    for j in range(TPE):
                        hidden(bp, v, j)
                    for j in range(TPE):
                        hidden_low(bp, TPE * v + j)
                    if v > 0:
                        add(bp, v - 1)
                add(bp, NV - 1)
                for bi in range(PAIR):
                    for t in range(NT):
                        dve.wait_ge(rows_ready.sem, rows_ready.at(bp, bi * NT + t + 1))
                        dve.wait_ge(stored[t].sem, stored[t].at(bp, bi))
                        dve.tensor_copy(rows[:, t, :], pd[t][:, :]).then_inc(rows_done.sem, 1)


def build(nc, a, out):
    gates = nc.dram_tensor("gates", (NCOND, B, P, NC_, T), F32, kind="Internal").ap()
    sideT = nc.dram_tensor("sideT", (B, P, NC_, T), F32, kind="Internal").ap()
    with ExitStack() as ctx:
        ident = ctx.enter_context(nc.sbuf_tensor("ident", [P, P], F32))
        xT = ctx.enter_context(nc.sbuf_tensor("xT", [P, NC_, B * T], F32))
        small = [ctx.enter_context(nc.sbuf_tensor(name, shape, F32)) for name, shape in
                 (("wcol", [P, NCOND * NC_]), ("ucol", [P, NCOND * NC_]), ("decay", [P, B, NCOND * NC_]), ("lngain", [P, B]))]
        ident_done = ctx.enter_context(nc.semaphore("ident_done"))
        with nc.Block() as block:
            @block.gpsimd
            def _(pool):
                pool.memset(ident[:, :], 0.0).then_inc(ident_done, 1)
                pool.wait_ge(ident_done, 1)
                pool.affine_select(out=ident[:, :], in_=ident[:, :], compare_op=ALU.not_equal, fill=1.0, base=0,
                                   pattern=[[-1, P]], channel_multiplier=1).then_inc(ident_done, 1)
                pool.wait_ge(ident_done, 2)
        prepare(nc, a["x"], a["fside"], a["cond"], a["w"], a["u"], ident, xT, sideT, gates, small)
        attention(nc, ident, xT, sideT, gates, small, a["att"], a["wv"], a["sink"], (a["cos"], a["sin"]), a["mask"], a["perm"])
        sparse_ffn(nc, xT, gates[1], a["ffn"])
        fourier_attention(nc, xT, gates[2], a["fft_q"], a["fft_kv"], a["fft_oT"], a["dft"], a["idftT"], a["norm"], a["dc"])
        expert_ffn(nc, ident, xT, gates[3], a["g1T"], a["g2T"], a["moe"], a["bup"], a["bdown"], a["lower"], a["onehot"], out)


def constants():
    c = {}
    freq = np.float32(1.0 / 1024.0) ** np.linspace(0, 1, HD // 4, dtype=np.float32)
    freq = np.concatenate([freq.astype(np.float32), np.zeros(HD // 4, np.float32)])
    theta = np.arange(T, dtype=np.float32)[None, :] * freq[:, None]
    c["cos"] = np.tile(np.cos(theta), (4, 1)).astype(np.float32)
    c["sin"] = np.concatenate([np.sin(theta), -np.sin(theta)] * 2).astype(np.float32)
    off = np.arange(MW)[None, :] - (NT - 1) * P - np.arange(P)[:, None]
    c["mask"] = np.where((off <= 0) & (off > -128), MASKED, 0.0).astype(np.float32)
    r = np.arange(P)
    c["perm"] = (r[:, None] == (r ^ (HD // 2))[None, :]).astype(np.float32)
    n, s = np.arange(2 * BINS)[:, None], np.arange(BINS)[None, :]
    theta = np.pi * n * s / BINS
    re, im = np.cos(theta), -np.sin(theta)
    im[:, 0] = (-1.0) ** n[:, 0]
    weight = np.where(s == 0, 1.0, 2.0)
    dft, idft = np.zeros((C, 2, NCH, BINS)), np.zeros((C, 2, NCH, BINS))
    for h in range(NCH):
        rows = slice(2 * BINS * h, 2 * BINS * (h + 1))
        for plane, f in ((0, re), (1, im)):
            dft[rows, plane, h] = f
            idft[rows, plane, h] = f * weight / (2 * BINS)
    c["dft"], c["idftT"] = (d.reshape(C, C).astype(np.float32) for d in (dft, idft))
    c["norm"] = ((r[:, None] // BINS == r[None, :] // BINS) * np.where(r[:, None] % BINS == 0, 1.0, 2.0)).astype(np.float32)
    c["dc"] = np.stack([r % BINS != 0, r % BINS == 0, r >= 0], 1).astype(np.float32)
    e = np.arange(NE)
    c["lower"] = np.tile((e[None, :] < e[:, None]).astype(np.float32)[None], (P, 1, 1))
    c["onehot"] = np.repeat(np.eye(NE, dtype=np.float32), P, axis=1)
    return c


def layouts(v):
    def columns(names):
        return np.stack([v[n] for n in names]).reshape(NCOND, NC_, P).transpose(2, 0, 1).reshape(P, NCOND * NC_)

    def hidden_tiles(w):
        return w.reshape(NC_, P, NG, P, 4).transpose(2, 4, 1, 0, 3).reshape(NHID, P, C)

    conds = ["L0_cond", "L0_cond2", "L1_cond", "L1_cond2"]
    wqkv, nq = v["L0_attn_W_qkv"], NKV * QM * HD
    wq = wqkv[:, :nq].reshape(C, NPAIR, 2, QM, HD).transpose(0, 1, 3, 2, 4).reshape(C, nq)
    wk = wqkv[:, nq:nq + NKV * HD]
    wo = v["L0_attn_W_out"].reshape(NPAIR, 2, QM, HD, C).transpose(0, 2, 1, 3, 4).reshape(nq, C)

    def attention_tile(kind, i):
        if kind == "o":
            p, oc = divmod(i, NC_)
            tile = wo[p * QM * P:(p + 1) * QM * P, oc * P:(oc + 1) * P]
        else:
            tile = (wk if kind == "k" else wq)[:, i * P:(i + 1) * P]
        return tile.reshape(NC_, P, P).transpose(1, 0, 2).reshape(P, C)

    return {
        "x": v["x"], "fside": v["fside_BxSxS_0"], "cond": v["cond_512"],
        "w": columns([n + "_w" for n in conds]), "u": columns([n + "_u" for n in conds]),
        "att": np.stack([attention_tile(*job) for job in attention_jobs() if job[0] in ("k", "q", "o")]),
        "wv": wqkv[:, nq + NKV * HD:],
        "sink": v["L0_attn_s"].reshape(NPAIR, 2, QM).transpose(0, 2, 1).reshape(1, NHEAD),
        "ffn": np.stack([hidden_tiles(v["L0_ffn_w_gate"]), hidden_tiles(v["L0_ffn_w_up"]),
                         v["L0_ffn_w_down"].reshape(NG, P, 4, C).transpose(0, 2, 1, 3).reshape(NHID, P, C)], 2),
        "fft_q": v["L1_attn_W_q"], "fft_kv": v["L1_attn_W_kv"], "fft_oT": v["L1_attn_W_o"].T,
        "g1T": v["L1_ffn_Wg1"].T, "g2T": v["L1_ffn_Wg2"].T,
        "moe": np.stack([v["L1_ffn_Wup"].reshape(NE, TPE, P, NC_, P).transpose(0, 4, 1, 3, 2).reshape(NE, P, TPE, C),
                         v["L1_ffn_Wdown"].transpose(0, 2, 1).reshape(NE, TPE, P, C).transpose(0, 2, 1, 3)], 3),
        "bup": v["L1_ffn_bup"].reshape(NEH, P).T,
        "bdown": v["L1_ffn_bdown"],
    }


def kernel(**inputs):
    import concourse.bacc as bacc
    from concourse.bass_utils import run_bass_kernel_spmd

    nc = bacc.Bacc("TRN2", target_bir_lowering=False, num_devices=1)
    arrays, aps = {}, {}
    for name, a in {**layouts(inputs), **constants()}.items():
        a = np.ascontiguousarray(a)
        arrays[f"in_{name}"] = a
        aps[name] = nc.dram_tensor(f"in_{name}", a.shape, mybir.dt.from_np(a.dtype), kind="ExternalInput").ap()
    out = nc.dram_tensor("out", (B, T, C), F32, kind="ExternalOutput").ap()
    build(nc, aps, out)
    r = run_bass_kernel_spmd(nc, [arrays], core_ids=[0])
    return r.results[0]["out"]
```
